# Optimizing a Trainium2 kernel written in Bass

```python
import numpy as np
import jax
import jax.numpy as jnp

def _softmax(x, axis=-1):
    return jax.nn.softmax(x, axis=axis)

def _gelu(x):
    return jax.nn.gelu(x, approximate=True)

def _silu(x):
    return jax.nn.silu(x)

def _sigmoid(x):
    return jax.nn.sigmoid(x)

def _layernorm(x, axis=-1, eps=1e-05):
    m = jnp.mean(x, axis=axis, keepdims=True)
    v = jnp.var(x, axis=axis, keepdims=True)
    return (x - m) / jnp.sqrt(v + eps)

def _scatter_add(tgt, idx, src, axis=0):
    return tgt.at[idx].add(src)

def _segment_sum(src, seg, n):
    return jax.ops.segment_sum(src, seg, n)
kernel_name = 'mk_decoder_preln_d4_seqx_r8_5f64c3'

def setup_inputs(seed: int=0):
    np.random.seed(seed)
    _w = jnp.asarray

    def _rec_inputs():
        import jax
        import jax.numpy as jnp
        _rk = jax.random.key(seed)
        x = -0.0002928 + 1 * jax.random.normal(jax.random.fold_in(_rk, 1), (4, 512, 128), jnp.float32)
        _lenS = 512 - jax.random.randint(jax.random.fold_in(_rk, 7), (4,), 0, max(1, 512 // 4) + 1, jnp.int32)
        _lenS2 = 77 - jax.random.randint(jax.random.fold_in(_rk, 8), (4,), 0, max(1, 77 // 4) + 1, jnp.int32)
        _ctx_1024P = jax.random.normal(jax.random.fold_in(_rk, 11), (4, 16, 128), jnp.float32)
        _ctx_1024c = jax.random.dirichlet(jax.random.fold_in(_rk, 511), 0.3 * jnp.ones((16,), jnp.float32), (4, 77))
        _ctx_1024t = jnp.einsum('bsk,bkd->bsd', _ctx_1024c, _ctx_1024P)
        _ctx_1024t = _ctx_1024t * jax.lax.rsqrt(jnp.mean(jnp.square(_ctx_1024t)) + 1e-12) * 0.953939
        ctx_1024 = -1.39393e-06 + 0.999914 * (_ctx_1024t + 0.3 * jax.random.normal(jax.random.fold_in(_rk, 611), (4, 77, 128), jnp.float32))
        _validS = jnp.arange(512)[None, :] < _lenS[:, None]
        _validS2 = jnp.arange(77)[None, :] < _lenS2[:, None]
        _causal = jnp.tril(jnp.ones((512, 512), dtype=bool))
        mask_BxS2_bk1 = jnp.broadcast_to(_validS2[:, :], (4, 77))
        return (x, ctx_1024, mask_BxS2_bk1)
    x, ctx_1024, mask_BxS2_bk1 = _rec_inputs()

    def _L0_attn_setup():
        import jax, jax.numpy as jnp
        import numpy as np
        B, T, D = (2, 256, 128)
        HV, HK = (16, 8)
        DK, DV = (64, 64)
        K_DIM = HK * DK
        V_DIM = HV * DV
        CONV_DIM = 2 * K_DIM + V_DIM
        KS = 4
        EPS = 1e-06

        def _causal_conv_silu(x, w):
            xp = jnp.pad(x, ((0, 0), (KS - 1, 0), (0, 0)))
            y = sum((xp[:, i:i + x.shape[1], :] * w[:, i] for i in range(KS)))
            return jax.nn.silu(y)

        def _l2norm(x):
            return x * jax.lax.rsqrt(jnp.sum(x * x, -1, keepdims=True) + EPS)

        def _forward(hidden_states, W_qkv, W_z, W_b, W_a, dt_bias, A_log, conv_w, norm_w, W_out):
            b_, t_ = hidden_states.shape[:2]
            mixed_qkv = hidden_states @ W_qkv
            z = (hidden_states @ W_z).reshape(b_, t_, HV, DV)
            beta = jax.nn.sigmoid(hidden_states @ W_b)
            g = -jnp.exp(A_log) * jax.nn.softplus(hidden_states @ W_a + dt_bias)
            mixed_qkv = _causal_conv_silu(mixed_qkv, conv_w)
            q, k, v = jnp.split(mixed_qkv, [K_DIM, 2 * K_DIM], axis=-1)
            q = q.reshape(b_, t_, HK, DK)
            k = k.reshape(b_, t_, HK, DK)
            v = v.reshape(b_, t_, HV, DV)
            rep = HV // HK
            q = jnp.repeat(q, rep, axis=2)
            k = jnp.repeat(k, rep, axis=2)
            q = _l2norm(q) * DK ** (-0.5)
            k = _l2norm(k)
            qT = q.transpose(1, 0, 2, 3)
            kT = k.transpose(1, 0, 2, 3)
            vT = v.transpose(1, 0, 2, 3)
            gT = g.transpose(1, 0, 2)
            bT = beta.transpose(1, 0, 2)

            def step(S, xs):
                q_t, k_t, v_t, g_t, b_t = xs
                S = S * jnp.exp(g_t)[..., None, None]
                kv = jnp.einsum('bhk,bhkv->bhv', k_t, S)
                S = S + jnp.einsum('bhk,bhv->bhkv', k_t, (v_t - kv) * b_t[..., None])
                o_t = jnp.einsum('bhk,bhkv->bhv', q_t, S)
                return (S, o_t)
            S0 = jnp.zeros((b_, HV, DK, DV), jnp.float32)
            _, oT = jax.lax.scan(step, S0, (qT, kT, vT, gT, bT))
            o = oT.transpose(1, 0, 2, 3)
            var = jnp.mean(o * o, axis=-1, keepdims=True)
            o = o * jax.lax.rsqrt(var + EPS) * norm_w * jax.nn.silu(z)
            return o.reshape(b_, t_, V_DIM) @ W_out
        key = jax.random.key(seed)
        ks = jax.random.split(key, 9)
        g = lambda k, shape, sc: jax.random.normal(k, shape, jnp.float32) * sc
        return {'hidden_states': g(ks[0], (B, T, D), 1.0), 'W_qkv': g(ks[1], (D, CONV_DIM), 0.02), 'W_z': g(ks[2], (D, V_DIM), 0.02), 'W_b': g(ks[3], (D, HV), 0.02), 'W_a': g(ks[4], (D, HV), 0.02), 'dt_bias': jnp.ones((HV,), jnp.float32), 'A_log': jnp.log(jax.random.uniform(ks[5], (HV,), jnp.float32, 0.001, 16.0)), 'conv_w': g(ks[6], (CONV_DIM, KS), 0.2), 'norm_w': jnp.ones((DV,), jnp.float32), 'W_out': g(ks[7], (V_DIM, D), 0.02)}
    _L0_attn_all = _L0_attn_setup()
    _L0_attn_in = {k: v for k, v in _L0_attn_all.items() if k in ('W_qkv', 'W_z', 'W_b', 'W_a', 'dt_bias', 'A_log', 'conv_w', 'norm_w', 'W_out')}
    del _L0_attn_all

    def _L0_xattn_setup():
        import jax, jax.numpy as jnp
        import numpy as np
        D_MODEL = 128
        N_HEAD = 16
        D_K = D_MODEL // N_HEAD
        key = jax.random.key(seed)
        ks = jax.random.split(key, 12)
        B, S = (2, 256)
        s = 1.0 / np.sqrt(D_MODEL)
        return {'query': jax.random.normal(ks[0], (B, S, D_MODEL), jnp.float32), 'key': jax.random.normal(ks[1], (B, S, D_MODEL), jnp.float32), 'value': jax.random.normal(ks[2], (B, S, D_MODEL), jnp.float32), 'Wq': jax.random.normal(ks[3], (D_MODEL, D_MODEL), jnp.float32) * s, 'bq': jnp.zeros((D_MODEL,), jnp.float32), 'Wk': jax.random.normal(ks[4], (D_MODEL, D_MODEL), jnp.float32) * s, 'bk': jnp.zeros((D_MODEL,), jnp.float32), 'Wv': jax.random.normal(ks[5], (D_MODEL, D_MODEL), jnp.float32) * s, 'bv': jnp.zeros((D_MODEL,), jnp.float32), 'Wo': jax.random.normal(ks[6], (D_MODEL, D_MODEL), jnp.float32) * s, 'bo': jnp.zeros((D_MODEL,), jnp.float32)}
    _L0_xattn_all = _L0_xattn_setup()
    _L0_xattn_in = {k: v for k, v in _L0_xattn_all.items() if k in ('Wq', 'bq', 'Wk', 'bk', 'Wv', 'bv', 'Wo', 'bo')}
    del _L0_xattn_all

    def _L0_ffn_setup():
        import jax, jax.numpy as jnp
        import numpy as np
        DIM = 128
        INTER = 64
        E = 16
        TOPK = 4
        N_GROUPS = 4
        TOPK_GROUPS = 2
        ROUTE_SCALE = 1.0
        INIT_STD = 0.02
        B, S = (2, 128)
        key = jax.random.key(seed)
        ks = jax.random.split(key, 8)
        return {'x': jax.random.normal(ks[0], (B, S, DIM), jnp.float32), 'gate_w': jax.random.normal(ks[1], (E, DIM), jnp.float32) * INIT_STD, 'gate_bias': jnp.zeros((E,), jnp.float32), 'w1': jax.random.normal(ks[2], (E, INTER, DIM), jnp.float32) * INIT_STD, 'w2': jax.random.normal(ks[3], (E, DIM, INTER), jnp.float32) * INIT_STD, 'w3': jax.random.normal(ks[4], (E, INTER, DIM), jnp.float32) * INIT_STD, 'ws1': jax.random.normal(ks[5], (INTER, DIM), jnp.float32) * INIT_STD, 'ws2': jax.random.normal(ks[6], (DIM, INTER), jnp.float32) * INIT_STD, 'ws3': jax.random.normal(ks[7], (INTER, DIM), jnp.float32) * INIT_STD}
    _L0_ffn_all = _L0_ffn_setup()
    _L0_ffn_in = {k: v for k, v in _L0_ffn_all.items() if k in ('gate_w', 'gate_bias', 'w1', 'w2', 'w3', 'ws1', 'ws2', 'ws3')}
    del _L0_ffn_all

    def _L1_attn_setup():
        import jax, jax.numpy as jnp
        import numpy as np
        N_HEAD = 16
        LATENT = 32

        def _rotate_half(x):
            xe = x[..., ::2]
            xo = x[..., 1::2]
            return jnp.stack((-xo, xe), axis=-1).reshape(x.shape)

        def _rope_tables(T, latent_dim, dtype):
            inv_freq = 1.0 / 10000.0 ** (jnp.arange(0, latent_dim, 2, dtype=jnp.float32) / latent_dim)
            t = jnp.arange(T, dtype=jnp.float32)
            freqs = jnp.outer(t, inv_freq)
            cos = jnp.repeat(jnp.cos(freqs), 2, axis=-1)[:, :latent_dim]
            sin = jnp.repeat(jnp.sin(freqs), 2, axis=-1)[:, :latent_dim]
            return (cos.astype(dtype), sin.astype(dtype))
        key = jax.random.key(seed)
        ks = jax.random.split(key, 14)
        C = 128
        hd = C // N_HEAD
        L = LATENT
        s = 0.02
        return {'x': jax.random.normal(ks[0], (4, 256, C), jnp.float32), 'c_attn_w': jax.random.normal(ks[1], (3 * C, C), jnp.float32) * s, 'c_attn_b': jnp.zeros((3 * C,), jnp.float32), 'q2l_w': jax.random.normal(ks[2], (L, hd), jnp.float32) * s, 'q2l_b': jnp.zeros((L,), jnp.float32), 'kv2l_w': jax.random.normal(ks[3], (L, hd), jnp.float32) * s, 'kv2l_b': jnp.zeros((L,), jnp.float32), 'l2o_w': jax.random.normal(ks[4], (hd, L), jnp.float32) * s, 'l2o_b': jnp.zeros((hd,), jnp.float32), 'wqk_w': jax.random.normal(ks[5], (L, L), jnp.float32) * s, 'wqk_b': jnp.zeros((L,), jnp.float32), 'cproj_w': jax.random.normal(ks[6], (C, C), jnp.float32) * s, 'cproj_b': jnp.zeros((C,), jnp.float32)}
    _L1_attn_all = _L1_attn_setup()
    _L1_attn_in = {k: v for k, v in _L1_attn_all.items() if k in ('c_attn_w', 'c_attn_b', 'q2l_w', 'q2l_b', 'kv2l_w', 'kv2l_b', 'l2o_w', 'l2o_b', 'wqk_w', 'wqk_b', 'cproj_w', 'cproj_b')}
    del _L1_attn_all

    def _L1_xattn_setup():
        import jax, jax.numpy as jnp
        import numpy as np
        EMBED_DIM = 128
        NUM_HEADS = 16
        HEAD_DIM = EMBED_DIM // NUM_HEADS
        key = jax.random.key(seed)
        ks = jax.random.split(key, 11)
        B, S, D = (2, 256, EMBED_DIM)
        scale = 1.0 / np.sqrt(D)
        inp = {'query': jax.random.normal(ks[0], (B, S, D), dtype=jnp.float32), 'key': jax.random.normal(ks[1], (B, S, D), dtype=jnp.float32), 'value': jax.random.normal(ks[2], (B, S, D), dtype=jnp.float32), 'Wq': jax.random.normal(ks[3], (D, D), dtype=jnp.float32) * scale, 'bq': jnp.zeros((D,), dtype=jnp.float32), 'Wk': jax.random.normal(ks[4], (D, D), dtype=jnp.float32) * scale, 'bk': jnp.zeros((D,), dtype=jnp.float32), 'Wv': jax.random.normal(ks[5], (D, D), dtype=jnp.float32) * scale, 'bv': jnp.zeros((D,), dtype=jnp.float32), 'Wo': jax.random.normal(ks[6], (D, D), dtype=jnp.float32) * scale, 'bo': jnp.zeros((D,), dtype=jnp.float32)}
        return inp
    _L1_xattn_all = _L1_xattn_setup()
    _L1_xattn_in = {k: v for k, v in _L1_xattn_all.items() if k in ('Wq', 'bq', 'Wk', 'bk', 'Wv', 'bv', 'Wo', 'bo')}
    del _L1_xattn_all

    def _L1_ffn_setup():
        import jax, jax.numpy as jnp
        import numpy as np
        B, S, D, E, F, K = (4, 128, 128, 8, 352, 1)
        key = jax.random.key(seed)
        ks = jax.random.split(key, 8)
        sc = 0.02
        return {'x_bsD': jax.random.normal(ks[0], (B, S, D), jnp.float32), 'router_DE': jax.random.normal(ks[1], (D, E), jnp.float32) * sc, 'w1_eDF': jax.random.normal(ks[2], (E, D, F), jnp.float32) * sc, 'w3_eDF': jax.random.normal(ks[3], (E, D, F), jnp.float32) * sc, 'w2_eFD': jax.random.normal(ks[4], (E, F, D), jnp.float32) * sc, 'ws1_DF': jax.random.normal(ks[5], (D, F), jnp.float32) * sc, 'ws3_DF': jax.random.normal(ks[6], (D, F), jnp.float32) * sc, 'ws2_FD': jax.random.normal(ks[7], (F, D), jnp.float32) * sc}
    _L1_ffn_all = _L1_ffn_setup()
    _L1_ffn_in = {k: v for k, v in _L1_ffn_all.items() if k in ('router_DE', 'w1_eDF', 'w3_eDF', 'w2_eFD', 'ws1_DF', 'ws3_DF', 'ws2_FD')}
    del _L1_ffn_all

    def _L2_attn_setup():
        import jax, jax.numpy as jnp
        import numpy as np
        EMB = 128
        HEADS = 16
        HEADSIZE = EMB // HEADS
        EPS = 1e-05

        def _layernorm(x, g, b):
            m = jnp.mean(x, axis=-1, keepdims=True)
            v = jnp.mean((x - m) ** 2, axis=-1, keepdims=True)
            return (x - m) * jax.lax.rsqrt(v + EPS) * g + b
        key = jax.random.key(seed)
        ks = jax.random.split(key, 6)
        B, T = (4, 256)
        s = 1.0 / np.sqrt(EMB)
        return {'x': jax.random.normal(ks[0], (B, T, EMB), dtype=jnp.float32), 'Wk': jax.random.normal(ks[1], (EMB, EMB), dtype=jnp.float32) * s, 'Wq': jax.random.normal(ks[2], (EMB, EMB), dtype=jnp.float32) * s, 'Wv': jax.random.normal(ks[3], (EMB, EMB), dtype=jnp.float32) * s, 'Wo': jax.random.normal(ks[4], (EMB, EMB), dtype=jnp.float32) * s, 'bo': jnp.zeros((EMB,), dtype=jnp.float32), 'kln_g': jnp.ones((HEADSIZE,), dtype=jnp.float32), 'kln_b': jnp.zeros((HEADSIZE,), dtype=jnp.float32), 'qln_g': jnp.ones((HEADSIZE,), dtype=jnp.float32), 'qln_b': jnp.zeros((HEADSIZE,), dtype=jnp.float32)}
    _L2_attn_all = _L2_attn_setup()
    _L2_attn_in = {k: v for k, v in _L2_attn_all.items() if k in ('Wk', 'Wq', 'Wv', 'Wo', 'bo', 'kln_g', 'kln_b', 'qln_g', 'qln_b')}
    del _L2_attn_all

    def _L2_xattn_setup():
        import jax, jax.numpy as jnp
        import numpy as np
        B, N, M = (4, 128, 512)
        DQ, DC = (128, 128)
        H, DH = (16, 64)
        INNER = H * DH
        SCALE = DH ** (-0.5)
        key = jax.random.key(seed)
        ks = jax.random.split(key, 6)
        x = jax.random.normal(ks[0], (B, N, DQ), dtype=jnp.float32)
        context = jax.random.normal(ks[1], (B, M, DC), dtype=jnp.float32)
        mask = jax.random.bernoulli(ks[2], 0.9, (B, M))
        Wq = jax.random.normal(ks[3], (DQ, INNER), dtype=jnp.float32) / np.sqrt(DQ)
        Wkv = jax.random.normal(ks[4], (DC, 2 * INNER), dtype=jnp.float32) / np.sqrt(DC)
        Wo = jax.random.normal(ks[5], (INNER, DQ), dtype=jnp.float32) / np.sqrt(INNER)
        bo = jnp.zeros((DQ,), dtype=jnp.float32)
        return {'x': x, 'context': context, 'mask': mask, 'Wq': Wq, 'Wkv': Wkv, 'Wo': Wo, 'bo': bo}
    _L2_xattn_all = _L2_xattn_setup()
    _L2_xattn_in = {k: v for k, v in _L2_xattn_all.items() if k in ('Wq', 'Wkv', 'Wo', 'bo')}
    del _L2_xattn_all

    def _L2_ffn_setup():
        import jax, jax.numpy as jnp
        import numpy as np
        from jax import lax
        H, DK, DV, N_EXP, CHUNK = (8, 64, 64, 4, 64)
        LORA, GATE_LR = (64, 16)
        NORMALIZER = 16.0
        EPS = 1e-05

        def chunk_gla(q, k, v, gk, C=CHUNK):
            L, h, dk = q.shape
            dv = v.shape[-1]
            nc = L // C
            qc, kc, vc, gc = (t.reshape(nc, C, h, -1) for t in (q, k, v, gk))
            g = jnp.cumsum(gc, axis=1)
            g_last = g[:, -1]
            qg = qc * jnp.exp(g)
            kg = kc * jnp.exp(-g)
            A = jnp.einsum('cthd,cshd->chts', qg, kg)
            A = A * jnp.tril(jnp.ones((C, C), q.dtype))
            o_intra = jnp.einsum('chts,cshe->cthe', A, vc)
            k_out = kc * jnp.exp(g_last[:, None] - g)
            chunk_kv = jnp.einsum('cthd,cthe->chde', k_out, vc)
            decay = jnp.exp(g_last)

            def step(S, inp):
                kv, dec, qg_c = inp
                o_inter = jnp.einsum('thd,hde->the', qg_c, S)
                return (S * dec[..., None] + kv, o_inter)
            S0 = jnp.zeros((h, dk, dv), q.dtype)
            _, o_inter = lax.scan(step, S0, (chunk_kv, decay, qg))
            return (o_intra + o_inter).reshape(L, h, dv)
        key = jax.random.key(seed)
        ks = jax.random.split(key, 20)
        B, L, Dh = (1, 512, 128)
        KD, VD = (H * DK, H * DV)
        w = lambda i, shape: jax.random.normal(ks[i], shape, jnp.float32) * 0.02
        return {'x': jax.random.normal(ks[0], (B, L, Dh), jnp.float32), 'Wq': w(1, (Dh, KD)), 'Wk': w(2, (Dh, KD)), 'Wv': w(3, (Dh, VD)), 'Wqa': w(4, (Dh, LORA)), 'Wqb': w(5, (LORA, KD)), 'Wka': w(6, (Dh, LORA)), 'Wkb': w(7, (LORA, KD)), 'Wg1a': w(8, (Dh, GATE_LR)), 'Wg1b': w(9, (GATE_LR, KD)), 'bg1': jnp.zeros((KD,), jnp.float32), 'Wg2a': w(10, (Dh, GATE_LR)), 'Wg2b': w(11, (GATE_LR, KD)), 'bg2': jnp.zeros((KD,), jnp.float32), 'We': w(12, (Dh, N_EXP)), 'Wga': w(13, (Dh, LORA)), 'Wgb': w(14, (LORA, VD)), 'norm_w': jnp.ones((DV,), jnp.float32), 'Wo': w(15, (VD, Dh))}
    _L2_ffn_all = _L2_ffn_setup()
    _L2_ffn_in = {k: v for k, v in _L2_ffn_all.items() if k in ('Wq', 'Wk', 'Wv', 'Wqa', 'Wqb', 'Wka', 'Wkb', 'Wg1a', 'Wg1b', 'bg1', 'Wg2a', 'Wg2b', 'bg2', 'We', 'Wga', 'Wgb', 'norm_w', 'Wo')}
    del _L2_ffn_all

    def _L3_attn_setup():
        import jax, jax.numpy as jnp
        import numpy as np
        D_MODEL = 128
        D_STATE = 64
        D_CONV = 4
        EXPAND = 2
        HEADDIM = 128
        BLOCK_LEN = 64
        D_INNER = EXPAND * D_MODEL
        NHEADS = D_INNER // HEADDIM

        def _segsum(a):
            T = a.shape[-1]
            cs = jnp.cumsum(a, axis=-1)
            seg = cs[..., :, None] - cs[..., None, :]
            mask = jnp.tril(jnp.ones((T, T), dtype=bool))
            return jnp.where(mask, seg, -jnp.inf)

        def _ssd_minimal(X, A, Bm, Cm, blk):
            b, l, h, p = X.shape
            c = l // blk
            X = X.reshape(b, c, blk, h, p)
            A = A.reshape(b, c, blk, h).transpose(0, 3, 1, 2)
            Bm = Bm.reshape(b, c, blk, h, -1)
            Cm = Cm.reshape(b, c, blk, h, -1)
            A_cs = jnp.cumsum(A, axis=-1)
            Lmat = jnp.exp(_segsum(A))
            Y_diag = jnp.einsum('bclhn,bcshn,bhcls,bcshp->bclhp', Cm, Bm, Lmat, X)
            decay_states = jnp.exp(A_cs[..., -1:] - A_cs)
            states = jnp.einsum('bclhn,bhcl,bclhp->bchpn', Bm, decay_states, X)
            init = jnp.zeros_like(states[:, :1])
            states = jnp.concatenate([init, states], axis=1)
            A_last = jnp.pad(A_cs[..., -1], ((0, 0), (0, 0), (1, 0)))
            decay_chunk = jnp.exp(_segsum(A_last))
            new_states = jnp.einsum('bhzc,bchpn->bzhpn', decay_chunk, states)
            states, final_state = (new_states[:, :-1], new_states[:, -1])
            out_decay = jnp.exp(A_cs)
            Y_off = jnp.einsum('bclhn,bchpn,bhcl->bclhp', Cm, states, out_decay)
            Y = (Y_diag + Y_off).reshape(b, l, h, p)
            return (Y, final_state)

        def _forward(inp, W_in, conv_w, conv_b, W_ssm, A_log, D_skip, dt_bias, W_out):
            B, L, _ = inp.shape
            H, P, N, k = (NHEADS, HEADDIM, D_STATE, D_CONV)
            xz = inp @ W_in.T
            x, z = jnp.split(xz, 2, axis=-1)
            xc = x.transpose(0, 2, 1)
            y_conv = jax.lax.conv_general_dilated(xc, conv_w, window_strides=(1,), padding=[(k - 1, 0)], dimension_numbers=('NCH', 'OIH', 'NCH'), feature_group_count=D_INNER)
            y_conv = y_conv + conv_b[None, :, None]
            conv_state = xc[..., -(k - 1):]
            x = y_conv.transpose(0, 2, 1)
            x = x * jax.nn.sigmoid(x)
            ssm_params = x @ W_ssm.T
            dt_raw = ssm_params[..., :H]
            B_raw = ssm_params[..., H:H + H * N]
            C_raw = ssm_params[..., H + H * N:]
            dt = jax.nn.softplus(dt_raw + dt_bias[None, None, :])
            B_mat = B_raw.reshape(B, L, H, N)
            C_mat = C_raw.reshape(B, L, H, N)
            X = x.reshape(B, L, H, P)
            A_cont = -jnp.exp(A_log)
            A_disc = dt * A_cont[None, None, :]
            X_disc = X * dt[..., None]
            Y_heads, ssm_state = _ssd_minimal(X_disc, A_disc, B_mat, C_mat, BLOCK_LEN)
            Y_heads = Y_heads + D_skip[None, None, :, None] * X
            y = Y_heads.reshape(B, L, D_INNER)
            y = y * jax.nn.sigmoid(z)
            out = y @ W_out.T
            return (out, conv_state, ssm_state)

        def _reference_tuple_inner(inp, W_in, conv_w, conv_b, W_ssm, A_log, D_skip, dt_bias, W_out):
            return _forward(inp, W_in, conv_w, conv_b, W_ssm, A_log, D_skip, dt_bias, W_out)
        key = jax.random.key(seed)
        ks = jax.random.split(key, 10)
        B, L = (2, 256)
        inp = jax.random.normal(ks[0], (B, L, D_MODEL), dtype=jnp.float32)
        s_in = 1.0 / np.sqrt(D_MODEL)
        s_inner = 1.0 / np.sqrt(D_INNER)
        W_in = jax.random.uniform(ks[1], (2 * D_INNER, D_MODEL), minval=-s_in, maxval=s_in)
        conv_w = jax.random.uniform(ks[2], (D_INNER, 1, D_CONV), minval=-0.5, maxval=0.5)
        conv_b = jax.random.uniform(ks[3], (D_INNER,), minval=-0.5, maxval=0.5)
        W_ssm = jax.random.uniform(ks[4], (NHEADS + 2 * NHEADS * D_STATE, D_INNER), minval=-s_inner, maxval=s_inner)
        A = jax.random.uniform(ks[5], (NHEADS,), minval=1.0, maxval=16.0)
        A_log = jnp.log(A)
        D_skip = jnp.ones((NHEADS,), dtype=jnp.float32)
        dt = jnp.exp(jax.random.uniform(ks[6], (NHEADS,)) * (np.log(0.1) - np.log(0.001)) + np.log(0.001))
        dt = jnp.clip(dt, 0.0001, None)
        dt_bias = dt + jnp.log(-jnp.expm1(-dt))
        W_out = jax.random.uniform(ks[7], (D_MODEL, D_INNER), minval=-s_inner, maxval=s_inner)
        return {'inp': inp, 'W_in': W_in, 'conv_w': conv_w, 'conv_b': conv_b, 'W_ssm': W_ssm, 'A_log': A_log, 'D_skip': D_skip, 'dt_bias': dt_bias, 'W_out': W_out}
    _L3_attn_all = _L3_attn_setup()
    _L3_attn_in = {k: v for k, v in _L3_attn_all.items() if k in ('W_in', 'conv_w', 'conv_b', 'W_ssm', 'A_log', 'D_skip', 'dt_bias', 'W_out')}
    del _L3_attn_all

    def _L3_xattn_setup():
        import jax, jax.numpy as jnp
        import numpy as np
        B, N, D, K = (4, 512, 128, 128)
        key = jax.random.key(seed)
        ks = jax.random.split(key, 5)
        q = jax.random.normal(ks[0], (B, N, D), dtype=jnp.float32)
        k = jax.random.normal(ks[1], (B, N, D), dtype=jnp.float32)
        weight = jax.random.normal(ks[2], (D, K), dtype=jnp.float32)
        kp_w = jax.random.normal(ks[3], (D, D), dtype=jnp.float32) * (1.0 / np.sqrt(D))
        kp_b = jax.random.normal(ks[4], (D,), dtype=jnp.float32) * 0.01
        return {'q': q, 'k': k, 'weight': weight, 'kp_w': kp_w, 'kp_b': kp_b}
    _L3_xattn_all = _L3_xattn_setup()
    _L3_xattn_in = {k: v for k, v in _L3_xattn_all.items() if k in ('weight', 'kp_w', 'kp_b')}
    del _L3_xattn_all

    def _L3_ffn_setup():
        import jax, jax.numpy as jnp
        import numpy as np
        H = 128
        I = 256
        E = 8
        B, S = (2, 512)
        EPS = 1e-05
        INIT = 0.02

        def _layernorm(x, w, b):
            mu = jnp.mean(x, axis=-1, keepdims=True)
            var = jnp.mean(jnp.square(x - mu), axis=-1, keepdims=True)
            return (x - mu) * jax.lax.rsqrt(var + EPS) * w + b
        key = jax.random.key(seed)
        ks = jax.random.split(key, 9)
        return {'hidden_states': jax.random.normal(ks[0], (B, S, H), jnp.float32), 'ln_w': jnp.ones((H,), jnp.float32), 'ln_b': jnp.zeros((H,), jnp.float32), 'router_w': jax.random.normal(ks[1], (H, E), jnp.float32) * INIT, 'gate_w': jax.random.normal(ks[2], (E, H, I), jnp.float32) * INIT, 'up_w': jax.random.normal(ks[3], (E, H, I), jnp.float32) * INIT, 'down_w': jax.random.normal(ks[4], (E, I, H), jnp.float32) * INIT, 'sh_gate': jax.random.normal(ks[5], (H, I), jnp.float32) * INIT, 'sh_up': jax.random.normal(ks[6], (H, I), jnp.float32) * INIT, 'sh_down': jax.random.normal(ks[7], (I, H), jnp.float32) * INIT}
    _L3_ffn_all = _L3_ffn_setup()
    _L3_ffn_in = {k: v for k, v in _L3_ffn_all.items() if k in ('ln_w', 'ln_b', 'router_w', 'gate_w', 'up_w', 'down_w', 'sh_gate', 'sh_up', 'sh_down')}
    del _L3_ffn_all
    return {'x': x, 'ctx_1024': ctx_1024, 'mask_BxS2_bk1': mask_BxS2_bk1, 'L0_attn_W_qkv': _L0_attn_in['W_qkv'], 'L0_attn_W_z': _L0_attn_in['W_z'], 'L0_attn_W_b': _L0_attn_in['W_b'], 'L0_attn_W_a': _L0_attn_in['W_a'], 'L0_attn_dt_bias': _L0_attn_in['dt_bias'], 'L0_attn_A_log': _L0_attn_in['A_log'], 'L0_attn_conv_w': _L0_attn_in['conv_w'], 'L0_attn_norm_w': _L0_attn_in['norm_w'], 'L0_attn_W_out': _L0_attn_in['W_out'], 'L0_xattn_Wq': _L0_xattn_in['Wq'], 'L0_xattn_bq': _L0_xattn_in['bq'], 'L0_xattn_Wk': _L0_xattn_in['Wk'], 'L0_xattn_bk': _L0_xattn_in['bk'], 'L0_xattn_Wv': _L0_xattn_in['Wv'], 'L0_xattn_bv': _L0_xattn_in['bv'], 'L0_xattn_Wo': _L0_xattn_in['Wo'], 'L0_xattn_bo': _L0_xattn_in['bo'], 'L0_ffn_gate_w': _L0_ffn_in['gate_w'], 'L0_ffn_gate_bias': _L0_ffn_in['gate_bias'], 'L0_ffn_w1': _L0_ffn_in['w1'], 'L0_ffn_w2': _L0_ffn_in['w2'], 'L0_ffn_w3': _L0_ffn_in['w3'], 'L0_ffn_ws1': _L0_ffn_in['ws1'], 'L0_ffn_ws2': _L0_ffn_in['ws2'], 'L0_ffn_ws3': _L0_ffn_in['ws3'], 'L1_attn_c_attn_w': _L1_attn_in['c_attn_w'], 'L1_attn_c_attn_b': _L1_attn_in['c_attn_b'], 'L1_attn_q2l_w': _L1_attn_in['q2l_w'], 'L1_attn_q2l_b': _L1_attn_in['q2l_b'], 'L1_attn_kv2l_w': _L1_attn_in['kv2l_w'], 'L1_attn_kv2l_b': _L1_attn_in['kv2l_b'], 'L1_attn_l2o_w': _L1_attn_in['l2o_w'], 'L1_attn_l2o_b': _L1_attn_in['l2o_b'], 'L1_attn_wqk_w': _L1_attn_in['wqk_w'], 'L1_attn_wqk_b': _L1_attn_in['wqk_b'], 'L1_attn_cproj_w': _L1_attn_in['cproj_w'], 'L1_attn_cproj_b': _L1_attn_in['cproj_b'], 'L1_xattn_Wq': _L1_xattn_in['Wq'], 'L1_xattn_bq': _L1_xattn_in['bq'], 'L1_xattn_Wk': _L1_xattn_in['Wk'], 'L1_xattn_bk': _L1_xattn_in['bk'], 'L1_xattn_Wv': _L1_xattn_in['Wv'], 'L1_xattn_bv': _L1_xattn_in['bv'], 'L1_xattn_Wo': _L1_xattn_in['Wo'], 'L1_xattn_bo': _L1_xattn_in['bo'], 'L1_ffn_router_DE': _L1_ffn_in['router_DE'], 'L1_ffn_w1_eDF': _L1_ffn_in['w1_eDF'], 'L1_ffn_w3_eDF': _L1_ffn_in['w3_eDF'], 'L1_ffn_w2_eFD': _L1_ffn_in['w2_eFD'], 'L1_ffn_ws1_DF': _L1_ffn_in['ws1_DF'], 'L1_ffn_ws3_DF': _L1_ffn_in['ws3_DF'], 'L1_ffn_ws2_FD': _L1_ffn_in['ws2_FD'], 'L2_attn_Wk': _L2_attn_in['Wk'], 'L2_attn_Wq': _L2_attn_in['Wq'], 'L2_attn_Wv': _L2_attn_in['Wv'], 'L2_attn_Wo': _L2_attn_in['Wo'], 'L2_attn_bo': _L2_attn_in['bo'], 'L2_attn_kln_g': _L2_attn_in['kln_g'], 'L2_attn_kln_b': _L2_attn_in['kln_b'], 'L2_attn_qln_g': _L2_attn_in['qln_g'], 'L2_attn_qln_b': _L2_attn_in['qln_b'], 'L2_xattn_Wq': _L2_xattn_in['Wq'], 'L2_xattn_Wkv': _L2_xattn_in['Wkv'], 'L2_xattn_Wo': _L2_xattn_in['Wo'], 'L2_xattn_bo': _L2_xattn_in['bo'], 'L2_ffn_Wq': _L2_ffn_in['Wq'], 'L2_ffn_Wk': _L2_ffn_in['Wk'], 'L2_ffn_Wv': _L2_ffn_in['Wv'], 'L2_ffn_Wqa': _L2_ffn_in['Wqa'], 'L2_ffn_Wqb': _L2_ffn_in['Wqb'], 'L2_ffn_Wka': _L2_ffn_in['Wka'], 'L2_ffn_Wkb': _L2_ffn_in['Wkb'], 'L2_ffn_Wg1a': _L2_ffn_in['Wg1a'], 'L2_ffn_Wg1b': _L2_ffn_in['Wg1b'], 'L2_ffn_bg1': _L2_ffn_in['bg1'], 'L2_ffn_Wg2a': _L2_ffn_in['Wg2a'], 'L2_ffn_Wg2b': _L2_ffn_in['Wg2b'], 'L2_ffn_bg2': _L2_ffn_in['bg2'], 'L2_ffn_We': _L2_ffn_in['We'], 'L2_ffn_Wga': _L2_ffn_in['Wga'], 'L2_ffn_Wgb': _L2_ffn_in['Wgb'], 'L2_ffn_norm_w': _L2_ffn_in['norm_w'], 'L2_ffn_Wo': _L2_ffn_in['Wo'], 'L3_attn_W_in': _L3_attn_in['W_in'], 'L3_attn_conv_w': _L3_attn_in['conv_w'], 'L3_attn_conv_b': _L3_attn_in['conv_b'], 'L3_attn_W_ssm': _L3_attn_in['W_ssm'], 'L3_attn_A_log': _L3_attn_in['A_log'], 'L3_attn_D_skip': _L3_attn_in['D_skip'], 'L3_attn_dt_bias': _L3_attn_in['dt_bias'], 'L3_attn_W_out': _L3_attn_in['W_out'], 'L3_xattn_weight': _L3_xattn_in['weight'], 'L3_xattn_kp_w': _L3_xattn_in['kp_w'], 'L3_xattn_kp_b': _L3_xattn_in['kp_b'], 'L3_ffn_ln_w': _L3_ffn_in['ln_w'], 'L3_ffn_ln_b': _L3_ffn_in['ln_b'], 'L3_ffn_router_w': _L3_ffn_in['router_w'], 'L3_ffn_gate_w': _L3_ffn_in['gate_w'], 'L3_ffn_up_w': _L3_ffn_in['up_w'], 'L3_ffn_down_w': _L3_ffn_in['down_w'], 'L3_ffn_sh_gate': _L3_ffn_in['sh_gate'], 'L3_ffn_sh_up': _L3_ffn_in['sh_up'], 'L3_ffn_sh_down': _L3_ffn_in['sh_down']}

def reference(x, ctx_1024, mask_BxS2_bk1, L0_attn_W_qkv, L0_attn_W_z, L0_attn_W_b, L0_attn_W_a, L0_attn_dt_bias, L0_attn_A_log, L0_attn_conv_w, L0_attn_norm_w, L0_attn_W_out, L0_xattn_Wq, L0_xattn_bq, L0_xattn_Wk, L0_xattn_bk, L0_xattn_Wv, L0_xattn_bv, L0_xattn_Wo, L0_xattn_bo, L0_ffn_gate_w, L0_ffn_gate_bias, L0_ffn_w1, L0_ffn_w2, L0_ffn_w3, L0_ffn_ws1, L0_ffn_ws2, L0_ffn_ws3, L1_attn_c_attn_w, L1_attn_c_attn_b, L1_attn_q2l_w, L1_attn_q2l_b, L1_attn_kv2l_w, L1_attn_kv2l_b, L1_attn_l2o_w, L1_attn_l2o_b, L1_attn_wqk_w, L1_attn_wqk_b, L1_attn_cproj_w, L1_attn_cproj_b, L1_xattn_Wq, L1_xattn_bq, L1_xattn_Wk, L1_xattn_bk, L1_xattn_Wv, L1_xattn_bv, L1_xattn_Wo, L1_xattn_bo, L1_ffn_router_DE, L1_ffn_w1_eDF, L1_ffn_w3_eDF, L1_ffn_w2_eFD, L1_ffn_ws1_DF, L1_ffn_ws3_DF, L1_ffn_ws2_FD, L2_attn_Wk, L2_attn_Wq, L2_attn_Wv, L2_attn_Wo, L2_attn_bo, L2_attn_kln_g, L2_attn_kln_b, L2_attn_qln_g, L2_attn_qln_b, L2_xattn_Wq, L2_xattn_Wkv, L2_xattn_Wo, L2_xattn_bo, L2_ffn_Wq, L2_ffn_Wk, L2_ffn_Wv, L2_ffn_Wqa, L2_ffn_Wqb, L2_ffn_Wka, L2_ffn_Wkb, L2_ffn_Wg1a, L2_ffn_Wg1b, L2_ffn_bg1, L2_ffn_Wg2a, L2_ffn_Wg2b, L2_ffn_bg2, L2_ffn_We, L2_ffn_Wga, L2_ffn_Wgb, L2_ffn_norm_w, L2_ffn_Wo, L3_attn_W_in, L3_attn_conv_w, L3_attn_conv_b, L3_attn_W_ssm, L3_attn_A_log, L3_attn_D_skip, L3_attn_dt_bias, L3_attn_W_out, L3_xattn_weight, L3_xattn_kp_w, L3_xattn_kp_b, L3_ffn_ln_w, L3_ffn_ln_b, L3_ffn_router_w, L3_ffn_gate_w, L3_ffn_up_w, L3_ffn_down_w, L3_ffn_sh_gate, L3_ffn_sh_up, L3_ffn_sh_down):
    import jax
    import jax.numpy as jnp

    def _L0_attn_ref(hidden_states, W_qkv, W_z, W_b, W_a, dt_bias, A_log, conv_w, norm_w, W_out):
        import jax, jax.numpy as jnp
        import numpy as np
        B, T, D = (2, 256, 128)
        HV, HK = (16, 8)
        DK, DV = (64, 64)
        K_DIM = HK * DK
        V_DIM = HV * DV
        CONV_DIM = 2 * K_DIM + V_DIM
        KS = 4
        EPS = 1e-06

        def _causal_conv_silu(x, w):
            xp = jnp.pad(x, ((0, 0), (KS - 1, 0), (0, 0)))
            y = sum((xp[:, i:i + x.shape[1], :] * w[:, i] for i in range(KS)))
            return jax.nn.silu(y)

        def _l2norm(x):
            return x * jax.lax.rsqrt(jnp.sum(x * x, -1, keepdims=True) + EPS)

        def _forward(hidden_states, W_qkv, W_z, W_b, W_a, dt_bias, A_log, conv_w, norm_w, W_out):
            b_, t_ = hidden_states.shape[:2]
            mixed_qkv = hidden_states @ W_qkv
            z = (hidden_states @ W_z).reshape(b_, t_, HV, DV)
            beta = jax.nn.sigmoid(hidden_states @ W_b)
            g = -jnp.exp(A_log) * jax.nn.softplus(hidden_states @ W_a + dt_bias)
            mixed_qkv = _causal_conv_silu(mixed_qkv, conv_w)
            q, k, v = jnp.split(mixed_qkv, [K_DIM, 2 * K_DIM], axis=-1)
            q = q.reshape(b_, t_, HK, DK)
            k = k.reshape(b_, t_, HK, DK)
            v = v.reshape(b_, t_, HV, DV)
            rep = HV // HK
            q = jnp.repeat(q, rep, axis=2)
            k = jnp.repeat(k, rep, axis=2)
            q = _l2norm(q) * DK ** (-0.5)
            k = _l2norm(k)
            qT = q.transpose(1, 0, 2, 3)
            kT = k.transpose(1, 0, 2, 3)
            vT = v.transpose(1, 0, 2, 3)
            gT = g.transpose(1, 0, 2)
            bT = beta.transpose(1, 0, 2)

            def step(S, xs):
                q_t, k_t, v_t, g_t, b_t = xs
                S = S * jnp.exp(g_t)[..., None, None]
                kv = jnp.einsum('bhk,bhkv->bhv', k_t, S)
                S = S + jnp.einsum('bhk,bhv->bhkv', k_t, (v_t - kv) * b_t[..., None])
                o_t = jnp.einsum('bhk,bhkv->bhv', q_t, S)
                return (S, o_t)
            S0 = jnp.zeros((b_, HV, DK, DV), jnp.float32)
            _, oT = jax.lax.scan(step, S0, (qT, kT, vT, gT, bT))
            o = oT.transpose(1, 0, 2, 3)
            var = jnp.mean(o * o, axis=-1, keepdims=True)
            o = o * jax.lax.rsqrt(var + EPS) * norm_w * jax.nn.silu(z)
            return o.reshape(b_, t_, V_DIM) @ W_out
        return _forward(hidden_states, W_qkv, W_z, W_b, W_a, dt_bias, A_log, conv_w, norm_w, W_out)

    def _L0_xattn_ref(query, key, value, Wq, bq, Wk, bk, Wv, bv, Wo, bo):
        import jax, jax.numpy as jnp
        import numpy as np
        D_MODEL = 128
        N_HEAD = 16
        D_K = D_MODEL // N_HEAD
        B, S, _ = query.shape
        q = query @ Wq.T + bq
        k = key @ Wk.T + bk
        v = value @ Wv.T + bv
        q = q.reshape(B, S, N_HEAD, D_K).transpose(0, 2, 1, 3)
        k = k.reshape(B, -1, N_HEAD, D_K).transpose(0, 2, 1, 3)
        v = v.reshape(B, -1, N_HEAD, D_K).transpose(0, 2, 1, 3)
        attn = jnp.einsum('bhqd,bhkd->bhqk', q, k) / jnp.sqrt(jnp.float32(D_K))
        attn = jax.nn.softmax(attn, axis=-1)
        out = jnp.einsum('bhqk,bhkd->bhqd', attn, v)
        out = out.transpose(0, 2, 1, 3).reshape(B, S, D_MODEL)
        return out @ Wo.T + bo

    def _L0_ffn_ref(x, gate_w, gate_bias, w1, w2, w3, ws1, ws2, ws3):
        import jax, jax.numpy as jnp
        import numpy as np
        DIM = 128
        INTER = 64
        E = 16
        TOPK = 4
        N_GROUPS = 4
        TOPK_GROUPS = 2
        ROUTE_SCALE = 1.0
        INIT_STD = 0.02
        B, S = (2, 128)
        Bx, Sx, D = x.shape
        T = Bx * Sx
        xf = x.reshape(T, D)
        scores = jax.nn.sigmoid(xf @ gate_w.T)
        original_scores = scores
        s = scores + gate_bias
        sg = s.reshape(T, N_GROUPS, E // N_GROUPS)
        group_scores = sg.max(axis=-1)
        _, gidx = jax.lax.top_k(group_scores, TOPK_GROUPS)
        keep = jnp.zeros((T, N_GROUPS), bool).at[jnp.arange(T)[:, None], gidx].set(True)
        s_masked = jnp.where(keep[:, :, None], sg, -jnp.inf).reshape(T, E)
        _, idx = jax.lax.top_k(s_masked, TOPK)
        weights = jnp.take_along_axis(original_scores, idx, axis=1) * ROUTE_SCALE
        comb = jnp.zeros((T, E), x.dtype).at[jnp.arange(T)[:, None], idx].add(weights)
        h1 = jnp.einsum('td,eid->tei', xf, w1)
        h3 = jnp.einsum('td,eid->tei', xf, w3)
        h = jax.nn.silu(h1) * h3
        y = jnp.einsum('tei,edi,te->td', h, w2, comb)
        z = jax.nn.silu(xf @ ws1.T) * (xf @ ws3.T) @ ws2.T
        return (y + z).reshape(Bx, Sx, D)

    def _L1_attn_ref(x, c_attn_w, c_attn_b, q2l_w, q2l_b, kv2l_w, kv2l_b, l2o_w, l2o_b, wqk_w, wqk_b, cproj_w, cproj_b):
        import jax, jax.numpy as jnp
        import numpy as np
        N_HEAD = 16
        LATENT = 32

        def _rotate_half(x):
            xe = x[..., ::2]
            xo = x[..., 1::2]
            return jnp.stack((-xo, xe), axis=-1).reshape(x.shape)

        def _rope_tables(T, latent_dim, dtype):
            inv_freq = 1.0 / 10000.0 ** (jnp.arange(0, latent_dim, 2, dtype=jnp.float32) / latent_dim)
            t = jnp.arange(T, dtype=jnp.float32)
            freqs = jnp.outer(t, inv_freq)
            cos = jnp.repeat(jnp.cos(freqs), 2, axis=-1)[:, :latent_dim]
            sin = jnp.repeat(jnp.sin(freqs), 2, axis=-1)[:, :latent_dim]
            return (cos.astype(dtype), sin.astype(dtype))
        B, T, C = x.shape
        H = N_HEAD
        hd = C // H
        L = q2l_w.shape[0]
        qkv = x @ c_attn_w.T + c_attn_b
        q, k, v = jnp.split(qkv, 3, axis=2)

        def heads(t):
            return t.reshape(B, T, H, hd).transpose(0, 2, 1, 3)
        q, k, v = (heads(q), heads(k), heads(v))
        q_lat = q @ q2l_w.T + q2l_b
        k_lat = k @ kv2l_w.T + kv2l_b
        v_lat = v @ kv2l_w.T + kv2l_b
        cos, sin = _rope_tables(T, L, x.dtype)
        cos = cos[None, None]
        sin = sin[None, None]
        q_lat = q_lat * cos + _rotate_half(q_lat) * sin
        k_lat = k_lat * cos + _rotate_half(k_lat) * sin
        q_for_k = q_lat @ wqk_w.T + wqk_b
        att = jnp.einsum('bhql,bhkl->bhqk', q_for_k, k_lat) * L ** (-0.5)
        causal = jnp.tril(jnp.ones((T, T), dtype=bool))
        att = jnp.where(causal[None, None], att, -jnp.inf)
        att = jax.nn.softmax(att, axis=-1)
        y_lat = jnp.einsum('bhqk,bhkl->bhql', att, v_lat)
        y = y_lat @ l2o_w.T + l2o_b
        y = y.transpose(0, 2, 1, 3).reshape(B, T, C)
        return y @ cproj_w.T + cproj_b

    def _L1_xattn_ref(query, key, value, Wq, bq, Wk, bk, Wv, bv, Wo, bo):
        import jax, jax.numpy as jnp
        import numpy as np
        EMBED_DIM = 128
        NUM_HEADS = 16
        HEAD_DIM = EMBED_DIM // NUM_HEADS
        B, Sq, D = query.shape
        Sk = key.shape[1]
        H, Hd = (NUM_HEADS, HEAD_DIM)
        Q = (query @ Wq.T + bq).reshape(B, Sq, H, Hd).transpose(0, 2, 1, 3)
        K = (key @ Wk.T + bk).reshape(B, Sk, H, Hd).transpose(0, 2, 1, 3)
        V = (value @ Wv.T + bv).reshape(B, Sk, H, Hd).transpose(0, 2, 1, 3)
        scores = jnp.einsum('bhqd,bhkd->bhqk', Q, K) / jnp.sqrt(jnp.float32(Hd))
        attn = jax.nn.softmax(scores, axis=-1)
        out = jnp.einsum('bhqk,bhkd->bhqd', attn, V)
        out = out.transpose(0, 2, 1, 3).reshape(B, Sq, D)
        return out @ Wo.T + bo

    def _L1_ffn_ref(x_bsD, router_DE, w1_eDF, w3_eDF, w2_eFD, ws1_DF, ws3_DF, ws2_FD):
        import jax, jax.numpy as jnp
        import numpy as np
        B, S, D, E, F, K = (4, 128, 128, 8, 352, 1)
        b, s, d = x_bsD.shape
        a = b * s
        x_aD = x_bsD.reshape(a, d)
        scores_aE = x_aD @ router_DE
        vals_aK, idx_aK = jax.lax.top_k(scores_aE, K)
        masked_aE = jnp.full_like(scores_aE, -jnp.inf).at[jnp.arange(a)[:, None], idx_aK].set(vals_aK)
        gates_Ea = jax.nn.sigmoid(masked_aE).T
        routed_in_EaD = jax.lax.stop_gradient(gates_Ea[:, :, None] * x_aD[None, :, :])
        mid_EaF = jax.nn.silu(jnp.einsum('ead,edf->eaf', routed_in_EaD, w1_eDF)) * jnp.einsum('ead,edf->eaf', routed_in_EaD, w3_eDF)
        routed_out_EaD = jnp.einsum('eaf,efd->ead', mid_EaF, w2_eFD)
        shared_aD = jax.nn.silu(x_aD @ ws1_DF) * (x_aD @ ws3_DF) @ ws2_FD
        out_aD = shared_aD + routed_out_EaD.sum(axis=0)
        return out_aD.reshape(b, s, d)

    def _L2_attn_ref(x, Wk, Wq, Wv, Wo, bo, kln_g, kln_b, qln_g, qln_b):
        import jax, jax.numpy as jnp
        import numpy as np
        EMB = 128
        HEADS = 16
        HEADSIZE = EMB // HEADS
        EPS = 1e-05

        def _layernorm(x, g, b):
            m = jnp.mean(x, axis=-1, keepdims=True)
            v = jnp.mean((x - m) ** 2, axis=-1, keepdims=True)
            return (x - m) * jax.lax.rsqrt(v + EPS) * g + b
        B, T, E = x.shape
        k = jnp.einsum('bte,fe->btf', x, Wk).reshape(B, T, HEADS, HEADSIZE)
        q = jnp.einsum('bte,fe->btf', x, Wq).reshape(B, T, HEADS, HEADSIZE)
        v = jnp.einsum('bte,fe->btf', x, Wv).reshape(B, T, HEADS, HEADSIZE)
        k = _layernorm(k, kln_g, kln_b)
        q = _layernorm(q, qln_g, qln_b)
        scale = E ** (-0.25)
        q = q * scale
        k = k * scale
        dot = jnp.einsum('bihd,bjhd->bhij', q, k)
        causal = jnp.triu(jnp.ones((T, T), dtype=bool), k=1)
        dot = jnp.where(causal, -jnp.inf, dot)
        att = jax.nn.softmax(dot, axis=-1)
        out = jnp.einsum('bhij,bjhd->bihd', att, v).reshape(B, T, E)
        return jnp.einsum('bte,fe->btf', out, Wo) + bo

    def _L2_xattn_ref(x, context, mask, Wq, Wkv, Wo, bo):
        import jax, jax.numpy as jnp
        import numpy as np
        B, N, M = (4, 128, 512)
        DQ, DC = (128, 128)
        H, DH = (16, 64)
        INNER = H * DH
        SCALE = DH ** (-0.5)
        q = x @ Wq
        kv = context @ Wkv
        k, v = jnp.split(kv, 2, axis=-1)

        def heads(t):
            b, s, _ = t.shape
            return t.reshape(b, s, H, DH).transpose(0, 2, 1, 3)
        q, k, v = (heads(q), heads(k), heads(v))
        sim = jnp.einsum('bhid,bhjd->bhij', q, k) * SCALE
        max_neg = -jnp.finfo(sim.dtype).max
        sim = jnp.where(mask[:, None, None, :], sim, max_neg)
        sim = jnp.clip(sim, -5.0, 5.0)
        attn = jax.nn.softmax(sim, axis=-1)
        out = jnp.einsum('bhij,bhjd->bhid', attn, v)
        out = out.transpose(0, 2, 1, 3).reshape(x.shape[0], x.shape[1], INNER)
        return out @ Wo + bo

    def _L2_ffn_ref(x, Wq, Wk, Wv, Wqa, Wqb, Wka, Wkb, Wg1a, Wg1b, bg1, Wg2a, Wg2b, bg2, We, Wga, Wgb, norm_w, Wo):
        import jax, jax.numpy as jnp
        import numpy as np
        from jax import lax
        H, DK, DV, N_EXP, CHUNK = (8, 64, 64, 4, 64)
        LORA, GATE_LR = (64, 16)
        NORMALIZER = 16.0
        EPS = 1e-05

        def chunk_gla(q, k, v, gk, C=CHUNK):
            L, h, dk = q.shape
            dv = v.shape[-1]
            nc = L // C
            qc, kc, vc, gc = (t.reshape(nc, C, h, -1) for t in (q, k, v, gk))
            g = jnp.cumsum(gc, axis=1)
            g_last = g[:, -1]
            qg = qc * jnp.exp(g)
            kg = kc * jnp.exp(-g)
            A = jnp.einsum('cthd,cshd->chts', qg, kg)
            A = A * jnp.tril(jnp.ones((C, C), q.dtype))
            o_intra = jnp.einsum('chts,cshe->cthe', A, vc)
            k_out = kc * jnp.exp(g_last[:, None] - g)
            chunk_kv = jnp.einsum('cthd,cthe->chde', k_out, vc)
            decay = jnp.exp(g_last)

            def step(S, inp):
                kv, dec, qg_c = inp
                o_inter = jnp.einsum('thd,hde->the', qg_c, S)
                return (S * dec[..., None] + kv, o_inter)
            S0 = jnp.zeros((h, dk, dv), q.dtype)
            _, o_inter = lax.scan(step, S0, (chunk_kv, decay, qg))
            return (o_intra + o_inter).reshape(L, h, dv)
        B, L, Dh = x.shape
        scale = DK ** (-0.5)
        q1 = (x @ Wq).reshape(B, L, H, DK) * scale
        k1 = (x @ Wk).reshape(B, L, H, DK)
        v = (x @ Wv).reshape(B, L, H, DV)
        q2 = (x @ Wqa @ Wqb).reshape(B, L, H, DK) * scale
        k2 = jax.nn.softmax((x @ Wka @ Wkb).reshape(B, L, H, DK), axis=-1)
        gk1 = (jax.nn.log_sigmoid(x @ Wg1a @ Wg1b + bg1) / NORMALIZER).reshape(B, L, H, DK)
        gk2 = (jax.nn.log_sigmoid(x @ Wg2a @ Wg2b + bg2) / NORMALIZER).reshape(B, L, H, DK)
        e = jax.nn.softmax(x @ We, axis=-1)
        _, idx = lax.top_k(e, 1)
        mask = jax.nn.one_hot(idx, N_EXP, dtype=x.dtype).sum(-2)
        rw = e * mask
        fac = jnp.swapaxes(rw, 1, 2)[:, :, :, None, None]
        mfac = jnp.swapaxes(mask, 1, 2)[:, :, :, None, None]
        q_e = q2[:, None] * fac
        k_e = k2[:, None] * fac
        gk_e = gk2[:, None] * mfac
        gla_b = jax.vmap(chunk_gla)
        o_dense = gla_b(q1, k1, v, gk1)
        gla_be = jax.vmap(jax.vmap(chunk_gla, in_axes=(0, 0, None, 0)))
        o_sparse = gla_be(q_e, k_e, v, gk_e).sum(axis=1)
        o = o_dense + o_sparse
        g = (x @ Wga @ Wgb).reshape(B, L, H, DV)
        o = o * lax.rsqrt(jnp.mean(o * o, axis=-1, keepdims=True) + EPS) * norm_w
        o = o * (g * jax.nn.sigmoid(g))
        return o.reshape(B, L, H * DV) @ Wo

    def _L3_attn_ref(inp, W_in, conv_w, conv_b, W_ssm, A_log, D_skip, dt_bias, W_out):
        import jax, jax.numpy as jnp
        import numpy as np
        D_MODEL = 128
        D_STATE = 64
        D_CONV = 4
        EXPAND = 2
        HEADDIM = 128
        BLOCK_LEN = 64
        D_INNER = EXPAND * D_MODEL
        NHEADS = D_INNER // HEADDIM

        def _segsum(a):
            T = a.shape[-1]
            cs = jnp.cumsum(a, axis=-1)
            seg = cs[..., :, None] - cs[..., None, :]
            mask = jnp.tril(jnp.ones((T, T), dtype=bool))
            return jnp.where(mask, seg, -jnp.inf)

        def _ssd_minimal(X, A, Bm, Cm, blk):
            b, l, h, p = X.shape
            c = l // blk
            X = X.reshape(b, c, blk, h, p)
            A = A.reshape(b, c, blk, h).transpose(0, 3, 1, 2)
            Bm = Bm.reshape(b, c, blk, h, -1)
            Cm = Cm.reshape(b, c, blk, h, -1)
            A_cs = jnp.cumsum(A, axis=-1)
            Lmat = jnp.exp(_segsum(A))
            Y_diag = jnp.einsum('bclhn,bcshn,bhcls,bcshp->bclhp', Cm, Bm, Lmat, X)
            decay_states = jnp.exp(A_cs[..., -1:] - A_cs)
            states = jnp.einsum('bclhn,bhcl,bclhp->bchpn', Bm, decay_states, X)
            init = jnp.zeros_like(states[:, :1])
            states = jnp.concatenate([init, states], axis=1)
            A_last = jnp.pad(A_cs[..., -1], ((0, 0), (0, 0), (1, 0)))
            decay_chunk = jnp.exp(_segsum(A_last))
            new_states = jnp.einsum('bhzc,bchpn->bzhpn', decay_chunk, states)
            states, final_state = (new_states[:, :-1], new_states[:, -1])
            out_decay = jnp.exp(A_cs)
            Y_off = jnp.einsum('bclhn,bchpn,bhcl->bclhp', Cm, states, out_decay)
            Y = (Y_diag + Y_off).reshape(b, l, h, p)
            return (Y, final_state)

        def _forward(inp, W_in, conv_w, conv_b, W_ssm, A_log, D_skip, dt_bias, W_out):
            B, L, _ = inp.shape
            H, P, N, k = (NHEADS, HEADDIM, D_STATE, D_CONV)
            xz = inp @ W_in.T
            x, z = jnp.split(xz, 2, axis=-1)
            xc = x.transpose(0, 2, 1)
            y_conv = jax.lax.conv_general_dilated(xc, conv_w, window_strides=(1,), padding=[(k - 1, 0)], dimension_numbers=('NCH', 'OIH', 'NCH'), feature_group_count=D_INNER)
            y_conv = y_conv + conv_b[None, :, None]
            conv_state = xc[..., -(k - 1):]
            x = y_conv.transpose(0, 2, 1)
            x = x * jax.nn.sigmoid(x)
            ssm_params = x @ W_ssm.T
            dt_raw = ssm_params[..., :H]
            B_raw = ssm_params[..., H:H + H * N]
            C_raw = ssm_params[..., H + H * N:]
            dt = jax.nn.softplus(dt_raw + dt_bias[None, None, :])
            B_mat = B_raw.reshape(B, L, H, N)
            C_mat = C_raw.reshape(B, L, H, N)
            X = x.reshape(B, L, H, P)
            A_cont = -jnp.exp(A_log)
            A_disc = dt * A_cont[None, None, :]
            X_disc = X * dt[..., None]
            Y_heads, ssm_state = _ssd_minimal(X_disc, A_disc, B_mat, C_mat, BLOCK_LEN)
            Y_heads = Y_heads + D_skip[None, None, :, None] * X
            y = Y_heads.reshape(B, L, D_INNER)
            y = y * jax.nn.sigmoid(z)
            out = y @ W_out.T
            return (out, conv_state, ssm_state)

        def _reference_tuple_inner(inp, W_in, conv_w, conv_b, W_ssm, A_log, D_skip, dt_bias, W_out):
            return _forward(inp, W_in, conv_w, conv_b, W_ssm, A_log, D_skip, dt_bias, W_out)
        return _reference_tuple_inner(inp, W_in, conv_w, conv_b, W_ssm, A_log, D_skip, dt_bias, W_out)[0]

    def _L3_xattn_ref(q, k, weight, kp_w, kp_b):
        import jax, jax.numpy as jnp
        import numpy as np
        B, N, D, K = (4, 512, 128, 128)
        n = q.shape[1]
        k_mod = k.mean(axis=1) @ kp_w.T + kp_b
        dynamic_weight = weight[None, :, :] * k_mod[:, :, None]
        q_f = jnp.fft.rfft(q, axis=1)
        w_f = jnp.fft.rfft(dynamic_weight, n=n, axis=2)
        y_f = q_f * jnp.transpose(w_f, (0, 2, 1))
        y = jnp.fft.irfft(y_f, n=n, axis=1)
        return y.astype(q.dtype)

    def _L3_ffn_ref(hidden_states, ln_w, ln_b, router_w, gate_w, up_w, down_w, sh_gate, sh_up, sh_down):
        import jax, jax.numpy as jnp
        import numpy as np
        H = 128
        I = 256
        E = 8
        B, S = (2, 512)
        EPS = 1e-05
        INIT = 0.02

        def _layernorm(x, w, b):
            mu = jnp.mean(x, axis=-1, keepdims=True)
            var = jnp.mean(jnp.square(x - mu), axis=-1, keepdims=True)
            return (x - mu) * jax.lax.rsqrt(var + EPS) * w + b
        b, s, h = hidden_states.shape
        normed = _layernorm(hidden_states, ln_w, ln_b)
        xf = normed.reshape(-1, h)
        logits = xf @ router_w
        top_idx = jnp.argmax(logits, axis=-1)
        top_score = jax.nn.sigmoid(jnp.max(logits, axis=-1))

        def body(acc, ew):
            g, u, d, e = ew
            w = jnp.where(top_idx == e, top_score, 0.0)[:, None]
            xe = xf * w
            hmid = jax.nn.silu(xe @ g) * (xe @ u)
            return (acc + hmid @ d, None)
        routed, _ = jax.lax.scan(body, jnp.zeros_like(xf), (gate_w, up_w, down_w, jnp.arange(E)))
        shared = jax.nn.silu(xf @ sh_gate) * (xf @ sh_up) @ sh_down
        moe_out = (routed + shared).reshape(b, s, h)
        return hidden_states + moe_out
    x = x + _L0_attn_ref(_layernorm(x, axis=-1), L0_attn_W_qkv, L0_attn_W_z, L0_attn_W_b, L0_attn_W_a, L0_attn_dt_bias, L0_attn_A_log, L0_attn_conv_w, L0_attn_norm_w, L0_attn_W_out)
    x = x + _L0_xattn_ref(_layernorm(x, axis=-1), ctx_1024, ctx_1024, L0_xattn_Wq, L0_xattn_bq, L0_xattn_Wk, L0_xattn_bk, L0_xattn_Wv, L0_xattn_bv, L0_xattn_Wo, L0_xattn_bo)
    x = x + _L0_ffn_ref(_layernorm(x, axis=-1), L0_ffn_gate_w, L0_ffn_gate_bias, L0_ffn_w1, L0_ffn_w2, L0_ffn_w3, L0_ffn_ws1, L0_ffn_ws2, L0_ffn_ws3)
    x = x + _L1_attn_ref(_layernorm(x, axis=-1), L1_attn_c_attn_w, L1_attn_c_attn_b, L1_attn_q2l_w, L1_attn_q2l_b, L1_attn_kv2l_w, L1_attn_kv2l_b, L1_attn_l2o_w, L1_attn_l2o_b, L1_attn_wqk_w, L1_attn_wqk_b, L1_attn_cproj_w, L1_attn_cproj_b)
    x = x + _L1_xattn_ref(_layernorm(x, axis=-1), ctx_1024, ctx_1024, L1_xattn_Wq, L1_xattn_bq, L1_xattn_Wk, L1_xattn_bk, L1_xattn_Wv, L1_xattn_bv, L1_xattn_Wo, L1_xattn_bo)
    x = x + _L1_ffn_ref(_layernorm(x, axis=-1), L1_ffn_router_DE, L1_ffn_w1_eDF, L1_ffn_w3_eDF, L1_ffn_w2_eFD, L1_ffn_ws1_DF, L1_ffn_ws3_DF, L1_ffn_ws2_FD)
    x = x + _L2_attn_ref(_layernorm(x, axis=-1), L2_attn_Wk, L2_attn_Wq, L2_attn_Wv, L2_attn_Wo, L2_attn_bo, L2_attn_kln_g, L2_attn_kln_b, L2_attn_qln_g, L2_attn_qln_b)
    x = x + _L2_xattn_ref(_layernorm(x, axis=-1), ctx_1024, mask_BxS2_bk1, L2_xattn_Wq, L2_xattn_Wkv, L2_xattn_Wo, L2_xattn_bo)
    x = x + _L2_ffn_ref(_layernorm(x, axis=-1), L2_ffn_Wq, L2_ffn_Wk, L2_ffn_Wv, L2_ffn_Wqa, L2_ffn_Wqb, L2_ffn_Wka, L2_ffn_Wkb, L2_ffn_Wg1a, L2_ffn_Wg1b, L2_ffn_bg1, L2_ffn_Wg2a, L2_ffn_Wg2b, L2_ffn_bg2, L2_ffn_We, L2_ffn_Wga, L2_ffn_Wgb, L2_ffn_norm_w, L2_ffn_Wo)
    x = x + _L3_attn_ref(_layernorm(x, axis=-1), L3_attn_W_in, L3_attn_conv_w, L3_attn_conv_b, L3_attn_W_ssm, L3_attn_A_log, L3_attn_D_skip, L3_attn_dt_bias, L3_attn_W_out)
    x = x + _L3_xattn_ref(_layernorm(x, axis=-1), ctx_1024, L3_xattn_weight, L3_xattn_kp_w, L3_xattn_kp_b)
    x = x + _L3_ffn_ref(_layernorm(x, axis=-1), L3_ffn_ln_w, L3_ffn_ln_b, L3_ffn_router_w, L3_ffn_gate_w, L3_ffn_up_w, L3_ffn_down_w, L3_ffn_sh_gate, L3_ffn_sh_up, L3_ffn_sh_down)
    return x

_drawn_inputs = setup_inputs


def setup_inputs(seed=0):
    import zlib

    import numpy as np

    out = dict(_drawn_inputs(seed))
    spreads = {'L0_attn_dt_bias': (1.0, 0.6),
     'L0_attn_norm_w': (1.0, 0.6),
     'L0_xattn_bq': (0.0, 0.464),
     'L0_xattn_bk': (0.0, 0.8),
     'L0_xattn_bv': (0.0, 0.1),
     'L0_xattn_bo': (0.0, 0.1),
     'L0_ffn_gate_bias': (0.0, 0.8),
     'L1_attn_c_attn_b': (0.0, 0.8),
     'L1_attn_q2l_b': (0.0, 0.8),
     'L1_attn_kv2l_b': (0.0, 0.8),
     'L1_attn_l2o_b': (0.0, 0.41),
     'L1_attn_wqk_b': (0.0, 0.8),
     'L1_attn_cproj_b': (0.0, 0.1),
     'L1_xattn_bq': (0.0, 0.528),
     'L1_xattn_bk': (0.0, 0.8),
     'L1_xattn_bv': (0.0, 0.1),
     'L1_xattn_bo': (0.0, 0.1),
     'L2_attn_bo': (0.0, 0.1),
     'L2_attn_kln_g': (1.0, 0.6),
     'L2_attn_kln_b': (0.0, 0.8),
     'L2_attn_qln_g': (1.0, 0.6),
     'L2_attn_qln_b': (0.0, 0.8),
     'L2_xattn_bo': (0.0, 0.1),
     'L2_ffn_bg1': (0.0, 0.8),
     'L2_ffn_bg2': (0.0, 0.8),
     'L2_ffn_norm_w': (1.0, 0.6),
     'L3_attn_D_skip': (1.0, 0.6),
     'L3_ffn_ln_w': (1.0, 0.6),
     'L3_ffn_ln_b': (0.0, 0.8)}
    factors = {'L0_attn_W_qkv': 3.537,
     'L0_attn_W_z': 3.573,
     'L0_attn_W_b': 8.0,
     'L0_attn_W_a': 8.0,
     'L0_attn_A_log': 8.0,
     'L0_attn_conv_w': 3.554,
     'L0_attn_W_out': 3.594,
     'L0_ffn_gate_w': 8.0,
     'L0_ffn_w1': 8.0,
     'L0_ffn_w2': 8.0,
     'L0_ffn_w3': 8.0,
     'L0_ffn_ws1': 8.0,
     'L0_ffn_ws2': 8.0,
     'L0_ffn_ws3': 8.0,
     'L1_attn_c_attn_w': 8.0,
     'L1_attn_q2l_w': 8.0,
     'L1_attn_kv2l_w': 8.0,
     'L1_attn_l2o_w': 8.0,
     'L1_attn_wqk_w': 8.0,
     'L1_attn_cproj_w': 2.763,
     'L1_ffn_router_DE': 8.0,
     'L1_ffn_w1_eDF': 8.0,
     'L1_ffn_w3_eDF': 8.0,
     'L1_ffn_w2_eFD': 8.0,
     'L1_ffn_ws1_DF': 8.0,
     'L1_ffn_ws3_DF': 8.0,
     'L1_ffn_ws2_FD': 8.0,
     'L2_attn_Wk': 3.323,
     'L2_attn_Wq': 3.369,
     'L2_ffn_Wq': 8.0,
     'L2_ffn_Wk': 8.0,
     'L2_ffn_Wv': 8.0,
     'L2_ffn_Wqa': 8.0,
     'L2_ffn_Wqb': 8.0,
     'L2_ffn_Wka': 8.0,
     'L2_ffn_Wkb': 8.0,
     'L2_ffn_Wg1a': 8.0,
     'L2_ffn_Wg1b': 8.0,
     'L2_ffn_Wg2a': 8.0,
     'L2_ffn_Wg2b': 8.0,
     'L2_ffn_We': 8.0,
     'L2_ffn_Wga': 8.0,
     'L2_ffn_Wgb': 8.0,
     'L2_ffn_Wo': 8.0,
     'L3_attn_W_ssm': 8.0,
     'L3_attn_A_log': 8.0,
     'L3_attn_dt_bias': 8.0,
     'L3_xattn_kp_b': 2.897,
     'L3_ffn_router_w': 8.0,
     'L3_ffn_gate_w': 8.0,
     'L3_ffn_up_w': 8.0,
     'L3_ffn_down_w': 8.0,
     'L3_ffn_sh_gate': 8.0,
     'L3_ffn_sh_up': 8.0,
     'L3_ffn_sh_down': 8.0}
    for name, (base, spread) in spreads.items():
        noise = np.random.default_rng([zlib.crc32(name.encode()), seed]).standard_normal(out[name].shape)
        drawn = base * np.exp(spread * noise) if base else spread * noise
        out[name] = jnp.asarray(drawn.astype(out[name].dtype))
    for name, factor in factors.items():
        out[name] = (out[name] * factor).astype(out[name].dtype)
    return out
```

```python
from contextlib import ExitStack

import numpy as np

import concourse.bass as bass
from concourse import mybir

F32 = mybir.dt.float32
I32 = mybir.dt.int32
BF16 = mybir.dt.bfloat16
U8 = mybir.dt.uint8
ALU = mybir.AluOpType
ACT = mybir.ActivationFunctionType
AX = mybir.AxisListType.X

P = 128
B, T, D = 4, 512, 128
NT = T // P
S2 = 77
OUT = 7
STAGES = list(range(12))


class Core:

    def __init__(self, nc, ctx):
        self.nc, self.ctx = nc, ctx
        self.pass_sems, self.half_sems = [], []
        self.half = ctx.enter_context(ExitStack())
        self.x = self.sb("residual", [P, NT, D])
        self.xn = self.sb("xn", [P, NT, D])
        self.xnT = self.sb("xnT", [P, T])
        self.ctxT = self.sb("ctxT", [P, S2])
        self.bound = self.sb("bound", [S2, 1])
        self.mod = self.sb("mod", [P, 1])
        self.ident_bf = self.sb("ident_bf", [P, P], BF16)
        self.later_bf = self.sb("later_bf", [P, P], BF16)
        self.psum = ctx.enter_context(nc.psum_tensor("psum", [P, 8, 512], F32))

    def sb(self, name, shape, dt=F32):
        return self.ctx.enter_context(self.nc.sbuf_tensor(name, shape, dt))

    def pass_sem(self, name):
        s = self.ctx.enter_context(self.nc.semaphore(name))
        self.pass_sems.append(s.num)
        return s

    def sem(self, name):
        s = self.half.enter_context(self.nc.semaphore(name))
        self.half_sems.append(s.num)
        return s

    def clear(self, sync, nums):
        nums = sorted(nums)
        start = 0
        for i in range(1, len(nums) + 1):
            if i == len(nums) or nums[i] != nums[i - 1] + 1:
                sync.sem_clear(range(nums[start], nums[i - 1] + 1))
                start = i

    def end_half(self, sync):
        self.clear(sync, self.half_sems)
        self.half_sems = []
        self.half.close()

    def bank(self, n):
        return self.psum[:, n, :]


class Chain:

    def __init__(self, engine, sem, count=0):
        self.engine, self.sem, self.count = engine, sem, count

    def link(self, ins):
        self.count += 1
        ins.then_inc(self.sem, 1)
        self.engine.wait_ge(self.sem, self.count)


def newton_rsqrt(dve, chain, v, y, t):
    chain.link(dve.tensor_scalar(y.bitcast(I32), v.bitcast(I32), 1, None, ALU.arith_shift_right))
    chain.link(dve.tensor_scalar(y.bitcast(I32), y.bitcast(I32), -1, 0x5F3759DF, ALU.mult, ALU.add))
    for last in (False, False, True):
        chain.link(dve.scalar_tensor_tensor(out=t, in0=y, scalar=-0.5, in1=y, op0=ALU.mult, op1=ALU.mult))
        chain.link(dve.tensor_tensor(t, t, v, ALU.mult))
        chain.link(dve.scalar_tensor_tensor(out=t if last else y, in0=t, scalar=0.5 if last else 1.5, in1=y,
                                            op0=ALU.add, op1=ALU.mult))
    chain.link(dve.tensor_tensor(y, y, t, ALU.add))


class Norm:

    def __init__(self, m):
        self.m = m
        nc, ctx = m.nc, m.ctx
        self.stats = m.sb("norm_stats", [P, NT, 6])
        self.mv = m.sb("norm_mean_var", [P, NT, 2])
        self.var = m.sb("norm_var", [P, NT])
        self.rstd = m.sb("norm_rstd", [P, NT])
        self.tmp = m.sb("norm_tmp", [P, NT])
        self.subT = m.sb("norm_subT", [P, T])
        sem = m.pass_sem
        self.chain = sem("norm_chain")
        self.sub_copied = sem("norm_sub_copied")
        self.sub_turned = sem("norm_sub_turned")
        self.xn_ready = sem("norm_xn_ready")
        self.xn_turned = sem("norm_xn_turned")
        self.uses, self.adds, self.links = 0, 0, 0

    def statistics(self, dve, chain, src, eps):
        for t in range(NT):
            ins = dve.bn_stats(self.stats[:, t, :], src[:, t, :])
        chain.link(ins)
        for t in range(NT):
            ins = dve.bn_aggr(self.mv[:, t, :], self.stats[:, t, :])
        chain.link(ins)
        chain.link(dve.tensor_scalar(self.var[:, :], self.mv[:, :, 1], eps, None, ALU.add))
        newton_rsqrt(dve, chain, self.var[:, :], self.rstd[:, :], self.tmp[:, :])

    def block(self, add, bias=None, keep=False, norm=True, scale=None, shift=None, src=None, eps=1e-5):
        m, nc, u, a = self.m, self.m.nc, self.uses, self.adds
        src = m.x if src is None else src
        scaled = isinstance(bias, tuple)
        with nc.Block(no_gpsimd_drain=True) as block:
            @block.scalar
            def _(act):
                if add:
                    act.activation(self.subT[:, :], m.bank(OUT), ACT.Identity,
                                   scale=bias[1] if scaled else 1.0,
                                   bias=0.0 if bias is None or scaled else bias).then_inc(self.sub_copied, 1)
                if norm:
                    act.wait_ge(self.xn_turned, u + 1)
                    act.activation(m.xnT[:, :], m.bank(1), ACT.Identity,
                                   scale=1.0 if scale is None else scale,
                                   bias=0.0 if shift is None else shift)

            @block.tensor
            def _(pe):
                if add:
                    pe.wait_ge(self.sub_copied, a + 1)
                    for t in range(NT):
                        ins = pe.transpose(m.psum[:, 0, t * P:(t + 1) * P],
                                           self.subT[:, t * P:(t + 1) * P], m.ident)
                    ins.then_inc(self.sub_turned, 1)
                if norm:
                    pe.wait_ge(self.xn_ready, u + 1)
                    for t in range(NT):
                        ins = pe.transpose(m.psum[:, 1, t * P:(t + 1) * P], m.xn[:, t, :], m.ident)
                    ins.then_inc(self.xn_turned, 1)

            @block.vector
            def _(dve):
                chain = Chain(dve, self.chain, self.links)
                if keep:
                    chain.link(dve.tensor_tensor(m.x[:, :, :], m.x[:, :, :], m.xn[:, :, :], ALU.add))
                if add:
                    dve.wait_ge(self.sub_turned, a + 1)
                    chain.link(dve.tensor_tensor(
                        m.x[:, :, :], m.x[:, :, :],
                        m.bank(0).rearrange("p (t d) -> p t d", d=D), ALU.add))
                if norm:
                    self.statistics(dve, chain, src, eps)
                    for t in range(NT):
                        ins = dve.tensor_scalar(m.xn[:, t, :], src[:, t, :], self.mv[:, t, 0:1],
                                                self.rstd[:, t:t + 1], ALU.subtract, ALU.mult)
                    ins.then_inc(self.xn_ready, 1)
                self.links = chain.count
        self.uses += bool(norm)
        self.adds += bool(add)


def rank_experts(dve, chain, score, cmp, cmp2, lower, rank, E):
    shape = [P, NT, E, E]
    of_j = score.unsqueeze(2).to_broadcast(shape)
    of_e = score.unsqueeze(3).to_broadcast(shape)
    chain.link(dve.tensor_tensor(cmp, of_j, of_e, ALU.is_ge))
    chain.link(dve.tensor_tensor(cmp, cmp, lower.unsqueeze(1).to_broadcast(shape), ALU.mult))
    chain.link(dve.tensor_tensor(cmp2, of_j, of_e, ALU.is_gt))
    chain.link(dve.tensor_tensor(cmp, cmp, cmp2, ALU.max))
    chain.link(dve.tensor_reduce(rank, cmp, AX, ALU.add))


def experts_stage(m, name, w, E, inter, route, weigh_output):
    nc = m.nc
    if weigh_output:
        per = P // inter
        tiles = [(None, E * inter, inter)] + [(g, g * P, P) for g in range(E // per)]
    else:
        cuts = [(c, min(P, inter - c)) for c in range(0, inter, P)]
        tiles = [(None, E * inter + c, r) for c, r in cuts]
        tiles += [(e, e * inter + c, r) for e in range(E) for c, r in cuts]
    groups = 1 + max(g for g, _, _ in tiles if g is not None)
    first = {g: min(n for n, t in enumerate(tiles) if t[0] == g) for g in range(groups)}
    last = {g: max(n for n, t in enumerate(tiles) if t[0] == g) for g in range(groups)}
    N = len(tiles)
    with ExitStack() as ctx:
        sb = lambda n, shape, dt=F32: ctx.enter_context(nc.sbuf_tensor(f"{name}_{n}", shape, dt))
        sem = lambda n: m.sem(f"{name}_{n}")
        silu = sb("silu", [P, 2, T])
        prod = sb("prod", [P, 2, T])
        hidden = sb("hidden", [P, 2, T])
        gated = sb("gated_x", [P, 2, T])
        gate = sb("gate", [P, NT, E])
        gateT = sb("gateT", [E, T])
        work = sb("work", [P, 8, NT, E])
        cmp = sb("cmp", [P, 2, NT, E, E])
        chain_sem = sem("chain")
        logits_ready = sem("logits")
        sig_ready = sem("sig")
        gate_ready = sem("gate")
        gate_turned = sem("gate_turned")
        gateT_ready = sem("gateT")
        spread_ready = sem("spread")
        gated_ready = sem("gated")
        up_ready = sem("up")
        silu_ready = sem("silu")
        hidden_ready = sem("hidden")
        down_done = sem("down")

        with nc.Block(no_gpsimd_drain=True) as block:
            @block.tensor
            def _(pe):
                for t in range(NT):
                    ins = pe.matmul(m.psum[:, 6, t * E:(t + 1) * E], m.xnT[:, t * P:(t + 1) * P],
                                    w["router"], start=True, stop=True)
                ins.then_inc(logits_ready, 1)

                def spread(g):
                    if g == 0:
                        pe.wait_ge(gate_ready, 1)
                        for t in range(NT):
                            ins = pe.transpose(m.psum[0:E, 6, t * P:(t + 1) * P], gate[:, t, :], m.ident)
                        ins.then_inc(gate_turned, 1)
                        pe.wait_ge(gateT_ready, 1)
                    if g >= 2:
                        if weigh_output:
                            pe.wait_ge(hidden_ready, first[g - 2] + 1)
                        else:
                            pe.wait_ge(gated_ready, g - 1)
                    pe.matmul(m.bank(4 + g % 2), w["spread"][:, g, :], gateT[:, :],
                              start=True, stop=True).then_inc(spread_ready, 1)

                def up(n):
                    g, c, r = tiles[n]
                    rhs = m.xnT[:, :]
                    if g is not None and not weigh_output:
                        pe.wait_ge(gated_ready, g + 1)
                        rhs = gated[:, g % 2, :]
                    if n >= 2:
                        pe.wait_ge(hidden_ready, n - 1)
                    pe.matmul(m.bank(n % 2)[0:r], w["up"][:, c:c + r], rhs, start=True, stop=True)
                    pe.matmul(m.bank(2 + n % 2)[0:r], w["gate"][:, c:c + r], rhs,
                              start=True, stop=True).then_inc(up_ready, 1)

                def down(n):
                    r = tiles[n][2]
                    pe.wait_ge(hidden_ready, n + 1)
                    pe.matmul(m.bank(OUT), w["down"][0:r, n, :], hidden[0:r, n % 2, :],
                              start=n == 0, stop=n == N - 1).then_inc(down_done, 1)

                for n in range(N + 1):
                    if n < N:
                        g = tiles[n][0]
                        if weigh_output:
                            if n >= 1:
                                spread(g)
                        elif n == first[0]:
                            spread(0)
                            spread(1)
                        elif g is not None and n == first[g] and g + 1 < groups:
                            spread(g + 1)
                        up(n)
                    if n >= 1:
                        down(n - 1)

            @block.scalar
            def _(act):
                def silu_of(n):
                    r = tiles[n][2]
                    act.wait_ge(up_ready, n + 1)
                    if n >= 2:
                        act.wait_ge(hidden_ready, n - 1)
                    act.activation(silu[0:r, n % 2, :], m.bank(n % 2)[0:r], ACT.Silu).then_inc(silu_ready, 1)

                act.wait_ge(logits_ready, 1)
                act.activation(work[:, 0, :, :], m.psum[:, 6, 0:NT * E].rearrange("p (t e) -> p t e", e=E),
                               ACT.Sigmoid).then_inc(sig_ready, 1)
                for n in range(N):
                    if n == first[0]:
                        act.wait_ge(gate_turned, 1)
                        act.activation(gateT[:, :], m.psum[0:E, 6, :], ACT.Copy).then_inc(gateT_ready, 1)
                    silu_of(n)

            @block.vector
            def _(dve):
                chain = Chain(dve, chain_sem)
                dve.wait_ge(sig_ready, 1)
                route(dve, chain, m.psum[:, 6, 0:NT * E].rearrange("p (t e) -> p t e", e=E),
                      work, cmp, gate, gate_ready)

                def weigh_input(g):
                    dve.wait_ge(spread_ready, g + 1)
                    if g >= 2:
                        dve.wait_ge(up_ready, last[g - 2] + 1)
                    dve.tensor_tensor(gated[:, g % 2, :], m.xnT[:, :], m.bank(4 + g % 2),
                                      ALU.mult).then_inc(gated_ready, 1)

                for n in range(N):
                    g, _, r = tiles[n]
                    if not weigh_output:
                        if n == first[0]:
                            weigh_input(0)
                            weigh_input(1)
                        elif g is not None and n == first[g] and g + 1 < groups:
                            weigh_input(g + 1)
                    dve.wait_ge(silu_ready, n + 1)
                    if n >= 2:
                        dve.wait_ge(down_done, n - 1)
                    if weigh_output and g is not None:
                        chain.link(dve.tensor_tensor(prod[0:r, n % 2, :], silu[0:r, n % 2, :],
                                                     m.bank(2 + n % 2)[0:r], ALU.mult))
                        dve.wait_ge(spread_ready, g + 1)
                        dve.tensor_tensor(hidden[0:r, n % 2, :], prod[0:r, n % 2, :],
                                          m.bank(4 + g % 2), ALU.mult).then_inc(hidden_ready, 1)
                    else:
                        dve.tensor_tensor(hidden[0:r, n % 2, :], silu[0:r, n % 2, :],
                                          m.bank(2 + n % 2)[0:r], ALU.mult).then_inc(hidden_ready, 1)


def route_grouped(m, lower16, lower4, bias):
    E, G = 16, 4

    def route(dve, chain, logits, work, cmp, gate, gate_ready):
        score = work[:, 0, :, :]
        biased, group, keep, rank = (work[:, i, :, :] for i in (1, 2, 3, 4))
        chain.link(dve.tensor_tensor(biased, score, bias.unsqueeze(1).to_broadcast([P, NT, E]), ALU.add))
        chain.link(dve.tensor_reduce(group[:, :, 0:G], biased.rearrange("p t (g e) -> p t g e", g=G), AX, ALU.max))
        rank_experts(dve, chain, group[:, :, 0:G], cmp[:, 0, :, 0:G, 0:G], cmp[:, 1, :, 0:G, 0:G],
                     lower4, rank[:, :, 0:G], G)
        chain.link(dve.tensor_scalar(keep[:, :, 0:G], rank[:, :, 0:G], 2.0, None, ALU.is_lt))
        kept = keep[:, :, 0:G].unsqueeze(3).to_broadcast([P, NT, G, E // G])
        grouped = lambda a: a.rearrange("p t (g e) -> p t g e", g=G)
        chain.link(dve.tensor_tensor(grouped(biased), grouped(biased), kept, ALU.mult))
        chain.link(dve.tensor_scalar(group[:, :, 0:G], keep[:, :, 0:G], 1e30, -1e30, ALU.mult, ALU.add))
        chain.link(dve.tensor_tensor(grouped(biased), grouped(biased),
                                     group[:, :, 0:G].unsqueeze(3).to_broadcast([P, NT, G, E // G]), ALU.add))
        rank_experts(dve, chain, biased, cmp[:, 0], cmp[:, 1], lower16, rank, E)
        chain.link(dve.tensor_scalar(rank, rank, 4.0, None, ALU.is_lt))
        dve.tensor_tensor(gate[:, :, :], rank, score, ALU.mult).then_inc(gate_ready, 1)
    return route


def route_top1(m, lower):
    E = 8

    def route(dve, chain, logits, work, cmp, gate, gate_ready):
        score, raw, rank = (work[:, i, :, :] for i in (0, 1, 2))
        chain.link(dve.tensor_copy(raw, logits))
        rank_experts(dve, chain, raw, cmp[:, 0], cmp[:, 1], lower, rank, E)
        chain.link(dve.tensor_scalar(rank, rank, 1.0, None, ALU.is_lt))
        dve.tensor_tensor(gate[:, :, :], rank, score, ALU.mult).then_inc(gate_ready, 1)
    return route


H = 16
HD = D // H


def cross_attention_stage(m, name, w):
    nc = m.nc
    cut = [(0, 6), (6, 12), (12, 16)]
    with ExitStack() as ctx:
        sb = lambda n, shape, dt=F32: ctx.enter_context(nc.sbuf_tensor(f"{name}_{n}", shape, dt))
        sem = lambda n: m.sem(f"{name}_{n}")
        qT = sb("qT", [P, T])
        kT = sb("kT", [P, S2])
        k_heads = sb("k_heads", [P, H, S2])
        v = sb("v", [S2, H, 32])
        prob = sb("prob", [P, NT, H, S2])
        peak = sb("peak", [P, NT, H])
        total = sb("total", [P, NT, H])
        turned = sb("turned", [S2, 3, T])
        mixed = sb("mixed", [P, T])
        qkv_ready = sem("qkv")
        q_ready = sem("q")
        k_ready = sem("k")
        k_heads_ready = sem("k_heads")
        scores_ready = sem("scores")
        shifted = sem("shifted")
        exps_ready = sem("exps")
        probs_ready = sem("probs")
        head_turned = sem("turned")
        copied_dve = sem("copied_dve")
        copied_act = sem("copied_act")
        mixed_psum = sem("mixed_psum")
        mixed_ready = sem("mixed")
        chain_sem = sem("chain")

        with nc.Block(no_gpsimd_drain=True) as block:
            @block.tensor
            def _(pe):
                pe.matmul(m.bank(0), w["wq"], m.xnT[:, :], start=True, stop=True)
                pe.matmul(m.psum[:, 1, 0:S2], w["wk"], m.ctxT[:, :], start=True, stop=True)
                pe.matmul(m.psum[0:S2, 2, 0:D], m.ctxT[:, :], w["wv"], start=True,
                          stop=True).then_inc(qkv_ready, 1)
                pe.wait_ge(q_ready, 1)
                pe.wait_ge(k_heads_ready, 1)
                for t in range(NT):
                    base = 3 * (t % 2)
                    if t >= 2:
                        pe.wait_ge(shifted, t - 1)
                    for n, (a, b) in enumerate(cut):
                        ins = pe.matmul(m.psum[:, base + n, 0:(b - a) * S2], qT[:, t * P:(t + 1) * P],
                                        k_heads[:, a:b, :].rearrange("p h s -> p (h s)"),
                                        start=True, stop=True)
                    ins.then_inc(scores_ready, 1)
                pe.wait_ge(probs_ready, NT)
                for h in range(H + 2):
                    if h < H:
                        if h >= 2:
                            pe.wait_ge(copied_dve if h % 2 == 0 else copied_act, h // 2)
                        for t in range(NT):
                            ins = pe.transpose(m.psum[0:S2, h % 2, t * P:(t + 1) * P],
                                               prob[:, t, h, :], m.ident)
                        ins.then_inc(head_turned, 1)
                    if h >= 2:
                        g = h - 2
                        pe.wait_ge(copied_dve if g % 2 == 0 else copied_act, g // 2 + 1)
                        rows = 32 * (g // 4)
                        pe.matmul(m.psum[rows:rows + 32, 6, :], v[:, g, :], turned[:, g % 3, :],
                                  start=g % 4 == 0, stop=g % 4 == 3).then_inc(mixed_psum, 1)
                pe.wait_ge(mixed_ready, 1)
                pe.matmul(m.bank(OUT), w["wo"], mixed[:, :], start=True, stop=True)

            @block.scalar
            def _(act):
                act.wait_ge(qkv_ready, 1)
                act.activation(kT[:, :], m.psum[:, 1, 0:S2], ACT.Identity, bias=w["bk"]).then_inc(k_ready, 1)
                act.activation(qT[:, :], m.bank(0), ACT.Identity, bias=w["bq"]).then_inc(q_ready, 1)
                for t in range(NT):
                    act.wait_ge(shifted, t + 1)
                    act.activation(prob[:, t, :, :], prob[:, t, :, :], ACT.Exp,
                                   scale=float(HD) ** -0.5).then_inc(exps_ready, 1)
                for h in range(1, H, 2):
                    act.wait_ge(head_turned, h + 1)
                    if h >= 3:
                        act.wait_ge(mixed_psum, h - 2)
                    act.activation(turned[:, h % 3, :], m.psum[0:S2, h % 2, :], ACT.Copy).then_inc(copied_act, 1)
                act.wait_ge(mixed_psum, H)
                act.activation(mixed[:, :], m.bank(6), ACT.Copy).then_inc(mixed_ready, 1)

            @block.vector
            def _(dve):
                chain = Chain(dve, chain_sem)
                def normalise_tile(dve, chain, t):
                    dve.wait_ge(exps_ready, t + 1)
                    chain.link(dve.tensor_reduce(total[:, t, :], prob[:, t, :, :], AX, ALU.add))
                    chain.link(dve.reciprocal(total[:, t, :], total[:, t, :]))
                    dve.tensor_tensor(prob[:, t, :, :], prob[:, t, :, :],
                                      total[:, t, :].unsqueeze(2).to_broadcast([P, H, S2]),
                                      ALU.mult).then_inc(probs_ready, 1)

                chain.link(dve.memset(v[:, :, :], 0.0))
                dve.wait_ge(k_ready, 1)
                dve.tensor_tensor(k_heads[:, :, :], kT[:, :].unsqueeze(1).to_broadcast([P, H, S2]),
                                  m.const["head_rows"].unsqueeze(2).to_broadcast([P, H, S2]), ALU.mult)
                for r in range(4):
                    ins = dve.tensor_tensor(
                        v[:, r:H:4, 8 * r:8 * r + 8],
                        m.psum[0:S2, 2, 0:D].rearrange("p (q r d) -> p q r d", r=4, d=HD)[:, :, r, :],
                        w["bv"].rearrange("p (q r d) -> p q r d", r=4, d=HD)[:, :, r, :], ALU.add)
                ins.then_inc(k_heads_ready, 1)
                for t in range(NT):
                    dve.wait_ge(scores_ready, t + 1)
                    base = 3 * (t % 2)
                    part = lambda n: m.psum[:, base + n, 0:(cut[n][1] - cut[n][0]) * S2].rearrange(
                        "p (h s) -> p h s", s=S2)
                    for n, (a, b) in enumerate(cut):
                        ins = dve.tensor_reduce(peak[:, t, a:b], part(n), AX, ALU.max)
                    chain.link(ins)
                    for n, (a, b) in enumerate(cut):
                        ins = dve.tensor_tensor(prob[:, t, a:b, :], part(n),
                                                peak[:, t, a:b].unsqueeze(2).to_broadcast([P, b - a, S2]),
                                                ALU.subtract)
                    ins.then_inc(shifted, 1)
                    if t >= 1:
                        normalise_tile(dve, chain, t - 1)
                normalise_tile(dve, chain, NT - 1)
                for h in range(0, H, 2):
                    dve.wait_ge(head_turned, h + 1)
                    if h >= 3:
                        dve.wait_ge(mixed_psum, h - 2)
                    dve.tensor_copy(turned[:, h % 3, :], m.psum[0:S2, h % 2, :]).then_inc(copied_dve, 1)

    return w["bo"]


def stage_l0_xattn(m):
    return cross_attention_stage(m, "l0_xattn", m.weights("l0_xattn"))


def stage_l1_xattn(m):
    return cross_attention_stage(m, "l1_xattn", m.weights("l1_xattn"))


def causal_attention(m, name, q_of, k_of, rows_of, v, bank_of, groups, scale, mixed):
    nc = m.nc
    U = H * NT
    TURN, COPY, MIX = 6, 6, 8
    with ExitStack() as ctx:
        sb = lambda n, shape, dt=F32: ctx.enter_context(nc.sbuf_tensor(f"{name}_{n}", shape, dt))
        sem = lambda n: m.sem(f"{name}_{n}")
        k_head = sb("k_head", [P, 2, T])
        prob = sb("prob", [P, 2, NT, T])
        turned = sb("turned", [P, NT, T])
        peak = sb("peak", [P, U])
        total = sb("total", [P, U])
        k_ready = sem("k_ready")
        scores_ready = sem("scores")
        peak_ready = sem("peak")
        exps_ready = sem("exps")
        probs_ready = sem("probs")
        step_turned = sem("turned")
        copied = sem("copied")
        step_mixed = sem("mixed")
        group_copied = sem("group")
        chain_sem = sem("chain")
        last_of = {g: max(h for h in range(H) if bank_of(h)[0] == g) for g in range(groups)}
        bank_of_step = lambda u: (0, 1, 2, OUT)[u % 4]

        with nc.Block(no_gpsimd_drain=True) as block:
            @block.gpsimd
            def _(pool):
                for h in range(H):
                    if h >= 2:
                        pool.wait_ge(scores_ready, NT * (h - 1))
                    pool.tensor_scalar(k_head[:, h % 2, :], k_of(h), rows_of(h), scale,
                                       ALU.mult, ALU.mult).then_inc(k_ready, 1)

            @block.tensor
            def _(pe):
                def score(u):
                    h, i = divmod(u, NT)
                    pe.wait_ge(k_ready, h + 1)
                    if u >= 4:
                        pe.wait_ge(exps_ready, u - 3)
                    pe.matmul(m.psum[:, bank_of_step(u), 0:(i + 1) * P], q_of(h)[:, i * P:(i + 1) * P],
                              k_head[:, h % 2, 0:(i + 1) * P], start=True, stop=False)
                    pe.matmul(m.psum[:, bank_of_step(u), i * P:(i + 1) * P], m.ident_bf[:, :], m.later_bf[:, :],
                              start=False, stop=True).then_inc(scores_ready, 1)

                def turn(v_):
                    h, j = divmod(v_, NT)
                    pe.wait_ge(probs_ready, h + 1)
                    if v_ >= 2:
                        pe.wait_ge(copied, v_ - 1)
                    for i in range(j, NT):
                        ins = pe.transpose(m.psum[:, 3 + v_ % 2, (i - j) * P:(i - j + 1) * P],
                                           prob[:, h % 2, i, j * P:(j + 1) * P], m.ident)
                    ins.then_inc(step_turned, 1)

                def mix(v_):
                    h, j = divmod(v_, NT)
                    pe.wait_ge(copied, v_ + 1)
                    g, quad = bank_of(h)
                    if j == 0 and g >= 2 and quad == 0:
                        pe.wait_ge(group_copied, g - 1)
                    first = j == 0 and (h == 0 or bank_of(h - 1) != bank_of(h))
                    last = j == NT - 1 and (h == H - 1 or bank_of(h + 1) != bank_of(h))
                    pe.matmul(m.psum[32 * quad:32 * quad + 32, 5 + g % 2, j * P:T], v[:, j, h, :],
                              turned[:, j, 0:T - j * P], start=first, stop=last).then_inc(step_mixed, 1)

                for u in range(U + MIX):
                    if u < U:
                        score(u)
                    if 0 <= u - TURN < U:
                        turn(u - TURN)
                    if 0 <= u - MIX < U:
                        mix(u - MIX)

            @block.scalar
            def _(act):
                for u in range(U + MIX + 1):
                    v_ = u - COPY
                    if 0 <= v_ < U:
                        act.wait_ge(step_turned, v_ + 1)
                        if v_ >= NT:
                            act.wait_ge(step_mixed, v_ - NT + 1)
                        n = T - (v_ % NT) * P
                        act.activation(turned[:, v_ % NT, 0:n], m.psum[:, 3 + v_ % 2, 0:n],
                                       ACT.Copy).then_inc(copied, 1)
                    if u < U:
                        h, i = divmod(u, NT)
                        act.wait_ge(peak_ready, u + 1)
                        if h >= 2:
                            act.wait_ge(step_turned, NT * (h - 1))
                        act.activation(prob[:, h % 2, i, 0:(i + 1) * P], m.psum[:, bank_of_step(u), 0:(i + 1) * P],
                                       ACT.Exp, bias=peak[:, u:u + 1],
                                       accum_out=total[:, u:u + 1]).then_inc(exps_ready, 1)
                    v_ = u - MIX - 1
                    if v_ >= 0 and v_ % NT == NT - 1 and v_ // NT in last_of.values():
                        g = bank_of(v_ // NT)[0]
                        act.wait_ge(step_mixed, v_ + 1)
                        act.activation(mixed[:, g, :], m.bank(5 + g % 2), ACT.Copy).then_inc(group_copied, 1)

            @block.vector
            def _(dve):
                chain = Chain(dve, chain_sem)
                for u in range(U + 1):
                    if u < U:
                        i = u % NT
                        dve.wait_ge(scores_ready, u + 1)
                        dve.tensor_reduce(peak[:, u:u + 1], m.psum[:, bank_of_step(u), 0:(i + 1) * P], AX, ALU.max,
                                          negate=True).then_inc(peak_ready, 1)
                    if u >= NT and u % NT == 0 and u // NT <= H:
                        h = u // NT - 1
                        dve.wait_ge(exps_ready, NT * (h + 1))
                        part = total[:, NT * h:NT * (h + 1)]
                        chain.link(dve.reciprocal(part, part))
                        for i in range(NT):
                            p = prob[:, h % 2, i, 0:(i + 1) * P]
                            ins = dve.tensor_scalar(p, p, total[:, NT * h + i:NT * h + i + 1], None, ALU.mult)
                        ins.then_inc(probs_ready, 1)


def stage_l1_attn(m):
    nc, w = m.nc, m.weights("l1_attn")
    G, name = 4, "l1_attn"
    with ExitStack() as ctx:
        sb = lambda n, shape, dt=F32: ctx.enter_context(nc.sbuf_tensor(f"{name}_{n}", shape, dt))
        sem = lambda n: m.sem(f"{name}_{n}")
        q = sb("q", [P, G, T])
        k = sb("k", [P, G, T])
        v = sb("v", [P, NT, H, 32])
        mixed = sb("mixed", [P, G, T])
        pre = ExitStack()
        psb = lambda n, shape, dt=F32: pre.enter_context(nc.sbuf_tensor(f"{name}_{n}", shape, dt))
        qkv = psb("qkv", [P, 3, T])
        latent = psb("latent", [P, 2, T])
        turned = psb("rotated", [P, 2, T])
        qkv_psum = sem("qkv_psum")
        qkv_ready = sem("qkv_ready")
        lat_psum = sem("lat_psum")
        lat_ready = sem("lat_ready")
        rot_psum = sem("rot_psum")
        rot_ready = sem("rot_ready")
        wqk_psum = sem("wqk_psum")
        wqk_read = sem("wqk_read")
        v_psum = sem("v_psum")
        v_read = sem("v_read")
        chain_sem = sem("pre_chain")
        with nc.Block(no_gpsimd_drain=True) as block:
            @block.tensor
            def _(pe):
                for n in range(3):
                    pe.matmul(m.bank(n), w["qkv"][:, n, :], m.xnT[:, :], start=True,
                              stop=True).then_inc(qkv_psum, 1)
                for n in range(2 * G + 2):
                    if n < 2 * G:
                        pe.wait_ge(qkv_ready, n // G + 1)
                        if n >= 2:
                            pe.wait_ge(lat_ready, n - 1)
                        pe.matmul(m.bank(3 + n % 2), w["q2l" if n < G else "kv2l"][:, n % G, :],
                                  qkv[:, n // G, :], start=True, stop=True).then_inc(lat_psum, 1)
                    if 1 <= n <= 2 * G:
                        pe.wait_ge(lat_ready, n)
                        if n >= 2:
                            pe.wait_ge(rot_ready, n - 1)
                        pe.matmul(m.bank(5), m.const["rotate"], latent[:, (n - 1) % 2, :], start=True,
                                  stop=True).then_inc(rot_psum, 1)
                    if 2 <= n < G + 2:
                        pe.wait_ge(rot_ready, n - 1)
                        if n >= 3:
                            pe.wait_ge(wqk_read, n - 2)
                        pe.matmul(m.bank(6), w["wqk"], turned[:, (n - 2) % 2, :], start=True,
                                  stop=True).then_inc(wqk_psum, 1)
                pe.wait_ge(qkv_ready, 3)
                for t in range(NT):
                    if t >= 2:
                        pe.wait_ge(v_read, t - 1)
                    pe.matmul(m.bank(t % 2), qkv[:, 2, t * P:(t + 1) * P],
                              w["kv2l"].rearrange("p g c -> p (g c)"), start=True,
                              stop=True).then_inc(v_psum, 1)

            @block.scalar
            def _(act):
                for n in range(3):
                    act.wait_ge(qkv_psum, n + 1)
                    act.activation(qkv[:, n, :], m.bank(n), ACT.Identity,
                                   bias=w["qkv_b"][:, n:n + 1]).then_inc(qkv_ready, 1)
                for n in range(2 * G):
                    act.wait_ge(lat_psum, n + 1)
                    if n >= 2:
                        act.wait_ge(rot_ready, n - 1)
                    act.activation(latent[:, n % 2, :], m.bank(3 + n % 2), ACT.Identity,
                                   bias=w["q2l_b" if n < G else "kv2l_b"]).then_inc(lat_ready, 1)

            @block.vector
            def _(dve):
                chain = Chain(dve, chain_sem)
                for n in range(2 * G + 1):
                    if n < 2 * G:
                        dve.wait_ge(lat_ready, n + 1)
                        dve.wait_ge(rot_psum, n + 1)
                        if 2 <= n < G:
                            dve.wait_ge(wqk_psum, n - 1)
                        out = turned[:, n % 2, :] if n < G else k[:, n - G, :]
                        chain.link(dve.tensor_tensor(out, m.bank(5), m.const["sin"], ALU.mult))
                        if n >= G:
                            tmp = mixed[:, n - G, :]
                        else:
                            tmp = q[:, n, :]
                        chain.link(dve.tensor_tensor(tmp, latent[:, n % 2, :], m.const["cos"], ALU.mult))
                        dve.tensor_tensor(out, out, tmp, ALU.add).then_inc(rot_ready, 1)
                    if 1 <= n <= G:
                        dve.wait_ge(rot_ready, n)
                        dve.wait_ge(wqk_psum, n)
                        dve.tensor_scalar(q[:, n - 1, :], m.bank(6), w["wqk_b"], None,
                                          ALU.add).then_inc(wqk_read, 1)
                for t in range(NT):
                    dve.wait_ge(v_psum, t + 1)
                    dve.tensor_tensor(v[:, t, :, :], m.bank(t % 2).rearrange("p (h l) -> p h l", l=32),
                                      w["v_b"].unsqueeze(1).to_broadcast([P, H, 32]),
                                      ALU.add).then_inc(v_read, 1)
        pre.close()
        causal_attention(m, name, lambda h: q[:, h // 4, :], lambda h: k[:, h // 4, :],
                         lambda h: m.const["quadrant"][:, h % 4:h % 4 + 1], v, lambda h: (h // 4, h % 4), G,
                         32.0 ** -0.5, mixed)
        y_psum = sem("y_psum")
        y_ready = sem("y_ready")
        with nc.Block(no_gpsimd_drain=True) as block:
            @block.tensor
            def _(pe):
                for g in range(G):
                    ins = pe.matmul(m.bank(6), w["l2o"][:, g, :], mixed[:, g, :], start=g == 0, stop=g == G - 1)
                ins.then_inc(y_psum, 1)
                pe.wait_ge(y_ready, 1)
                pe.matmul(m.bank(OUT), w["cproj"], q[:, 0, :], start=True, stop=True)

            @block.scalar
            def _(act):
                act.wait_ge(y_psum, 1)
                act.activation(q[:, 0, :], m.bank(6), ACT.Identity, bias=w["l2o_b"]).then_inc(y_ready, 1)
    return w["cproj_b"]


def stage_l2_attn(m):
    nc, w, name = m.nc, m.weights("l2_attn"), "l2_attn"
    with ExitStack() as ctx:
        sb = lambda n, shape, dt=F32: ctx.enter_context(nc.sbuf_tensor(f"{name}_{n}", shape, dt))
        sem = lambda n: m.sem(f"{name}_{n}")
        q = sb("q", [P, T])
        k = sb("k", [P, T])
        v = sb("v", [P, NT, H, 32])
        mixed = sb("mixed", [P, 1, T])
        pre = ExitStack()
        psb = lambda n, shape, dt=F32: pre.enter_context(nc.sbuf_tensor(f"{name}_{n}", shape, dt))
        c = psb("centred", [P, 2, NT, D])
        sq = psb("square", [P, 2, NT, D])
        mean = psb("mean", [P, 2, NT * H])
        var = psb("var", [P, 2, NT * H])
        std = psb("std", [P, 2, NT * H])
        tmp = psb("tmp", [P, 2, NT * H])
        qkv_psum = sem("qkv_psum")
        c_ready = sem("c_ready")
        c_turned = sem("c_turned")
        chain_sem = sem("pre_chain")
        with nc.Block(no_gpsimd_drain=True) as block:
            @block.tensor
            def _(pe):
                for t in range(NT):
                    for n in range(3):
                        ins = pe.matmul(m.psum[:, n, t * P:(t + 1) * P], m.xnT[:, t * P:(t + 1) * P],
                                        w["qkv"][:, n, :], start=True, stop=True)
                ins.then_inc(qkv_psum, 1)
                pe.wait_ge(c_ready, 1)
                for n in range(2):
                    for t in range(NT):
                        ins = pe.transpose(m.psum[:, 3 + n, t * P:(t + 1) * P], c[:, n, t, :], m.ident)
                ins.then_inc(c_turned, 1)

            @block.scalar
            def _(act):
                act.wait_ge(c_turned, 1)
                act.activation(q[:, :], m.bank(3), ACT.Identity, scale=w["q_g"], bias=w["q_b"])
                act.activation(k[:, :], m.bank(4), ACT.Identity, scale=w["k_g"], bias=w["k_b"])

            @block.vector
            def _(dve):
                chain = Chain(dve, chain_sem)
                chain.link(dve.memset(v[:, :, :, :], 0.0))
                dve.wait_ge(qkv_psum, 1)
                grouped = lambda a: a.rearrange("p t (h d) -> p (t h) d", d=HD)
                spread = lambda a: a.unsqueeze(2).to_broadcast([P, NT * H, HD])
                psum = lambda n: m.bank(n).rearrange("p (g d) -> p g d", d=HD)
                for n in range(2):
                    ins = dve.tensor_reduce(mean[:, n, :], psum(n), AX, ALU.add)
                chain.link(ins)
                chain.link(dve.tensor_scalar(mean[:, :, :], mean[:, :, :], 1.0 / HD, None, ALU.mult))
                for n in range(2):
                    ins = dve.tensor_tensor(grouped(c[:, n, :, :]), psum(n), spread(mean[:, n, :]), ALU.subtract)
                chain.link(ins)
                chain.link(dve.tensor_tensor(sq[:, :, :, :], c[:, :, :, :], c[:, :, :, :], ALU.mult))
                for n in range(2):
                    ins = dve.tensor_reduce(var[:, n, :], grouped(sq[:, n, :, :]), AX, ALU.add)
                chain.link(ins)
                chain.link(dve.tensor_scalar(var[:, :, :], var[:, :, :], 1.0 / HD, 1e-5, ALU.mult, ALU.add))
                newton_rsqrt(dve, chain, var[:, :, :], std[:, :, :], tmp[:, :, :])
                for n in range(2):
                    ins = dve.tensor_tensor(grouped(c[:, n, :, :]), grouped(c[:, n, :, :]), spread(std[:, n, :]), ALU.mult)
                ins.then_inc(c_ready, 1)
                for r in range(4):
                    for t in range(NT):
                        dve.tensor_copy(v[:, t, r:H:4, 8 * r:8 * r + 8],
                                        m.psum[:, 2, t * P:(t + 1) * P].rearrange(
                                            "p (q r d) -> p q r d", r=4, d=HD)[:, :, r, :])
        pre.close()
        causal_attention(m, name, lambda h: q[:, :], lambda h: k[:, :],
                         lambda h: m.const["head_rows"][:, h:h + 1], v, lambda h: (0, h // 4), 1,
                         float(D) ** -0.5, mixed)
        with nc.Block(no_gpsimd_drain=True) as block:
            @block.tensor
            def _(pe):
                pe.matmul(m.bank(OUT), w["wo"], mixed[:, 0, :], start=True, stop=True)
    return w["bo"]


def stage_l2_xattn(m):
    nc, w, name = m.nc, m.weights("l2_xattn"), "l2_xattn"
    W, J = 64, 8
    limit = 5.0 * W ** 0.5
    with ExitStack() as ctx:
        sb = lambda n, shape, dt=F32: ctx.enter_context(nc.sbuf_tensor(f"{name}_{n}", shape, dt))
        sem = lambda n: m.sem(f"{name}_{n}")
        k_heads = sb("k_heads", [P, H, S2])
        v = sb("v", [S2, J, 2, P])
        q = sb("q", [P, 2, T])
        clipped = sb("clipped", [S2, 2, T])
        prob = sb("prob", [S2, 3, T])
        rec = sb("reciprocal", [P, 2, T])
        mixed = sb("mixed", [P, 2, T])
        kv_psum = sem("kv_psum")
        kv_ready = sem("kv_ready")
        q_psum = sem("q_psum")
        q_ready = sem("q_ready")
        scores = sem("scores")
        clip_ready = sem("clip")
        prob_ready = sem("prob")
        pair_psum = sem("pair")
        mixed_ready = sem("mixed")
        out_done = sem("out")
        chain_sem = sem("chain")
        with nc.Block(no_gpsimd_drain=True) as block:
            @block.tensor
            def _(pe):
                for j in range(J):
                    ins = pe.matmul(m.psum[:, j // 6, (j % 6) * S2:(j % 6 + 1) * S2],
                                    w["wk"][:, j, :], m.ctxT[:, :], start=True, stop=True)
                for n in range(2):
                    ins = pe.matmul(m.psum[0:S2, 2 + n, :], m.ctxT[:, :], w["wv"][:, n, :],
                                    start=True, stop=True)
                ins.then_inc(kv_psum, 1)

                def query(j):
                    if j >= 1:
                        pe.wait_ge(q_ready, j)
                    pe.matmul(m.bank(4), w["wq"][:, j, :], m.xnT[:, :], start=True, stop=True).then_inc(q_psum, 1)

                def score(h):
                    pe.wait_ge(q_ready, h // 2 + 1)
                    if h >= 2:
                        pe.wait_ge(clip_ready, h - 1)
                    pe.matmul(m.psum[0:S2, 5 + h % 2, :], k_heads[:, h, :], q[:, (h // 2) % 2, :],
                              start=True, stop=True).then_inc(scores, 1)

                def mix(h):
                    j, half = divmod(h, 2)
                    pe.wait_ge(prob_ready, h + 1)
                    if half == 0 and j >= 2:
                        pe.wait_ge(mixed_ready, j - 1)
                    a = 2 * (j % 2)
                    pe.matmul(m.bank(a), v[:, j, half, :], prob[:, h % 3, :], start=half == 0, stop=half == 1)
                    pe.matmul(m.bank(a + 1), m.const["halves"][0:S2, half, :], prob[:, h % 3, :],
                              start=half == 0, stop=half == 1).then_inc(pair_psum, 1)

                def project(j):
                    pe.wait_ge(mixed_ready, j + 1)
                    pe.matmul(m.bank(OUT), w["wo"][:, j, :], mixed[:, j % 2, :], start=j == 0,
                              stop=j == J - 1).then_inc(out_done, 1)

                query(0)
                pe.wait_ge(kv_ready, 1)
                for h in range(H + 6):
                    if h % 2 == 0 and h // 2 + 1 < J:
                        query(h // 2 + 1)
                    if h < H:
                        score(h)
                    if 2 <= h < H + 2:
                        mix(h - 2)
                    if h >= 6 and h % 2 == 0 and (h - 6) // 2 < J:
                        project((h - 6) // 2)

            @block.scalar
            def _(act):
                def query(j):
                    act.wait_ge(q_psum, j + 1)
                    if j >= 2:
                        act.wait_ge(scores, 2 * (j - 1))
                    act.activation(q[:, j % 2, :], m.bank(4), ACT.Copy).then_inc(q_ready, 1)

                query(0)
                for h in range(H):
                    if h % 2 == 0 and h // 2 + 1 < J:
                        query(h // 2 + 1)
                    act.wait_ge(clip_ready, h + 1)
                    if h >= 3:
                        act.wait_ge(pair_psum, h - 2)
                    act.activation(prob[:, h % 3, :], clipped[:, h % 2, :], ACT.Exp,
                                   scale=W ** -0.5).then_inc(prob_ready, 1)

            @block.vector
            def _(dve):
                chain = Chain(dve, chain_sem)
                def quotient(dve, chain, j):
                    a = 2 * (j % 2)
                    dve.wait_ge(pair_psum, 2 * j + 2)
                    chain.link(dve.reciprocal(rec[:, j % 2, :], m.bank(a + 1)))
                    if j >= 2:
                        dve.wait_ge(out_done, j - 1)
                    dve.tensor_tensor(mixed[:, j % 2, :], m.bank(a), rec[:, j % 2, :],
                                      ALU.mult).then_inc(mixed_ready, 1)

                chain.link(dve.memset(v[:, :, :, :], 0.0))
                dve.wait_ge(kv_psum, 1)
                for half in range(2):
                    rows = m.const["halves_rows"][:, half:half + 1]
                    for n, (a, b) in enumerate(((0, 6), (6, 8))):
                        dve.tensor_scalar(k_heads[:, 2 * a + half:2 * b:2, :],
                                          m.psum[:, n, 0:(b - a) * S2].rearrange("p (j s) -> p j s", s=S2),
                                          rows, None, ALU.mult)
                    for n in range(2):
                        ins = dve.tensor_copy(
                            v[:, 4 * n:4 * n + 4, half, W * half:W * half + W],
                            m.psum[0:S2, 2 + n, :].rearrange("p (j a d) -> p j a d", a=2, d=W)[:, :, half, :])
                ins.then_inc(kv_ready, 1)
                for h in range(H + 3):
                    if h < H:
                        dve.wait_ge(scores, h + 1)
                        if h >= 2:
                            dve.wait_ge(prob_ready, h - 1)
                        dve.tensor_scalar(clipped[:, h % 2, :], m.psum[0:S2, 5 + h % 2, :], -limit,
                                          m.bound[:, :], ALU.max, ALU.min).then_inc(clip_ready, 1)
                    if h >= 4 and h % 2 == 0:
                        quotient(dve, chain, h // 2 - 2)

    return m.weights("columns")["l2_xattn_bo"]


def padded_conv(dve, chain, out, src, taps):
    chain.link(dve.tensor_scalar(out, src[:, 0:T], taps[:, 0:1], None, ALU.mult))
    for i in (1, 2):
        chain.link(dve.scalar_tensor_tensor(out=out, in0=src[:, i:i + T], scalar=taps[:, i:i + 1], in1=out,
                                            op0=ALU.mult, op1=ALU.add))
    return dve.scalar_tensor_tensor(out=out, in0=src[:, 3:3 + T], scalar=taps[:, 3:4], in1=out,
                                    op0=ALU.mult, op1=ALU.add)


def softplus_log(act, chain, x, out):
    chain.link(act.activation(out, x, ACT.Abs))
    chain.link(act.activation(out, out, ACT.Exp, scale=-1.0))
    return act.activation(out, out, ACT.Ln, bias=1.0)


def stage_l3_attn(m):
    nc, w, name = m.nc, m.weights("l3_attn"), "l3_attn"
    NH, NS = 2, 64
    with ExitStack() as ctx:
        sb = lambda n, shape, dt=F32: ctx.enter_context(nc.sbuf_tensor(f"{name}_{n}", shape, dt))
        sem = lambda n: m.sem(f"{name}_{n}")
        xpad = sb("xpad", [P, NH, 3 + T])
        conv = sb("conv", [P, NH, T])
        xs = sb("xs", [P, NH, T])
        zs = sb("zs", [P, NH, T])
        bT = sb("bT", [P, T])
        cT = sb("cT", [P, T])
        dt_raw = sb("dt_raw", [P, NT, NH])
        dt_log = sb("dt_log", [P, NT, NH])
        dt_ = sb("dt", [P, NT, NH])
        a = sb("a", [P, NT, NH])
        a_exp = sb("a_exp", [P, NH])
        a_from = sb("a_from", [P, NH, NT, T])
        xd = sb("xd", [P, NT, NH, P])
        decay = sb("decay", [P, 2, T])
        mix = sb("mix", [P, 2, T])
        y = sb("y", [P, NH, T])
        in_psum = sem("in_psum")
        x_ready = sem("x_ready")
        conv_ready = sem("conv")
        xs_ready = sem("xs")
        z_ready = sem("z")
        ssm_psum = sem("ssm_psum")
        bc_ready = sem("bc")
        dt_added = sem("dt_added")
        dt_logged = sem("dt_logged")
        a_ready = sem("a_ready")
        x_turned = sem("x_turned")
        xd_ready = sem("xd")
        sums_psum = sem("sums")
        decay_ready = sem("decay")
        mix_ready = sem("mix")
        mixed = sem("mixed")
        y_ready = sem("y")
        chain_sem, act_chain = sem("chain"), sem("act_chain")
        last = lambda i: T - i * P
        with nc.Block(no_gpsimd_drain=True) as block:
            @block.tensor
            def _(pe):
                for n in range(4):
                    pe.matmul(m.bank(n), w["w_in"][:, n, :], m.xnT[:, :], start=True,
                              stop=True).then_inc(in_psum, 1)
                pe.wait_ge(xs_ready, NH)
                for n, cols in ((4, w["w_b"]), (5, w["w_c"])):
                    for c in range(NH):
                        pe.matmul(m.bank(n), cols[:, c, :], xs[:, c, :], start=c == 0, stop=c == NH - 1)
                for t in range(NT):
                    for c in range(NH):
                        ins = pe.matmul(m.psum[:, 6, NH * t:NH * t + NH], xs[:, c, t * P:(t + 1) * P],
                                        w["w_dt"][:, c, :], start=c == 0, stop=c == NH - 1)
                ins.then_inc(ssm_psum, 1)
                for c in range(NH):
                    for t in range(NT):
                        ins = pe.transpose(m.psum[:, c, t * P:(t + 1) * P], xs[:, c, t * P:(t + 1) * P], m.ident)
                    ins.then_inc(x_turned, 1)
                pe.wait_ge(a_ready, 1)
                pe.wait_ge(bc_ready, 1)
                pe.wait_ge(xd_ready, NH)
                for n in range(2 * NT + 1):
                    if n < 2 * NT:
                        h, i = divmod(n, NT)
                        if n >= 2:
                            pe.wait_ge(mix_ready, n - 1)
                        bank = 2 * (n % 2)
                        for k in range(i, NT):
                            pe.matmul(m.psum[:, bank, (k - i) * P:last(i)],
                                      m.const["after"] if k == i else m.const["ones"],
                                      a_from[:, h, k, 0:last(k)], start=k == i, stop=k == NT - 1)
                        rows = slice(NS * h, NS * h + NS)
                        pe.matmul(m.psum[:, bank + 1, 0:last(i)], bT[rows, i * P:(i + 1) * P],
                                  cT[rows, i * P:T], start=True, stop=True).then_inc(sums_psum, 1)
                    if n >= 1:
                        h, i = divmod(n - 1, NT)
                        pe.wait_ge(mix_ready, n)
                        pe.matmul(m.psum[:, 4 + h, i * P:T], xd[:, i, h, :], mix[:, (n - 1) % 2, 0:last(i)],
                                  start=i == 0, stop=i == NT - 1).then_inc(mixed, 1)
                for h in range(NH):
                    pe.wait_ge(y_ready, h + 1)
                    pe.matmul(m.bank(OUT), w["w_out"][:, h, :], y[:, h, :], start=h == 0, stop=h == NH - 1)

            @block.scalar
            def _(act):
                chain = Chain(act, act_chain)
                for c in range(NH):
                    act.wait_ge(in_psum, c + 1)
                    act.activation(xpad[:, c, 3:3 + T], m.bank(c), ACT.Copy).then_inc(x_ready, 1)
                act.wait_ge(in_psum, 4)
                for c in range(NH):
                    act.activation(zs[:, c, :], m.bank(2 + c), ACT.Sigmoid).then_inc(z_ready, 1)
                for c in range(NH):
                    act.wait_ge(conv_ready, c + 1)
                    act.activation(xs[:, c, :], conv[:, c, :], ACT.Silu,
                                   bias=w["conv_b"][:, c:c + 1]).then_inc(xs_ready, 1)
                act.wait_ge(ssm_psum, 1)
                act.activation(bT[:, :], m.bank(4), ACT.Copy)
                act.activation(cT[:, :], m.bank(5), ACT.Copy).then_inc(bc_ready, 1)
                act.wait_ge(dt_added, 1)
                act.activation(a_exp[:, :], w["a_log"], ACT.Exp)
                softplus_log(act, chain, dt_raw[:, :, :], dt_log[:, :, :]).then_inc(dt_logged, 1)
                for n in range(2 * NT):
                    act.wait_ge(sums_psum, n + 1)
                    if n >= 2:
                        act.wait_ge(mix_ready, n - 1)
                    act.activation(decay[:, n % 2, 0:last(n % NT)], m.psum[:, 2 * (n % 2), 0:last(n % NT)],
                                   ACT.Exp).then_inc(decay_ready, 1)

            @block.vector
            def _(dve):
                chain = Chain(dve, chain_sem)
                chain.link(dve.memset(xpad[:, :, 0:3], 0.0))
                for c in range(NH):
                    dve.wait_ge(x_ready, c + 1)
                    padded_conv(dve, chain, conv[:, c, :], xpad[:, c, :], w["conv_w"][:, c, :]).then_inc(conv_ready, 1)
                dve.wait_ge(ssm_psum, 1)
                dve.tensor_tensor(dt_raw[:, :, :], m.psum[:, 6, 0:NT * NH].rearrange("p (t h) -> p t h", h=NH),
                                  w["dt_bias"].unsqueeze(1).to_broadcast([P, NT, NH]), ALU.add).then_inc(dt_added, 1)
                dve.wait_ge(dt_logged, 1)
                chain.link(dve.scalar_tensor_tensor(out=dt_[:, :, :], in0=dt_raw[:, :, :], scalar=0.0,
                                                    in1=dt_log[:, :, :], op0=ALU.max, op1=ALU.add))
                chain.link(dve.tensor_tensor(a[:, :, :], dt_[:, :, :],
                                             a_exp[:, :].unsqueeze(1).to_broadcast([P, NT, NH]), ALU.mult))
                for h in range(NH):
                    for k in range(NT):
                        ins = dve.tensor_scalar(a_from[:, h, k, 0:last(k)], m.const["upto"][:, 0:last(k)],
                                                a[:, k, h:h + 1], -1.0, ALU.mult, ALU.mult)
                ins.then_inc(a_ready, 1)
                for h in range(NH):
                    dve.wait_ge(x_turned, h + 1)
                    for t in range(NT):
                        ins = dve.tensor_scalar(xd[:, t, h, :], m.psum[:, h, t * P:(t + 1) * P],
                                                dt_[:, t, h:h + 1], None, ALU.mult)
                    ins.then_inc(xd_ready, 1)

                def output(h):
                    dve.wait_ge(mixed, NT * (h + 1))
                    chain.link(dve.scalar_tensor_tensor(out=y[:, h, :], in0=xs[:, h, :],
                                                        scalar=w["d_skip"][:, h:h + 1], in1=m.bank(4 + h),
                                                        op0=ALU.mult, op1=ALU.add))
                    dve.wait_ge(z_ready, h + 1)
                    dve.tensor_tensor(y[:, h, :], y[:, h, :], zs[:, h, :], ALU.mult).then_inc(y_ready, 1)

                for n in range(2 * NT):
                    i = n % NT
                    d = decay[:, n % 2, 0:last(i)]
                    dve.wait_ge(decay_ready, n + 1)
                    chain.link(dve.tensor_tensor(decay[:, n % 2, 0:P], decay[:, n % 2, 0:P],
                                                 m.const["upto"][:, 0:P], ALU.mult))
                    if n >= 2:
                        dve.wait_ge(mixed, n - 1)
                    dve.tensor_tensor(mix[:, n % 2, 0:last(i)], d, m.psum[:, 2 * (n % 2) + 1, 0:last(i)],
                                      ALU.mult).then_inc(mix_ready, 1)
                    if n == NT + 1:
                        output(0)
                output(1)
    return None


def stage_l3_xattn(m):
    nc, w, name = m.nc, m.weights("l3_xattn"), "l3_xattn"
    with ExitStack() as ctx:
        sb = lambda n, shape, dt=F32: ctx.enter_context(nc.sbuf_tensor(f"{name}_{n}", shape, dt))
        sem = lambda n: m.sem(f"{name}_{n}")
        kernel_f = sb("kernel_f", [P, 3, 2, D])
        prod = sb("prod", [P, 2, 2, D])
        tmp = sb("tmp", [P, 2, 2, D])
        mean = sb("mean", [P, 1])
        wave_psum = sem("wave")
        kernel_ready = sem("kernel")
        prod_ready = sem("prod")
        mean_ready = sem("mean")
        mod_psum = sem("mod")
        chain_sem = sem("chain")
        with nc.Block(no_gpsimd_drain=True) as block:
            @block.tensor
            def _(pe):
                for n, key in enumerate(("kernel_re", "kernel_re2", "kernel_im")):
                    for f in range(2):
                        ins = pe.matmul(m.psum[:, n // 2, (2 * (n % 2) + f) * D:(2 * (n % 2) + f + 1) * D],
                                        w[key][:, f, :], w["taps"], start=True, stop=True)
                ins.then_inc(wave_psum, 1)
                for f in range(4):
                    for t in range(NT):
                        ins = pe.matmul(m.psum[:, 2, f * D:(f + 1) * D], w["forward"][:, t, f * P:(f + 1) * P],
                                        m.xn[:, t, :], start=t == 0, stop=t == NT - 1)
                ins.then_inc(wave_psum, 1)
                pe.wait_ge(mean_ready, 1)
                pe.matmul(m.psum[:, 3, 0:1], w["kp_w"], mean[:, :], start=True, stop=True).then_inc(mod_psum, 1)
                pe.wait_ge(prod_ready, 1)
                for n in range(2):
                    for f in range(2):
                        pe.matmul(m.bank(OUT), prod[:, n, f, :], w["inverse"][:, 2 * n + f, :],
                                  start=n + f == 0, stop=n + f == 2)

            @block.scalar
            def _(act):
                act.wait_ge(wave_psum, 1)
                act.activation(kernel_f[:, 0:2, :, :],
                               m.bank(0).rearrange("p (a f d) -> p a f d", a=2, d=D), ACT.Copy)
                act.activation(kernel_f[:, 2, :, :],
                               m.psum[:, 1, 0:2 * D].rearrange("p (f d) -> p f d", d=D),
                               ACT.Copy).then_inc(kernel_ready, 1)
                act.wait_ge(mod_psum, 1)
                act.activation(m.mod[:, :], m.psum[:, 3, 0:1], ACT.Identity, scale=1.0 / S2, bias=w["kp_b"])

            @block.vector
            def _(dve):
                chain = Chain(dve, chain_sem)
                dve.tensor_reduce(mean[:, :], m.ctxT[:, :], AX, ALU.add).then_inc(mean_ready, 1)
                dve.wait_ge(kernel_ready, 1)
                dve.wait_ge(wave_psum, 2)
                x = m.bank(2).rearrange("p (a f d) -> p a f d", a=2, d=D)
                dve.tensor_tensor(prod[:, 0, :, :], x[:, 0], kernel_f[:, 0, :, :], ALU.mult)
                dve.tensor_tensor(prod[:, 1, :, :], x[:, 1], kernel_f[:, 1, :, :], ALU.mult)
                dve.tensor_tensor(tmp[:, 0, :, :], x[:, 1], kernel_f[:, 2, :, :], ALU.mult)
                chain.link(dve.tensor_tensor(tmp[:, 1, :, :], x[:, 0], kernel_f[:, 2, :, :], ALU.mult))
                dve.tensor_tensor(prod[:, 0, :, :], prod[:, 0, :, :], tmp[:, 0, :, :], ALU.subtract)
                dve.tensor_tensor(prod[:, 1, :, :], prod[:, 1, :, :], tmp[:, 1, :, :],
                                  ALU.add).then_inc(prod_ready, 1)
    return ("scale", m.mod[:, :])


def stage_l2_ffn(m):
    nc, w, name = m.nc, m.weights("l2_ffn"), "l2_ffn"
    NV, E, F, W, KD = 5, 4, 4, 64, 512
    HH = 2 * F
    with ExitStack() as ctx:
        sb = lambda n, shape, dt=F32: ctx.enter_context(nc.sbuf_tensor(f"{name}_{n}", shape, dt))
        sem = lambda n: m.sem(f"{name}_{n}")
        low_a = sb("low_a", [P, T])
        low_b = sb("low_b", [P, T])
        own = sb("own", [P, NT, E])
        share = sb("share", [P, NT, E])
        outT = sb("outT", [P, F, T])
        mid = ExitStack()
        msb = lambda n, shape, dt=F32: mid.enter_context(nc.sbuf_tensor(f"{name}_{n}", shape, dt))
        logit = msb("logit", [P, NT, E])
        cmp = msb("cmp", [P, 2, NT, E, E])
        top = msb("top", [P, NT])
        rank = msb("rank", [P, NT, E])
        gk = msb("gk", [P, 2, KD])
        gk_log = msb("gk_log", [P, 2, KD])
        k2 = msb("k2", [P, KD])
        k2_top = msb("k2_top", [P, HH])
        k2_sum = msb("k2_sum", [P, HH])
        k1 = msb("k1", [P, KD])
        v = msb("v", [P, KD])
        q1T, k1T, q2T, k2T = (msb(n, [P, F, P]) for n in ("q1T", "k1T", "q2T", "k2T"))
        shareT = msb("shareT", [P, E, P])
        diag = msb("diag", [P, E, P])
        mid_e = msb("mid_e", [P, E, P])
        after_e = msb("after_e", [P, E, P])
        half_e = msb("half_e", [P, E, 2])
        small = msb("small", [P, NT * F, 2 * NV])
        qg = msb("qg", [P, 2, NV, P])
        kg = msb("kg", [P, 2, NV, P])
        state = msb("state", [P, F, NV, P])
        state_mid = msb("state_mid", [P, 2, NV, P])
        rest = msb("rest", [P, KD])
        k_out = msb("k_out", [P, NV, KD])
        att = gk_log[:, :, :].rearrange("p a (h s) -> p (a h) s", s=P)

        low_psum = sem("low_psum")
        shares_ready = sem("shares")
        act_chain, chain_sem = sem("act_chain"), sem("chain")
        pre_act, pre_ready = sem("pre_act"), sem("pre_ready")
        with nc.Block(no_gpsimd_drain=True) as block:
            @block.tensor
            def _(pe):
                pe.matmul(m.bank(0), w["low_a"], m.xnT[:, :], start=True, stop=True)
                pe.matmul(m.bank(1), w["low_b"], m.xnT[:, :], start=True, stop=True)
                for t in range(NT):
                    ins = pe.matmul(m.psum[:, 2, t * E:(t + 1) * E], m.xnT[:, t * P:(t + 1) * P], w["router"],
                                    start=True, stop=True)
                ins.then_inc(low_psum, 1)

            @block.scalar
            def _(act):
                act.wait_ge(low_psum, 1)
                act.activation(low_a[:, :], m.bank(0), ACT.Copy)
                act.activation(low_b[:, :], m.bank(1), ACT.Identity, bias=w["one_rows"])
                act.wait_ge(pre_act, 1)
                act.activation(logit[:, :, :], logit[:, :, :], ACT.Exp).then_inc(pre_ready, 1)

            @block.vector
            def _(dve):
                chain = Chain(dve, chain_sem)
                dve.wait_ge(low_psum, 1)
                raw = m.psum[:, 2, 0:NT * E].rearrange("p (t e) -> p t e", e=E)
                over = lambda a: a.unsqueeze(2).to_broadcast([P, NT, E])
                chain.link(dve.tensor_reduce(top[:, :], raw, AX, ALU.max))
                dve.tensor_tensor(logit[:, :, :], raw, over(top[:, :]), ALU.subtract).then_inc(pre_act, 1)
                dve.wait_ge(pre_ready, 1)
                rank_experts(dve, chain, logit[:, :, :], cmp[:, 0], cmp[:, 1], m.const["lower4"], rank[:, :, :], E)
                chain.link(dve.tensor_scalar(own[:, :, :], rank[:, :, :], 1.0, None, ALU.is_lt))
                chain.link(dve.tensor_reduce(top[:, :], logit[:, :, :], AX, ALU.add))
                chain.link(dve.reciprocal(top[:, :], top[:, :]))
                chain.link(dve.tensor_tensor(share[:, :, :], own[:, :, :], logit[:, :, :], ALU.mult))
                dve.tensor_tensor(share[:, :, :], share[:, :, :], over(top[:, :]), ALU.mult).then_inc(shares_ready, 1)

        main_chain = sem("main_chain")
        masks_ready = sem("masks")
        by_act = sem("by_act")
        by_dve = sem("by_dve")
        unit_psum = sem("unit")
        k2_exp = sem("k2_exp")
        k2_ready = sem("k2_ready")
        gk_logged = sem("gk_logged")
        rest_ready = sem("rest")
        k_out_ready = sem("k_out")
        sums_psum = sem("sums")
        kg_ready = sem("kg")
        kg_shared = sem("kg_shared")
        sums_read = sem("sums_read")
        q_ready = sem("q")
        k_ready = sem("k")
        mid_ready = sem("mid")
        att_psum = sem("att_psum")
        att_ready = sem("att")
        o_psum = sem("o_psum")
        o_read = sem("o_read")
        kv_psum = sem("kv_psum")
        scaled = sem("scaled")
        kv_read = sem("kv_read")

        UNITS = ["g1", "g2", "k2", "k1", "v", "q1T", "k1T", "q2T", "share", "k2T"] + ["rest"] * NV
        NU = len(UNITS)
        DVE_READS = [j for j, u in enumerate(UNITS) if u in ("g1", "g2", "k2", "share")]
        ACT_READS = [j for j in range(NU) if j not in DVE_READS]

        def read(n):
            t, j = divmod(n, NU)
            reads, s = (DVE_READS, by_dve) if j in DVE_READS else (ACT_READS, by_act)
            return s, t * len(reads) + reads.index(j) + 1

        head = lambda h: slice(W * (h % 2), W * (h % 2) + W)
        tok = lambda t: slice(t * P, (t + 1) * P)

        with nc.Block(no_gpsimd_drain=True) as block:
            @block.tensor
            def _(pe):
                def unit(t, j, emit):
                    n = NU * t + j
                    if n >= 3:
                        pe.wait_ge(*read(n - 3))
                    emit(m.bank(n % 3)).then_inc(unit_psum, 1)

                def product(lhsT, rhs):
                    return lambda bank: pe.matmul(bank, lhsT, rhs, start=True, stop=True)

                def by_features(weight, rhs):
                    def emit(bank):
                        for f in range(F):
                            ins = pe.matmul(bank[:, tok(f)], weight[:, tok(f)], rhs, start=True, stop=True)
                        return ins
                    return emit

                def k2_turn(bank):
                    for f in range(F):
                        ins = pe.transpose(bank[:, tok(f)], k2[:, tok(f)], m.ident)
                    return ins

                for t in range(NT):
                    x = m.xnT[:, tok(t)]
                    unit(t, 0, product(low_b[64:81, tok(t)], w["up_b"][64:81, :]))
                    unit(t, 1, product(low_b[96:113, tok(t)], w["up_b"][96:113, :]))
                    unit(t, 2, product(low_a[64:128, tok(t)], w["up_a"][64:128, :]))
                    unit(t, 3, product(x, w["wk"]))
                    unit(t, 4, product(x, w["wv"]))
                    unit(t, 5, by_features(w["wq"], x))
                    unit(t, 6, by_features(w["wk"], x))
                    unit(t, 7, by_features(w["up_a"][0:64, :], low_a[0:64, tok(t)]))
                    pe.wait_ge(masks_ready, t + 1)
                    unit(t, 8, product(m.const["ones"], diag[:, :, :].rearrange("p e s -> p (e s)")))
                    pe.wait_ge(k2_ready, t + 1)
                    unit(t, 9, k2_turn)

                    def sums(f):
                        u = F * t + f
                        if u >= 1:
                            pe.wait_ge(sums_read, u)
                        if f == 0 and t > 0:
                            pe.wait_ge(kv_read, F * t)
                        gd, ge = gk[:, 0, tok(f)], gk[:, 1, tok(f)]
                        pe.matmul(m.bank(3), ge, mid_e[:, :, :].rearrange("p e s -> p (e s)"), start=True, stop=True)
                        pe.matmul(m.psum[:, 4, 0:P], gd, m.const["centred"], start=True, stop=True)
                        pe.matmul(m.psum[:, 4, P:P + 2], gd, m.const["half_all"], start=True, stop=True)
                        pe.matmul(m.psum[:, 4, P + 2:P + 2 * NV], ge, half_e[:, :, :].rearrange("p e s -> p (e s)"),
                                  start=True, stop=True).then_inc(sums_psum, 1)

                    def scores(f):
                        u = F * t + f
                        pe.wait_ge(q_ready, u + 1)
                        pe.wait_ge(k_ready, u + 1)
                        if u >= 1:
                            pe.wait_ge(att_ready, u)
                        for half in range(2):
                            rows = head(half)
                            for n in range(NV):
                                ins = pe.matmul(m.psum[:, 5 + half, 0:P], kg[rows, f % 2, n, :], qg[rows, f % 2, n, :],
                                                start=n == 0, stop=n == NV - 1)
                        ins.then_inc(att_psum, 1)

                    def output(f):
                        u = F * t + f
                        pe.wait_ge(att_ready, u + 1)
                        if u >= 1:
                            pe.wait_ge(o_read, u)
                        o = m.psum[:, OUT, 0:P]
                        if t > 0:
                            pe.wait_ge(mid_ready, u - F + 1)
                            for n in range(NV):
                                pe.matmul(o, state_mid[:, f % 2, n, :], qg[:, f % 2, n, :], start=n == 0,
                                          stop=n == NV - 1)
                        for half in range(2):
                            h = 2 * f + half
                            ins = pe.matmul(m.psum[head(half), OUT, 0:P], v[:, W * h:W * h + W], att[:, h, :],
                                            start=t == 0, stop=True, skip_group_check=True)
                        ins.then_inc(o_psum, 1)

                    for n in range(NV):
                        if n in (0, 3):
                            sums(n // 3)
                        lhsT = m.const["after"] if n == 0 else after_e[:, n - 1, :]
                        unit(t, 10 + n, product(lhsT, gk[:, min(n, 1), :]))
                    for f in range(1, F + 2):
                        if 2 <= f < F:
                            sums(f)
                        if f >= 2:
                            output(f - 2)
                        if f <= F:
                            scores(f - 1)
                    for f in range(F if t < NT - 1 else 0):
                        u = F * t + f
                        if f == 0:
                            pe.wait_ge(sums_read, F * (t + 1))
                            pe.wait_ge(k_out_ready, NV * (t + 1))
                        elif f == 1:
                            pe.wait_ge(att_ready, F * (t + 1))
                        else:
                            pe.wait_ge(kv_read, u - 1)
                        first = 3 + 2 * (f % 2)
                        for n in range(NV):
                            dst = m.psum[:, first, tok(n)] if n < 4 else m.psum[:, first + 1, 0:P]
                            ins = pe.matmul(dst, k_out[:, n, tok(f)], v[:, tok(f)], start=True, stop=True)
                        ins.then_inc(kv_psum, 1)

            @block.gpsimd
            def _(pool):
                pool.memset(state[:, :, :, :], 0.0)
                for t in range(NT):
                    over = lambda a: a.unsqueeze(1).to_broadcast([P, E, P])
                    of = lambda a: a[:, t, :].unsqueeze(2).to_broadcast([P, E, P])
                    if t > 0:
                        pool.wait_ge(sums_psum, F * t)
                    pool.tensor_tensor(diag[:, :, :], over(m.ident), of(share), ALU.mult)
                    pool.tensor_tensor(mid_e[:, :, :], over(m.const["centred"]), of(own), ALU.mult)
                    pool.tensor_tensor(half_e[:, :, :], m.const["half_all"].unsqueeze(1).to_broadcast([P, E, 2]),
                                       own[:, t, :].unsqueeze(2).to_broadcast([P, E, 2]), ALU.mult)
                    pool.tensor_tensor(after_e[:, :, :], over(m.const["after"]), of(own),
                                       ALU.mult).then_inc(masks_ready, 1)
                    for f in range(F):
                        u = F * t + f
                        s = f % 2
                        pool.wait_ge(kg_ready, u + 1)
                        if f == 0:
                            pool.wait_ge(*read(NU * t + 9))
                        pool.tensor_tensor(kg[:, s, 0, :], kg[:, s, 0, :], k1T[:, f, :], ALU.mult)
                        pool.wait_ge(kg_shared, u + 1)
                        pool.tensor_tensor(kg[:, s, 1:NV, :], kg[:, s, 1:NV, :], over(k2T[:, f, :]),
                                           ALU.mult).then_inc(k_ready, 1)
                    for f in range(F if 0 < t < NT - 1 else 0):
                        u = F * t + f
                        pool.wait_ge(mid_ready, u - F + 1)
                        pool.tensor_tensor(state[:, f, :, :], state[:, f, :, :],
                                           small[:, u, 1:2 * NV:2].unsqueeze(2).to_broadcast([P, NV, P]),
                                           ALU.mult).then_inc(scaled, 1)

            @block.scalar
            def _(act):
                chain = Chain(act, act_chain)

                def take(t, j, out, func=ACT.Copy, scale=1.0):
                    n = NU * t + j
                    act.wait_ge(unit_psum, n + 1)
                    act.activation(out, m.bank(n % 3), func, scale=scale).then_inc(by_act, 1)

                def copy_out(t, f):
                    act.wait_ge(o_psum, F * t + f + 1)
                    act.activation(outT[:, f, tok(t)], m.psum[:, OUT, 0:P], ACT.Copy).then_inc(o_read, 1)

                for t in range(NT):
                    if t > 0:
                        act.wait_ge(o_psum, F * t)
                        act.wait_ge(kv_psum, F * t)
                    for j in range(2):
                        act.wait_ge(unit_psum, NU * t + j + 1)
                        ins = act.activation(gk_log[:, j, :], m.bank((NU * t + j) % 3), ACT.Abs)
                    chain.link(ins)
                    chain.link(act.activation(gk_log[:, :, :], gk_log[:, :, :], ACT.Exp, scale=-1.0))
                    act.activation(gk_log[:, :, :], gk_log[:, :, :], ACT.Ln, bias=1.0).then_inc(gk_logged, 1)
                    act.wait_ge(*read(NU * t + 2))
                    act.activation(k2[:, :], k2[:, :], ACT.Exp).then_inc(k2_exp, 1)
                    flat = lambda a: a.rearrange("p f s -> p (f s)")
                    take(t, 3, k1[:, :])
                    take(t, 4, v[:, :])
                    take(t, 5, flat(q1T[:, :, :]), scale=W ** -0.5)
                    take(t, 6, flat(k1T[:, :, :]))
                    take(t, 7, flat(q2T[:, :, :]), scale=W ** -0.5)
                    take(t, 9, flat(k2T[:, :, :]))

                    def exponentials(f):
                        u = F * t + f
                        act.wait_ge(sums_psum, u + 1)
                        if u >= 2:
                            act.wait_ge(o_psum, u - 1)
                        if t > 0 and f == 0:
                            act.wait_ge(kv_read, F * t)
                        for sign, out, done in ((-1.0 / 16, kg, kg_ready), (1.0 / 16, qg, None)):
                            act.activation(out[:, f % 2, 0, :], m.psum[:, 4, 0:P], ACT.Exp, scale=sign)
                            ins = act.activation(out[:, f % 2, 1:NV, :], m.bank(3).rearrange("p (e s) -> p e s", s=P),
                                                 ACT.Exp, scale=sign)
                            if done is not None:
                                ins.then_inc(done, 1)
                        act.activation(small[:, u, :], m.psum[:, 4, P:P + 2 * NV], ACT.Exp,
                                       scale=1.0 / 16).then_inc(sums_read, 1)

                    for n in range(NV):
                        if n in (0, 3):
                            exponentials(n // 3)
                        if n >= 1 or t > 0:
                            act.wait_ge(k_out_ready, NV * t + n)
                        take(t, 10 + n, rest[:, :], ACT.Exp, 1.0 / 16)
                    for f in range(2, F):
                        exponentials(f)
                        copy_out(t, f - 2)
                    for f in range(F - 2, F):
                        copy_out(t, f)

            @block.vector
            def _(dve):
                chain = Chain(dve, main_chain)
                for t in range(NT):
                    heads = lambda a: a.rearrange("p (h d) -> p h d", d=W)
                    over = lambda a: a.unsqueeze(2).to_broadcast([P, HH, W])
                    if t > 0:
                        dve.wait_ge(unit_psum, NU * t)
                        dve.wait_ge(sums_psum, F * t)
                        dve.wait_ge(k_ready, F * t)
                        dve.wait_ge(k_out_ready, NV * t)
                        dve.wait_ge(q_ready, F * t)
                    bank = lambda j: m.bank((NU * t + j) % 3)
                    dve.wait_ge(gk_logged, t + 1)
                    for j in range(2):
                        dve.scalar_tensor_tensor(out=gk[:, j, :], in0=bank(j), scalar=0.0, in1=gk_log[:, j, :],
                                                 op0=ALU.min, op1=ALU.subtract).then_inc(by_dve, 1)
                    dve.wait_ge(unit_psum, NU * t + 3)
                    chain.link(dve.tensor_reduce(k2_top[:, :], heads(bank(2)), AX, ALU.max))
                    dve.tensor_tensor(heads(k2[:, :]), heads(bank(2)), over(k2_top[:, :]),
                                      ALU.subtract).then_inc(by_dve, 1)
                    dve.wait_ge(k2_exp, t + 1)
                    chain.link(dve.tensor_reduce(k2_sum[:, :], heads(k2[:, :]), AX, ALU.add))
                    chain.link(dve.reciprocal(k2_sum[:, :], k2_sum[:, :]))
                    dve.tensor_tensor(heads(k2[:, :]), heads(k2[:, :]), over(k2_sum[:, :]), ALU.mult).then_inc(k2_ready, 1)
                    dve.wait_ge(unit_psum, NU * t + 9)
                    dve.tensor_copy(shareT[:, :, :], bank(8).rearrange("p (e s) -> p e s", s=P)).then_inc(by_dve, 1)
                    dve.wait_ge(k2_ready, t + 1)
                    dve.wait_ge(by_dve, len(DVE_READS) * (t + 1))
                    def queries(f):
                        u = F * t + f
                        s = f % 2
                        dve.wait_ge(kg_ready, u + 1)
                        dve.tensor_tensor(kg[:, s, 1:NV, :], kg[:, s, 1:NV, :], shareT[:, :, :],
                                          ALU.mult).then_inc(kg_shared, 1)
                        dve.wait_ge(sums_read, u + 1)
                        dve.tensor_tensor(qg[:, s, 0, :], qg[:, s, 0, :], q1T[:, f, :], ALU.mult)
                        chain.link(dve.tensor_tensor(qg[:, s, 1:NV, :], qg[:, s, 1:NV, :], shareT[:, :, :], ALU.mult))
                        dve.tensor_tensor(qg[:, s, 1:NV, :], qg[:, s, 1:NV, :],
                                          q2T[:, f, :].unsqueeze(1).to_broadcast([P, E, P]), ALU.mult).then_inc(q_ready, 1)
                        if t > 0:
                            dve.wait_ge(kv_read, F * t)
                            dve.tensor_tensor(state_mid[:, s, :, :], state[:, f, :, :],
                                              small[:, u, 0:2 * NV:2].unsqueeze(2).to_broadcast([P, NV, P]),
                                              ALU.mult).then_inc(mid_ready, 1)

                    def masked(f):
                        u = F * t + f
                        dve.wait_ge(att_psum, u + 1)
                        for half in range(2):
                            ins = dve.tensor_tensor(att[:, 2 * f + half, :], m.psum[:, 5 + half, 0:P],
                                                    m.const["upto"][:, 0:P], ALU.mult)
                        ins.then_inc(att_ready, 1)

                    for n in range(NV):
                        if n in (0, 3):
                            queries(n // 3)
                        dve.wait_ge(*read(NU * t + 10 + n))
                        if n == 0:
                            dve.tensor_tensor(k_out[:, 0, :], rest[:, :], k1[:, :], ALU.mult).then_inc(k_out_ready, 1)
                        else:
                            dve.scalar_tensor_tensor(out=k_out[:, n, :], in0=rest[:, :], scalar=share[:, t, n - 1:n],
                                                     in1=k2[:, :], op0=ALU.mult,
                                                     op1=ALU.mult).then_inc(k_out_ready, 1)
                    for f in range(1, F + 1):
                        if 2 <= f < F:
                            queries(f)
                        masked(f - 1)
                    for f in range(F if t < NT - 1 else 0):
                        u = F * t + f
                        dve.wait_ge(kv_psum, u + 1)
                        if t > 0:
                            dve.wait_ge(scaled, F * (t - 1) + f + 1)
                        first = 3 + 2 * (f % 2)
                        for half in range(2):
                            rows, cols = head(half), slice(W * half, W * half + W)
                            new = m.psum[rows, first, :].rearrange("p (e s) -> p e s", s=P)[:, :, cols]
                            last = m.psum[rows, first + 1, cols]
                            if t == 0:
                                dve.tensor_copy(state[rows, f, 0:4, cols], new)
                                ins = dve.tensor_copy(state[rows, f, 4, cols], last)
                            else:
                                dve.tensor_tensor(state[rows, f, 0:4, cols], state[rows, f, 0:4, cols], new, ALU.add)
                                ins = dve.tensor_tensor(state[rows, f, 4, cols], state[rows, f, 4, cols], last, ALU.add)
                        ins.then_inc(kv_read, 1)
        mid.close()

        square = sb("square", [P, 2, T])
        rms = sb("rms", [P, F, T])
        gate = sb("gate", [P, 2, T])
        y = sb("y", [P, 2, T])
        square_ready = sem("square")
        var_psum = sem("var")
        rms_ready = sem("rms")
        normed = sem("normed")
        gate_psum = sem("gate_psum")
        gate_ready = sem("gate")
        y_ready = sem("y")
        y_used = sem("y_used")
        end_chain = sem("end_chain")
        with nc.Block(no_gpsimd_drain=True) as block:
            @block.tensor
            def _(pe):
                for f in range(F):
                    pe.wait_ge(square_ready, f + 1)
                    pe.matmul(m.bank(f), m.const["blocks"], square[:, f % 2, :], start=True,
                              stop=True).then_inc(var_psum, 1)
                for f in range(F + 1):
                    if f < F:
                        if f >= 2:
                            pe.wait_ge(gate_ready, f - 1)
                        pe.matmul(m.bank(4 + f % 2), w["up_b"][0:64, tok(f)], low_b[0:64, :], start=True,
                                  stop=True).then_inc(gate_psum, 1)
                    if f >= 1:
                        pe.wait_ge(y_ready, f)
                        pe.matmul(m.bank(OUT), w["wo"][:, f - 1, :], y[:, (f - 1) % 2, :], start=f == 1,
                                  stop=f == F).then_inc(y_used, 1)

            @block.scalar
            def _(act):
                chain = Chain(act, end_chain)
                for f in range(F):
                    if f >= 2:
                        act.wait_ge(var_psum, f - 1)
                    act.activation(square[:, f % 2, :], outT[:, f, :], ACT.Square).then_inc(square_ready, 1)
                act.wait_ge(var_psum, F)
                chain.link(act.activation(rms[:, :, :], m.psum[:, 0:F, :], ACT.Ln, scale=1.0 / W, bias=w["eps"]))
                act.activation(rms[:, :, :], rms[:, :, :], ACT.Exp, scale=-0.5).then_inc(rms_ready, 1)
                for f in range(F):
                    act.wait_ge(gate_psum, f + 1)
                    if f >= 2:
                        act.wait_ge(y_ready, f - 1)
                    act.activation(gate[:, f % 2, :], m.bank(4 + f % 2), ACT.Silu).then_inc(gate_ready, 1)

            @block.vector
            def _(dve):
                dve.wait_ge(rms_ready, 1)
                for f in range(F):
                    dve.scalar_tensor_tensor(out=rms[:, f, :], in0=outT[:, f, :], scalar=w["norm_w"],
                                             in1=rms[:, f, :], op0=ALU.mult, op1=ALU.mult).then_inc(normed, 1)
                dve.wait_ge(normed, F)
                for f in range(F):
                    dve.wait_ge(gate_ready, f + 1)
                    if f >= 2:
                        dve.wait_ge(y_used, f - 1)
                    dve.tensor_tensor(y[:, f % 2, :], rms[:, f, :], gate[:, f % 2, :], ALU.mult).then_inc(y_ready, 1)
    return None


def stage_l0_attn(m):
    nc, w, name = m.nc, m.weights("l0_attn"), "l0_attn"
    HV, W, F, L = 16, 64, 4, 6
    C = 16
    ORDER = list(range(4, 8)) + list(range(4)) + list(range(8, 16))
    PAIRS = NT * F
    NEWTON = 12
    with ExitStack() as ctx:
        sb = lambda n, shape, dt=F32: ctx.enter_context(nc.sbuf_tensor(f"{name}_{n}", shape, dt))
        sem = lambda n: m.sem(f"{name}_{n}")
        v = sb("v", [P, NT, HV * W])
        mid = ExitStack()
        msb = lambda n, shape, dt=F32: mid.enter_context(nc.sbuf_tensor(f"{name}_{n}", shape, dt))
        qT = msb("qT", [P, F, T])
        kT = msb("kT", [P, F, T])
        k = msb("k", [P, NT, F * P])
        beta = msb("beta", [P, NT, HV])
        g_raw = msb("g_raw", [P, NT, HV])
        g_log = msb("g_log", [P, NT, HV])
        a_exp = msb("a_exp", [P, HV])
        g = msb("g", [P, NT, HV])
        e_g = msb("e_g", [P, NT, HV])
        e_end = msb("e_end", [P, NT, HV])
        e_tile = msb("e_tile", [P, NT, F, 2])
        pre = ExitStack()
        psb = lambda n, shape, dt=F32: pre.enter_context(nc.sbuf_tensor(f"{name}_{n}", shape, dt))
        xpad = psb("xpad", [P, 2, 3 + T])
        conv = psb("conv", [P, 2, T])
        vT = psb("vT", [P, 2, T])
        sq = psb("sq", [P, 2, T])
        norm2 = psb("norm2", [P, NT, HV])
        rs = psb("rs", [P, NT, HV])
        rs_tmp = psb("rs_tmp", [P, NT, HV])
        rsT = psb("rsT", [HV, T])

        in_psum = sem("in_psum")
        x_ready = sem("x_ready")
        conv_ready = sem("conv")
        silu_ready = sem("silu")
        v_turned = sem("v_turned")
        v_copied = sem("v_copied")
        gates_read = sem("gates_read")
        sq_ready = sem("sq")
        sq_psum = sem("sq_psum")
        rs_ready = sem("rs")
        rs_turned = sem("rs_turned")
        rsT_ready = sem("rsT")
        rs_spread = sem("rs_spread")
        qk_ready = sem("qk")
        k_turned = sem("k_turned")
        k_copied = sem("k_copied")
        gates_psum = sem("gates_psum")
        raw_ready = sem("raw")
        logged = sem("logged")
        g_ready = sem("g")
        g_psum = sem("g_psum")
        e_ready = sem("e")
        pre_chain, pre_act = sem("pre_chain"), sem("pre_act")
        tok = lambda t: slice(t * P, (t + 1) * P)

        with nc.Block(no_gpsimd_drain=True) as block:
            @block.tensor
            def _(pe):
                for t in range(NT):
                    ins = pe.matmul(m.psum[:, 6, 2 * HV * t:2 * HV * (t + 1)], m.xnT[:, tok(t)], w["ba"],
                                    start=True, stop=True)
                ins.then_inc(gates_psum, 1)

                def norms(i):
                    c = ORDER[i]
                    pe.wait_ge(sq_ready, i + 1)
                    if i == 0:
                        pe.wait_ge(gates_read, 1)
                    for t in range(NT):
                        ins = pe.matmul(m.psum[:, 6, HV * t + 2 * c:HV * t + 2 * c + 2], sq[:, i % 2, tok(t)],
                                        m.const["halves_rows"], start=True, stop=True)
                    ins.then_inc(sq_psum, 1)

                def turn_v(i):
                    pe.wait_ge(silu_ready, i + 9)
                    if i >= 2:
                        pe.wait_ge(v_copied, i - 1)
                    for t in range(NT):
                        ins = pe.transpose(m.psum[:, 2 + i % 2, tok(t)], vT[:, i % 2, tok(t)], m.ident)
                    ins.then_inc(v_turned, 1)

                def spread(i):
                    if i == 0:
                        pe.wait_ge(rs_ready, 1)
                        for t in range(NT):
                            ins = pe.transpose(m.psum[0:HV, 6, tok(t)], rs[:, t, :], m.ident)
                        ins.then_inc(rs_turned, 1)
                        pe.wait_ge(rsT_ready, 1)
                    if i >= 2:
                        pe.wait_ge(qk_ready, i - 1)
                    pe.matmul(m.bank(4 + i % 2), m.weights("l0_ffn")["spread"][:, ORDER[i], :], rsT[:, :],
                              start=True, stop=True).then_inc(rs_spread, 1)

                for n in range(C + 2):
                    if n < C:
                        if n >= 2:
                            pe.wait_ge(x_ready, n - 1)
                        pe.matmul(m.bank(n % 2), w["qkv"][:, ORDER[n], :], m.xnT[:, :], start=True,
                                  stop=True).then_inc(in_psum, 1)
                    if 2 <= n < 10:
                        norms(n - 2)
                    if 10 <= n < 18:
                        turn_v(n - 10)
                    if n >= NEWTON + 1:
                        spread(n - NEWTON - 1)
                for i in range(C + 1 - NEWTON, 2 * F):
                    spread(i)
                for f in range(F):
                    pe.wait_ge(qk_ready, f + 1)
                    if f >= 2:
                        pe.wait_ge(k_copied, f - 1)
                    else:
                        pe.wait_ge(v_copied, 7 + f)
                    for t in range(NT):
                        ins = pe.transpose(m.psum[:, 2 + f % 2, tok(t)], kT[:, f, tok(t)], m.ident)
                    ins.then_inc(k_turned, 1)
                pe.wait_ge(g_ready, 1)
                for n, lhsT in enumerate((m.const["upto"][:, 0:P], m.const["after"], m.const["ones"])):
                    ins = pe.matmul(m.psum[:, 7, NT * HV * n:NT * HV * (n + 1)], lhsT,
                                    g[:, :, :].rearrange("p t h -> p (t h)"), start=True, stop=True)
                ins.then_inc(g_psum, 1)

            @block.scalar
            def _(act):
                chain = Chain(act, pre_act)
                by_tile = lambda a: a.rearrange("p (t d) -> p t d", d=P)
                act.wait_ge(raw_ready, 1)
                act.activation(beta[:, :, :], m.psum[:, 6, 0:2 * HV * NT].rearrange("p (t h) -> p t h", h=2 * HV)[:, :, 0:HV],
                               ACT.Sigmoid).then_inc(gates_read, 1)
                chain.link(act.activation(g_log[:, :, :], g_raw[:, :, :], ACT.Abs))
                chain.link(act.activation(g_log[:, :, :], g_log[:, :, :], ACT.Sigmoid))
                for n in range(C + 4):
                    if n < C:
                        act.wait_ge(in_psum, n + 1)
                        if n >= 2:
                            act.wait_ge(conv_ready, n - 1)
                        act.activation(xpad[:, n % 2, 3:3 + T], m.bank(n % 2), ACT.Copy).then_inc(x_ready, 1)
                    if 1 <= n < C + 1:
                        c = ORDER[n - 1]
                        act.wait_ge(conv_ready, n)
                        if n - 1 >= 10:
                            act.wait_ge(v_turned, n - 10)
                        out = vT[:, (n - 1) % 2, :] if c >= 8 else (kT[:, c - F, :] if c >= F else qT[:, c, :])
                        act.activation(out, conv[:, (n - 1) % 2, :], ACT.Silu).then_inc(silu_ready, 1)
                    if n == NEWTON + 1:
                        act.wait_ge(rs_turned, 1)
                        act.activation(rsT[:, :], m.psum[0:HV, 6, :], ACT.Copy).then_inc(rsT_ready, 1)
                    if n >= 11 and n - 11 < 8:
                        i = n - 11
                        act.wait_ge(v_turned, i + 1)
                        act.activation(v[:, :, i * P:(i + 1) * P], by_tile(m.bank(2 + i % 2)),
                                       ACT.Copy).then_inc(v_copied, 1)
                act.activation(a_exp[:, :], w["a_log"], ACT.Exp)
                act.activation(g_log[:, :, :], g_log[:, :, :], ACT.Ln).then_inc(logged, 1)
                for f in range(F):
                    act.wait_ge(k_turned, f + 1)
                    act.activation(k[:, :, tok(f)], by_tile(m.bank(2 + f % 2)), ACT.Copy).then_inc(k_copied, 1)
                act.wait_ge(g_psum, 1)
                sums = lambda n: m.psum[:, 7, NT * HV * n:NT * HV * (n + 1)]
                act.activation(e_g[:, :, :], sums(0).rearrange("p (t h) -> p t h", h=HV), ACT.Exp)
                act.activation(e_end[:, :, :], sums(1).rearrange("p (t h) -> p t h", h=HV), ACT.Exp)
                for p in range(2):
                    rows = slice(W * p, W * p + W)
                    ins = act.activation(e_tile[rows, :, :, :],
                                         sums(2)[rows].rearrange("p (t f a i) -> p t f a i", t=NT, a=2, i=2)[:, :, :, p, :],
                                         ACT.Exp)
                ins.then_inc(e_ready, 1)

            @block.gpsimd
            def _(pool):
                for i in range(2 * F):
                    c = ORDER[i]
                    pool.wait_ge(silu_ready, i + 1)
                    if i >= 2:
                        pool.wait_ge(sq_psum, i - 1)
                    a = kT[:, c - F, :] if c >= F else qT[:, c, :]
                    pool.tensor_tensor(sq[:, i % 2, :], a, a, ALU.mult).then_inc(sq_ready, 1)

            @block.vector
            def _(dve):
                chain = Chain(dve, pre_chain)
                chain.link(dve.memset(xpad[:, :, 0:3], 0.0))
                dve.wait_ge(gates_psum, 1)
                products = m.psum[:, 6, 0:2 * HV * NT].rearrange("p (t h) -> p t h", h=2 * HV)
                over = lambda a: a.unsqueeze(1).to_broadcast([P, NT, HV])
                dve.tensor_tensor(g_raw[:, :, :], products[:, :, HV:2 * HV], over(w["dt_bias"]),
                                  ALU.add).then_inc(raw_ready, 1)

                def normalise(i):
                    c = ORDER[i]
                    a = kT[:, c - F, :] if c >= F else qT[:, c, :]
                    dve.wait_ge(rs_spread, i + 1)
                    dve.tensor_tensor(a, a, m.bank(4 + i % 2), ALU.mult).then_inc(qk_ready, 1)

                for n in range(C):
                    if n == NEWTON:
                        dve.wait_ge(sq_psum, 2 * F)
                        chain.link(dve.tensor_scalar(norm2[:, :, :],
                                                     m.psum[:, 6, 0:HV * NT].rearrange("p (t h) -> p t h", h=HV),
                                                     1e-6, None, ALU.add))
                        newton_rsqrt(dve, chain, norm2[:, :, :], rs[:, :, :], rs_tmp[:, :, :])
                        dve.tensor_scalar(rs[:, :, 0:2 * F], rs[:, :, 0:2 * F], W ** -0.5, None,
                                          ALU.mult).then_inc(rs_ready, 1)
                    dve.wait_ge(x_ready, n + 1)
                    if n >= 2:
                        dve.wait_ge(silu_ready, n - 1)
                    padded_conv(dve, chain, conv[:, n % 2, :], xpad[:, n % 2, :],
                                w["conv_w"][:, ORDER[n], :]).then_inc(conv_ready, 1)
                    if n > NEWTON:
                        normalise(n - NEWTON - 1)
                for i in range(C - NEWTON - 1, 2 * F):
                    normalise(i)
                dve.wait_ge(logged, 1)
                chain.link(dve.scalar_tensor_tensor(out=g[:, :, :], in0=g_raw[:, :, :], scalar=0.0,
                                                    in1=g_log[:, :, :], op0=ALU.max, op1=ALU.subtract))
                chain.link(dve.tensor_tensor(g[:, :, :], g[:, :, :], over(a_exp[:, :]), ALU.mult))
                dve.tensor_scalar(g[:, :, :], g[:, :, :], -1.0, None, ALU.mult).then_inc(g_ready, 1)
                dve.wait_ge(e_ready, 1)
                dve.wait_ge(g_ready, 1)
                dve.tensor_tensor(e_end[:, :, :], e_end[:, :, :], beta[:, :, :], ALU.mult)
        pre.close()

        gu = msb("gu", [P, 2, 2, P])
        decay = msb("decay", [P, 2, 2, P])
        ap = msb("ap", [P, 2, 2, 2, 2, P])
        part = msb("part", [P, 2, 2, 2, P])
        part0 = msb("part0", [P, 2, 2, P])
        xx = msb("xx", [P, 2, 2, 2, 2, P])
        ax = msb("ax", [P, 2, 2, P])
        state = msb("state", [P, F, 2, W])
        r = msb("r", [P, 2, 2, W])
        u_ = msb("u", [P, 2, 2, W])
        u_end = msb("u_end", [P, 2, 2, W])
        qs = msb("qs", [P, 2, 2, W])

        gu_ready = sem("gu")
        prep_psum = sem("prep")
        decay_ready = sem("decay")
        a_ready = sem("a")
        part0_ready = sem("part0")
        a_turned = sem("a_turned")
        x0_ready = sem("x0")
        part_ready = sem("part")
        ax_psum = sem("ax_psum")
        ax_ready = sem("ax")
        xx_psum = sem("xx_psum")
        xxT_psum = sem("xxT_psum")
        xl_ready = sem("xl")
        xlT_ready = sem("xlT")
        ks_psum = sem("ks")
        r_ready = sem("r")
        u_psum = sem("u_psum")
        u_ready = sem("u")
        u_end_ready = sem("u_end")
        pu_psum = sem("pu")
        o_ready = sem("o")
        add_psum = sem("add")
        state_ready = sem("state")
        chain_sem, act_chain = sem("chain"), sem("act_chain")

        def slots(n):
            fill = {1: [("ks", n - 1)], 2: [("u", n - 1)], 3: [("pu", n - 1)], 4: [("add", n - 1), ("prep", n + 1)],
                    5: [], L: [("turn", n + 1)]}
            for l in range(1, L + 1):
                yield l, [(kind, i) for kind, i in fill[l] if 0 <= i < PAIRS]

        def at(n, l, p):
            return 2 * (L * n + l - 1) + p + 1

        def at_x(n, l, p):
            return 2 * ((L - 1) * n + l - 1) + p + 1

        X, XT = 0, 1
        A, PM = 0, 1
        later = lambda n: 2 * (n - F)
        upto = m.const["upto"][:, 0:P]
        with nc.Block(no_gpsimd_drain=True) as block:
            @block.tensor
            def _(pe):
                def prep(n):
                    t, f = divmod(n, F)
                    for p in range(2):
                        rows = slice(W * p, W * p + W)
                        pe.wait_ge(gu_ready, 2 * n + p + 1)
                        if n >= 1:
                            pe.wait_ge(x0_ready, 2 * n + p - 1)
                        bank = m.bank(4 + p)
                        for i in range(2):
                            sums = bank[:, 256 + i * P:256 + (i + 1) * P]
                            pe.matmul(sums, m.const["after"], gu[:, p, i, :], start=True, stop=False)
                            pe.matmul(sums, m.later_bf[:, :], m.ident_bf[:, :], start=False, stop=True)
                        pe.matmul(bank[:, 0:P], kT[rows, f, tok(t)], kT[rows, f, tok(t)], start=True, stop=True)
                        pe.matmul(bank[:, P:2 * P], kT[rows, f, tok(t)], qT[rows, f, tok(t)], start=True,
                                  stop=True).then_inc(prep_psum, 1)

                def turn(n):
                    for p in range(2):
                        pe.wait_ge(part0_ready, 2 * n + p + 1)
                        for i in range(2):
                            ins = pe.transpose(m.psum[:, 4 + p, tok(i)], part0[:, p, i, :], m.ident)
                        ins.then_inc(a_turned, 1)

                def ks(n):
                    t, f = divmod(n, F)
                    for p in range(2 if t > 0 else 0):
                        rows = slice(W * p, W * p + W)
                        pe.wait_ge(state_ready, 2 * (n - F) + p + 1)
                        pe.wait_ge(o_ready, 2 * n + p - 1)
                        if n - 1 < PAIRS - F:
                            pe.wait_ge(state_ready, 2 * n + p - 1)
                        s = state[rows, f, :, :].rearrange("p i v -> p (i v)")
                        pe.matmul(m.psum[:, 6 + p, 0:P], kT[rows, f, tok(t)], s, start=True, stop=True)
                        pe.matmul(m.psum[:, 6 + p, P:2 * P], qT[rows, f, tok(t)], s, start=True,
                                  stop=True).then_inc(ks_psum, 1)

                def corrected(n):
                    t, f = divmod(n, F)
                    for p in range(2):
                        pe.wait_ge(xlT_ready, at(n, L, p))
                        if t > 0:
                            pe.wait_ge(r_ready, later(n) + p + 1)
                        elif n >= 1:
                            pe.wait_ge(o_ready, 2 * n + p - 1)
                        for i in range(2):
                            h = 4 * f + 2 * p + i
                            rhs = v[:, t, W * h:W * h + W] if t == 0 else r[:, p, i, :]
                            ins = pe.matmul(m.psum[:, 6 + p, 256 + W * i:256 + W * i + W],
                                            xx[:, n % 2, p, XT, i, :], rhs, start=True, stop=True)
                        ins.then_inc(u_psum, 1)

                def output(n):
                    for p in range(2):
                        pe.wait_ge(u_ready, 2 * n + p + 1)
                        for i in range(2):
                            ins = pe.matmul(m.psum[:, 6 + p, 384 + W * i:384 + W * i + W], ap[:, n % 2, p, PM, i, :],
                                            u_[:, p, i, :], start=True, stop=True)
                        ins.then_inc(pu_psum, 1)

                def add(n):
                    t, f = divmod(n, F)
                    for p in range(2 if t < NT - 1 else 0):
                        j = 2 * f + p
                        pe.wait_ge(u_end_ready, 2 * n + p + 1)
                        pe.wait_ge(o_ready, 2 * n + p + 1)
                        pe.matmul(m.psum[W * p:W * p + W, 6 + p, 0:P], k[:, t, W * j:W * j + W],
                                  u_end[:, p, :, :].rearrange("p i v -> p (i v)"), start=True,
                                  stop=True).then_inc(add_psum, 1)

                fill = {"prep": prep, "turn": turn, "ks": ks, "u": corrected, "pu": output, "add": add}
                prep(0)
                turn(0)
                for n in range(PAIRS + 1):
                    s = n % 2
                    for l, work in slots(n):
                        if n < PAIRS:
                            for p in range(2):
                                if l == 1:
                                    pe.wait_ge(x0_ready, 2 * n + p + 1)
                                else:
                                    pe.wait_ge(xl_ready, at_x(n, l - 1, p))
                                pe.wait_ge(part_ready, at(n, l, p))
                                if n + l > 1:
                                    pe.wait_ge(xlT_ready, at(n, l, p) - 2)
                                for i in range(2):
                                    ins = pe.matmul(m.psum[:, p, tok(i)], part[:, l % 2, p, i, :],
                                                    xx[:, s, p, X, i, :], start=True, stop=True)
                                ins.then_inc(ax_psum, 1)
                        for kind, i in work:
                            fill[kind](i)
                        if n < PAIRS:
                            for p in range(2):
                                pe.wait_ge(ax_ready, at(n, l, p))
                                if l < L:
                                    for i in range(2):
                                        ins = pe.matmul(m.psum[:, 2 + p, tok(i)], xx[:, s, p, XT, i, :],
                                                        ax[:, p, i, :], start=True, stop=True)
                                    ins.then_inc(xx_psum, 1)
                                for i in range(2):
                                    ins = pe.matmul(m.psum[:, p, tok(2 + i)], ax[:, p, i, :],
                                                    xx[:, s, p, XT, i, :], start=True, stop=True)
                                ins.then_inc(xxT_psum, 1)

            @block.scalar
            def _(act):
                chain = Chain(act, act_chain)

                def prep(n):
                    t, f = divmod(n, F)
                    for p in range(2):
                        u = 2 * n + p
                        act.wait_ge(prep_psum, u + 1)
                        if n >= 1:
                            act.wait_ge(a_ready, u - 1)
                        chain.link(act.activation(decay[:, p, :, :],
                                                  m.psum[:, 4 + p, 256:512].rearrange("p (i t) -> p i t", i=2),
                                                  ACT.Exp))
                        for i in range(2):
                            h = 4 * f + 2 * p + i
                            ins = act.activation(decay[:, p, i, :], decay[:, p, i, :], ACT.Copy,
                                                 scale=beta[:, t, h:h + 1])
                        ins.then_inc(decay_ready, 1)

                def corrected(n):
                    for p in range(2):
                        act.wait_ge(u_psum, 2 * n + p + 1)
                        if n >= 1:
                            act.wait_ge(pu_psum, 2 * n + p - 1)
                            if n - 1 < PAIRS - F:
                                act.wait_ge(u_end_ready, 2 * n + p - 1)
                        act.activation(u_[:, p, :, :], m.psum[:, 6 + p, 256:384].rearrange("p (i v) -> p i v", i=2),
                                       ACT.Copy).then_inc(u_ready, 1)

                fill = {"prep": prep, "u": corrected}
                prep(0)
                for n in range(PAIRS + 1):
                    for l, work in slots(n):
                        if n < PAIRS:
                            for p in range(2):
                                act.wait_ge(ax_psum, at(n, l, p))
                                if n + l > 1:
                                    act.wait_ge(xxT_psum, at(n, l, p) - 2)
                                act.activation(ax[:, p, :, :], m.psum[:, p, 0:256].rearrange("p (i t) -> p i t", i=2),
                                               ACT.Copy).then_inc(ax_ready, 1)
                        for kind, i in work:
                            if kind in fill:
                                fill[kind](i)

            @block.gpsimd
            def _(pool):
                over = lambda a: a.unsqueeze(1).to_broadcast([P, 2, P])

                def sums(n):
                    t, f = divmod(n, F)
                    for p in range(2):
                        u = 2 * n + p
                        if n >= 1:
                            pool.wait_ge(prep_psum, u - 1)
                        of = g[:, t, 4 * f + 2 * p:4 * f + 2 * p + 2].unsqueeze(2).to_broadcast([P, 2, P])
                        pool.tensor_tensor(gu[:, p, :, :], over(upto), of, ALU.mult).then_inc(gu_ready, 1)

                sums(0)
                for n in range(PAIRS):
                    for l, work in slots(n):
                        for p in range(2):
                            if l == 1:
                                pool.wait_ge(a_ready, 2 * n + p + 1)
                            if 2 * (L * n + l) > 4:
                                pool.wait_ge(ax_psum, at(n, l, p) - 4)
                            pool.tensor_tensor(part[:, l % 2, p, :, :], ap[:, n % 2, p, A, :, :],
                                               over(w["levels"][:, l, :]), ALU.mult).then_inc(part_ready, 1)
                        if l == 1 and n + 1 < PAIRS:
                            sums(n + 1)

            @block.vector
            def _(dve):
                chain = Chain(dve, chain_sem)
                heads = lambda a: a.rearrange("p (i v) -> p i v", i=2)
                over = lambda a: a.unsqueeze(2).to_broadcast([P, 2, W])

                def prep(n):
                    t, f = divmod(n, F)
                    for p in range(2):
                        u = 2 * n + p
                        dve.wait_ge(decay_ready, u + 1)
                        if n >= 2:
                            dve.wait_ge(pu_psum, u - 3)
                            dve.wait_ge(part_ready, at(n - 2, L, p))
                        dve.tensor_tensor(ap[:, n % 2, p, :, :, :],
                                          decay[:, p, :, :].unsqueeze(1).to_broadcast([P, 2, 2, P]),
                                          m.psum[:, 4 + p, 0:256].rearrange("p (a t) -> p a t", a=2).unsqueeze(2)
                                          .to_broadcast([P, 2, 2, P]), ALU.mult).then_inc(a_ready, 1)
                        dve.wait_ge(a_ready, u + 1)
                        dve.tensor_tensor(part0[:, p, :, :], ap[:, n % 2, p, A, :, :],
                                          w["levels"][:, 0, :].unsqueeze(1).to_broadcast([P, 2, P]),
                                          ALU.mult).then_inc(part0_ready, 1)

                def turn(n):
                    for p in range(2):
                        u = 2 * n + p
                        if n >= 2:
                            dve.wait_ge(u_psum, u - 3)
                        dve.wait_ge(part0_ready, u + 1)
                        one = m.ident.unsqueeze(1).to_broadcast([P, 2, P])
                        dve.tensor_tensor(xx[:, n % 2, p, XT, :, :], one, part0[:, p, :, :], ALU.subtract)
                        dve.wait_ge(a_turned, u + 1)
                        dve.tensor_tensor(xx[:, n % 2, p, X, :, :], one,
                                          m.psum[:, 4 + p, 0:256].rearrange("p (i t) -> p i t", i=2),
                                          ALU.subtract).then_inc(x0_ready, 1)

                def ks(n):
                    t, f = divmod(n, F)
                    for p in range(2 if t > 0 else 0):
                        h = 4 * f + 2 * p
                        dve.wait_ge(ks_psum, later(n) + p + 1)
                        dve.tensor_tensor(qs[:, p, :, :], heads(m.psum[:, 6 + p, P:2 * P]), over(e_g[:, t, h:h + 2]),
                                          ALU.mult)
                        chain.link(dve.tensor_tensor(r[:, p, :, :], heads(m.psum[:, 6 + p, 0:P]),
                                                     over(e_g[:, t, h:h + 2]), ALU.mult))
                        dve.tensor_tensor(r[:, p, :, :], heads(v[:, t, W * h:W * h + 2 * W]), r[:, p, :, :],
                                          ALU.subtract).then_inc(r_ready, 1)

                def corrected(n):
                    t, f = divmod(n, F)
                    for p in range(2 if t < NT - 1 else 0):
                        h = 4 * f + 2 * p
                        dve.wait_ge(u_ready, 2 * n + p + 1)
                        if n >= 1:
                            dve.wait_ge(add_psum, 2 * n + p - 1)
                        dve.tensor_tensor(u_end[:, p, :, :], u_[:, p, :, :],
                                          over(e_end[:, t, h:h + 2]), ALU.mult).then_inc(u_end_ready, 1)

                def output(n):
                    t, f = divmod(n, F)
                    for p in range(2):
                        h = 4 * f + 2 * p
                        dve.wait_ge(pu_psum, 2 * n + p + 1)
                        o = heads(v[:, t, W * h:W * h + 2 * W])
                        pu = heads(m.psum[:, 6 + p, 384:512])
                        if t == 0:
                            ins = dve.tensor_copy(o, pu)
                        else:
                            dve.wait_ge(r_ready, later(n) + p + 1)
                            ins = dve.tensor_tensor(o, qs[:, p, :, :], pu, ALU.add)
                        ins.then_inc(o_ready, 1)

                def add(n):
                    t, f = divmod(n, F)
                    for p in range(2 if t < NT - 1 else 0):
                        rows = slice(W * p, W * p + W)
                        dve.wait_ge(add_psum, 2 * n + p + 1)
                        if t > 0:
                            dve.wait_ge(state_ready, 2 * (n - F) + p + 1)
                        s = state[rows, f, :, :]
                        for i in range(2):
                            new = m.psum[rows, 6 + p, W * i:W * i + W]
                            if t == 0:
                                ins = dve.tensor_copy(s[:, i, :], new)
                            else:
                                ins = dve.scalar_tensor_tensor(out=s[:, i, :], in0=s[:, i, :],
                                                               scalar=e_tile[rows, t, f, i:i + 1], in1=new,
                                                               op0=ALU.mult, op1=ALU.add)
                        ins.then_inc(state_ready, 1)

                fill = {"prep": prep, "turn": turn, "ks": ks, "u": corrected, "pu": output, "add": add}
                prep(0)
                turn(0)
                for n in range(PAIRS + 1):
                    for l, work in slots(n):
                        for kind, i in work:
                            if kind != "prep":
                                fill[kind](i)
                        if n < PAIRS:
                            for p in range(2):
                                def subtract(which, psum, psum_ready, count, ready):
                                    dve.wait_ge(psum_ready, count)
                                    if l == 1:
                                        dve.wait_ge(x0_ready, 2 * n + p + 1)
                                    else:
                                        dve.wait_ge(ready, count - 2)
                                    dst = xx[:, n % 2, p, which, :, :].rearrange("p i t -> p (i t)")
                                    dve.tensor_tensor(dst, dst, psum, ALU.subtract).then_inc(ready, 1)

                                if l < L:
                                    subtract(X, m.psum[:, 2 + p, 0:256], xx_psum, at_x(n, l, p), xl_ready)
                                subtract(XT, m.psum[:, p, 256:512], xxT_psum, at(n, l, p), xlT_ready)
                        for kind, i in work:
                            if kind == "prep":
                                fill[kind](i)
        mid.close()

        z = sb("z", [P, 2, HV * W])
        square = sb("square", [P, 2, HV * W])
        var = sb("var", [P, NT * HV])
        rms = sb("rms", [P, NT * HV])
        tmp = sb("tmp", [P, NT * HV])
        yT = sb("yT", [P, 8, T])
        z_psum = sem("z_psum")
        z_ready = sem("z")
        square_ready = sem("square")
        y_ready = sem("y")
        y_turned = sem("y_turned")
        yT_ready = sem("yT")
        end_chain = sem("end_chain")
        with nc.Block(no_gpsimd_drain=True) as block:
            @block.tensor
            def _(pe):
                for n in range(2 * NT):
                    t, half = divmod(n, 2)
                    if n >= 2:
                        pe.wait_ge(z_ready, n - 1)
                    pe.matmul(m.bank(n % 2), m.xnT[:, tok(t)], w["z"][:, 512 * half:512 * half + 512], start=True,
                              stop=True).then_inc(z_psum, 1)
                for n in range(2 * NT):
                    t, half = divmod(n, 2)
                    pe.wait_ge(y_ready, t + 1)
                    if n >= 2:
                        pe.wait_ge(yT_ready, n - 1)
                    for c in range(4):
                        ins = pe.transpose(m.psum[:, 2 + n % 2, tok(c)], v[:, t, tok(4 * half + c)], m.ident)
                    ins.then_inc(y_turned, 1)
                pe.wait_ge(yT_ready, 2 * NT)
                for c in range(8):
                    pe.matmul(m.bank(OUT), w["out"][:, c, :], yT[:, c, :], start=c == 0, stop=c == 7)

            @block.scalar
            def _(act):
                for n in range(2 * NT):
                    t, half = divmod(n, 2)
                    act.wait_ge(z_psum, n + 1)
                    if t >= 2:
                        act.wait_ge(y_ready, t - 1)
                    act.activation(z[:, t % 2, 512 * half:512 * half + 512], m.bank(n % 2),
                                   ACT.Silu).then_inc(z_ready, 1)
                for n in range(2 * NT):
                    t, half = divmod(n, 2)
                    act.wait_ge(y_turned, n + 1)
                    act.activation(yT[:, 4 * half:4 * half + 4, tok(t)],
                                   m.bank(2 + n % 2).rearrange("p (c s) -> p c s", s=P), ACT.Copy,
                                   scale=w["norm_w"]).then_inc(yT_ready, 1)

            @block.gpsimd
            def _(pool):
                for t in range(NT):
                    if t >= 2:
                        pool.wait_ge(end_chain, t - 1)
                    pool.tensor_tensor(square[:, t % 2, :], v[:, t, :], v[:, t, :], ALU.mult).then_inc(square_ready, 1)

            @block.vector
            def _(dve):
                chain = Chain(dve, end_chain)
                for t in range(NT):
                    dve.wait_ge(square_ready, t + 1)
                    chain.link(dve.tensor_reduce(var[:, HV * t:HV * t + HV],
                                                 square[:, t % 2, :].rearrange("p (h v) -> p h v", v=W), AX, ALU.add))
                chain.link(dve.tensor_scalar(var[:, :], var[:, :], 1.0 / W, 1e-6, ALU.mult, ALU.add))
                newton_rsqrt(dve, chain, var[:, :], rms[:, :], tmp[:, :])
                for t in range(NT):
                    o = v[:, t, :].rearrange("p (h v) -> p h v", v=W)
                    chain.link(dve.tensor_tensor(o, o, rms[:, HV * t:HV * t + HV].unsqueeze(2).to_broadcast([P, HV, W]),
                                                 ALU.mult))
                    dve.wait_ge(z_ready, 2 * t + 2)
                    dve.tensor_tensor(v[:, t, :], v[:, t, :], z[:, t % 2, :], ALU.mult).then_inc(y_ready, 1)
    return None


def stage_l0_ffn(m):
    w = m.weights("l0_ffn")
    experts_stage(m, "l0_ffn", w, 16, 64, route_grouped(m, m.const["lower16"], m.const["lower4"], w["bias"]), True)


def stage_l1_ffn(m):
    experts_stage(m, "l1_ffn", m.weights("l1_ffn"), 8, 352, route_top1(m, m.const["lower8"]), False)


def stage_l3_ffn(m):
    experts_stage(m, "l3_ffn", m.weights("l3_ffn"), 8, 256, route_top1(m, m.const["lower8"]), False)


RINGS = [{5: "l1_ffn", 8: "l2_ffn", 11: "l3_ffn"}, {0: "l0_attn", 7: "l2_xattn", 10: "l3_xattn"}]
SUBLAYERS = [stage_l0_attn, stage_l0_xattn, stage_l0_ffn, stage_l1_attn, stage_l1_xattn, stage_l1_ffn,
             stage_l2_attn, stage_l2_xattn, stage_l2_ffn, stage_l3_attn, stage_l3_xattn, stage_l3_ffn]


def program(nc, x_in, context, context_mask, x_out, packed, places):
    with ExitStack() as ctx:
        resident = ctx.enter_context(nc.semaphore("resident_weights"))
        m = Core(nc, ctx)
        rings = [{k: n for k, n in ring.items() if k in STAGES} for ring in RINGS]
        rings = [ring for ring in rings if ring]
        streamed_names = [n for ring in rings for n in ring.values()]
        absent = [n for ring in RINGS for n in ring.values() if n not in streamed_names]
        kept = [n for n in packed if n not in streamed_names + absent]
        home = {n: m.sb(f"w_{n}", list(packed[n].shape)) for n in kept}
        for r, ring in enumerate(rings):
            buffer = m.sb(f"streamed_weights{r}", [P, max(packed[n].shape[1] for n in ring.values())])
            home.update({n: buffer for n in ring.values()})

        def weights(n):
            out = {}
            for key, (c, s) in places[n].items():
                v = home[n][0:s[0], c:c + int(np.prod(s[1:]))]
                if len(s) == 3:
                    v = v.rearrange("p (a b) -> p a b", b=s[2])
                if len(s) == 4:
                    v = v.rearrange("p (a b c) -> p a b c", b=s[2], c=s[3])
                out[key] = v
            return out

        m.weights = weights
        m.const = weights("const")
        m.ident = m.const["ident"]
        x_loaded, x_stored = m.pass_sem("x_loaded"), m.pass_sem("x_stored")
        arrived = {n: ctx.enter_context(nc.semaphore(f"arrived_{n}")) for n in streamed_names}
        ctx_rows = m.sb("ctx_rows", [S2, D])
        mask_rows = m.sb("mask_rows", [S2, 1], U8)
        ctx_loaded, ctx_turned = m.pass_sem("ctx_loaded"), m.pass_sem("ctx_turned")
        norm = m.norm = Norm(m)
        ahead = [ring[0] for ring in rings if 0 in ring]
        with_pass = [next(iter(ring.values())) for ring in rings if 0 not in ring]

        def load(sync, n):
            width = packed[n].shape[1]
            return sync.dma_start(home[n][:, 0:width], packed[n])

        with nc.Block(no_gpsimd_drain=True) as block:
            @block.sync
            def _(sync):
                for n in kept:
                    load(sync, n).then_inc(resident, 16)
                for n in ahead:
                    load(sync, n).then_inc(arrived[n], 16)
                sync.wait_ge(resident, 16 * len(kept))

            @block.vector
            def _(dve):
                dve.wait_ge(resident, 16 * len(kept))
                dve.tensor_copy(m.ident_bf[:, :], m.ident)
                dve.tensor_copy(m.later_bf[:, :], m.const["later"])

        with nc.Fori(0, B) as b:
            rows = lambda a: a[bass.ds(b, 1), :, :].rearrange("a (t p) d -> p (a t) d", p=P)
            m.context = context[bass.ds(b, 1), :, :].rearrange("a s d -> (a s) d")
            m.context_mask = context_mask[bass.ds(b, 1), :, :].rearrange("a s d -> (a s) d")
            with nc.Block(no_gpsimd_drain=True) as block:
                @block.sync
                def _(sync):
                    sync.dma_start(m.x[:, :, :], rows(x_in)).then_inc(x_loaded, 16)
                    sync.dma_start(ctx_rows[:, :], m.context).then_inc(ctx_loaded, 16)
                    sync.dma_start(mask_rows[:, :], m.context_mask).then_inc(ctx_loaded, 16)
                    sync.wait_ge(x_loaded, 16)
                    sync.wait_ge(ctx_loaded, 32)
                    for n in with_pass:
                        load(sync, n).then_inc(arrived[n], 16)

                @block.tensor
                def _(pe):
                    pe.wait_ge(ctx_loaded, 32)
                    pe.transpose(m.psum[:, 0, 0:S2], ctx_rows[:, :], m.ident[0:S2, 0:S2]).then_inc(ctx_turned, 1)

                @block.vector
                def _(dve):
                    dve.wait_ge(ctx_loaded, 32)
                    dve.tensor_scalar(m.bound[:, :], mask_rows[:, :], 80.0, -40.0, ALU.mult, ALU.add)
                    dve.wait_ge(ctx_turned, 1)
                    dve.tensor_copy(m.ctxT[:, :], m.psum[:, 0, 0:S2])

            bias, add = None, False
            for k in STAGES:
                norm.block(add=add, bias=bias)
                if k == 11:
                    w = m.weights("columns")
                    norm.block(add=False, src=m.xn, keep=True, scale=w["l3_scale"], shift=w["l3_shift"])
                for r, ring in enumerate(rings):
                    if k in ring:
                        with nc.Block(no_gpsimd_drain=True) as block:
                            @block.sync
                            def _(sync):
                                sync.wait_ge(arrived[ring[k]], 16)
                                sync.sem_clear(range(arrived[ring[k]].num, arrived[ring[k]].num + 1))
                bias = SUBLAYERS[k](m)
                add = True
                for r, ring in enumerate(rings):
                    if k in ring and (k != list(ring)[-1] or 0 in ring):
                        following = list(ring.values())[(list(ring).index(k) + 1) % len(ring)]
                        with nc.Block(no_gpsimd_drain=True) as block:
                            @block.sync
                            def _(sync):
                                load(sync, following).then_inc(arrived[following], 16)
                                if k == 5:
                                    m.end_half(sync)
            norm.block(add=True, bias=bias, norm=False)
            with nc.Block(no_gpsimd_drain=True) as block:
                @block.sync
                def _(sync):
                    sync.dma_start(rows(x_out), m.x[:, :, :]).then_inc(x_stored, 16)
                    sync.wait_ge(x_stored, 16)
                    m.end_half(sync)
                    m.clear(sync, m.pass_sems)

        with nc.Block(no_gpsimd_drain=True) as block:
            @block.sync
            def _(sync):
                for n in ahead:
                    sync.wait_ge(arrived[n], 16)


def pack(parts):
    at, columns = {}, 0
    for key, a in parts:
        at[key] = (columns, a.shape)
        columns += int(np.prod(a.shape[1:]))
    packed = np.zeros((P, columns), np.float32)
    for key, a in parts:
        c, s = at[key]
        packed[:s[0], c:c + int(np.prod(s[1:]))] = a.reshape(s[0], -1)
    return packed, at


def constants():
    i = np.arange(P)
    lower = lambda n: np.broadcast_to(np.tril(np.ones((n, n)), -1), (P, n, n)).astype(np.float32)
    spread = lambda e, rows: np.stack([np.repeat(np.eye(e, dtype=np.float32)[:, g * (P // rows):(g + 1) * (P // rows)], rows, axis=1)
                                       for g in range(e * rows // P)], axis=1)
    halves = np.zeros((P, 2, P))
    halves[:, 0, :P // 2] = halves[:, 1, P // 2:] = 1
    rotate = np.zeros((P, P))
    rotate[i[1::2], i[0::2]] = -1
    rotate[i[0::2], i[1::2]] = 1
    inv_freq = (1.0 / np.float32(10000.0) ** (np.arange(0, 32, 2, dtype=np.float32) / 32)).astype(np.float32)
    angle = np.outer(inv_freq[(i % 32) // 2], np.arange(T, dtype=np.float32)).astype(np.float32)
    k, n = np.arange(T // 2), np.arange(T)
    wave = 2 * np.pi * np.outer(n, k) / T
    nyquist = (-1.0) ** n
    real, imag = np.cos(wave), -np.sin(wave)
    imag2, real2 = imag.copy(), real.copy()
    imag2[:, 0] = real2[:, 0] = nyquist
    forward = np.concatenate([real, imag2], axis=1).reshape(NT, P, T).transpose(1, 0, 2)
    weight = np.where(k == 0, 1.0, 2.0)[:, None] / T
    back_re, back_im = weight * real.T, weight * imag.T
    back_im[0] = nyquist / T
    inverse = np.concatenate([back_re, back_im]).reshape(4, P, T).transpose(1, 0, 2)
    row, col = i[:, None], i[None, :]
    levels = np.stack([(row >> l + 1 == col >> l + 1) & (row >> l < col >> l) for l in range(7)], axis=1)
    fold = lambda a: a[:P].reshape(P, 2, P)
    waves = [("forward", forward), ("inverse", inverse), ("kernel_re", fold(real)), ("kernel_re2", fold(real2)),
             ("kernel_im", fold(imag))]
    in_half = (i < P // 2).astype(float)
    parts = [("centred", (i[:, None] <= i[None, :]) - in_half[:, None]),
             ("half_all", np.stack([in_half, np.ones(P)], axis=1)), ("blocks", i[:, None] // 64 == i[None, :] // 64),
             ("after", i[:, None] > i[None, :]), ("ones", np.ones((P, P))),
             ("upto", np.arange(T)[None, :] >= i[:, None]), ("later", np.where(i[None, :] > i[:, None], -1e30, 0.0)), ("halves", halves), ("rotate", rotate), ("levels", levels),
             ("halves_rows", i[:, None] // 64 == np.arange(2)), ("quadrant", i[:, None] // 32 == np.arange(4)),
             ("head_rows", i[:, None] // 8 == np.arange(16)), ("cos", np.cos(angle)), ("sin", np.sin(angle)),
             ("ident", np.eye(P)), ("lower16", lower(16)), ("lower8", lower(8)), ("lower4", lower(4)),
             ("spread8", spread(8, P)), ("spread16", spread(16, 64))] + waves
    return [(k, np.asarray(a, np.float32)) for k, a in parts]


def tiles_of(a, rows=P):
    n = -(-a.shape[0] // rows)
    out = np.zeros((P, n, a.shape[1]), np.float32)
    for t in range(n):
        part = a[t * rows:(t + 1) * rows]
        out[:part.shape[0], t] = part
    return out


def experts_pack(spread, router, up, gate, down, s_up, s_gate, s_down, group):
    flat = lambda a, s: np.concatenate([a.transpose(1, 0, 2).reshape(D, -1), s], axis=1)
    if group:
        downs = np.concatenate([tiles_of(s_down), tiles_of(down.reshape(-1, D))], axis=1)
    else:
        downs = np.concatenate([tiles_of(s_down)] + [tiles_of(d) for d in down], axis=1)
    return [("router", router), ("up", flat(up, s_up)), ("gate", flat(gate, s_gate)), ("down", downs),
            ("spread", spread)]


def lay_out(i):
    rep = lambda a: np.broadcast_to(a[None, :], (P, a.shape[0]))
    const = dict(constants())
    packs = {"const": [(k, a) for k, a in const.items() if k not in OWN]}
    for l, build in PACKS.items():
        packs[l] = build(i, const)
    return packs


def pack_l0_ffn(i, const):
    w1, w3 = (i[f"L0_ffn_{n}"].transpose(0, 2, 1) for n in ("w1", "w3"))
    return experts_pack(const["spread16"], i["L0_ffn_gate_w"].T, w1, w3, i["L0_ffn_w2"].transpose(0, 2, 1),
                        i["L0_ffn_ws1"].T, i["L0_ffn_ws3"].T, i["L0_ffn_ws2"].T, True) + [
        ("bias", np.broadcast_to(i["L0_ffn_gate_bias"][None], (P, 16)))]


def pack_l1_ffn(i, const):
    g = lambda n: i[f"L1_ffn_{n}"]
    return experts_pack(const["spread8"], g("router_DE"), g("w1_eDF"), g("w3_eDF"), g("w2_eFD"),
                        g("ws1_DF"), g("ws3_DF"), g("ws2_FD"), False)


def pack_l3_ffn(i, const):
    g = lambda n: i[f"L3_ffn_{n}"]
    return experts_pack(const["spread8"], g("router_w"), g("gate_w"), g("up_w"), g("down_w"),
                        g("sh_gate"), g("sh_up"), g("sh_down"), False)


def pack_columns(i, const):
    return [("l3_scale", i["L3_ffn_ln_w"][:, None]), ("l3_shift", i["L3_ffn_ln_b"][:, None]),
            ("l2_xattn_bo", i["L2_xattn_bo"][:, None])]


def pack_xattn(prefix):
    def build(i, const):
        g = lambda n: i[f"{prefix}_{n}"]
        return [("wq", g("Wq").T), ("wk", g("Wk").T), ("wv", g("Wv").T), ("wo", g("Wo").T),
                ("bq", g("bq")[:, None]), ("bk", g("bk")[:, None]), ("bo", g("bo")[:, None]),
                ("bv", np.broadcast_to(g("bv")[None], (S2, D)))]
    return build


def pack_l1_attn(i, const):
    g = lambda n: i[f"L1_attn_{n}"]

    def into_latent(w):
        out = np.zeros((P, 4, P), np.float32)
        for h in range(16):
            out[8 * h:8 * h + 8, h // 4, 32 * (h % 4):32 * (h % 4) + 32] = w.T
        return out

    wqk = np.zeros((P, P), np.float32)
    for r in range(4):
        wqk[32 * r:32 * r + 32, 32 * r:32 * r + 32] = g("wqk_w").T
    l2o = np.zeros((P, 4, P), np.float32)
    for h in range(16):
        l2o[32 * (h % 4):32 * (h % 4) + 32, h // 4, 8 * h:8 * h + 8] = g("l2o_w").T
    col = lambda a, n: np.tile(a, n)[:, None]
    return [("qkv", g("c_attn_w").T.reshape(P, 3, P)), ("qkv_b", g("c_attn_b").reshape(3, P).T),
            ("q2l", into_latent(g("q2l_w"))), ("kv2l", into_latent(g("kv2l_w"))),
            ("q2l_b", col(g("q2l_b"), 4)), ("kv2l_b", col(g("kv2l_b"), 4)),
            ("v_b", np.broadcast_to(g("kv2l_b")[None], (P, 32))), ("wqk", wqk), ("wqk_b", col(g("wqk_b"), 4)),
            ("l2o", l2o), ("l2o_b", col(g("l2o_b"), 16)), ("cproj", g("cproj_w").T),
            ("cproj_b", g("cproj_b")[:, None])]


def pack_l2_attn(i, const):
    g = lambda n: i[f"L2_attn_{n}"]
    col = lambda a: np.tile(a, 16)[:, None]
    return [("qkv", np.stack([g("Wq").T, g("Wk").T, g("Wv").T], axis=1)), ("wo", g("Wo").T),
            ("bo", g("bo")[:, None]), ("q_g", col(g("qln_g"))), ("q_b", col(g("qln_b"))),
            ("k_g", col(g("kln_g"))), ("k_b", col(g("kln_b")))]


def pack_l2_xattn(i, const):
    g = lambda n: i[f"L2_xattn_{n}"]
    return [("wq", g("Wq").reshape(P, 8, P)), ("wk", g("Wkv")[:, :1024].reshape(P, 8, P)),
            ("wv", g("Wkv")[:, 1024:].reshape(P, 2, 512)), ("wo", tiles_of(g("Wo")))]


def pack_l3_attn(i, const):
    g = lambda n: i[f"L3_attn_{n}"]
    ssm = g("W_ssm")
    by_row = lambda a: a.reshape(2, P, -1).transpose(1, 0, 2)
    return [("w_in", g("W_in").T.reshape(P, 4, P)), ("w_dt", by_row(ssm[0:2].T)), ("w_b", by_row(ssm[2:130].T)),
            ("w_c", by_row(ssm[130:258].T)), ("w_out", by_row(g("W_out").T)),
            ("conv_w", by_row(g("conv_w").reshape(256, 4))), ("conv_b", g("conv_b").reshape(2, P).T),
            ("dt_bias", np.broadcast_to(g("dt_bias")[None], (P, 2))),
            ("a_log", np.broadcast_to(g("A_log")[None], (P, 2))),
            ("d_skip", np.broadcast_to(g("D_skip")[None], (P, 2)))]


def pack_l3_xattn(i, const):
    g = lambda n: i[f"L3_xattn_{n}"]
    return [("taps", g("weight").T), ("kp_w", g("kp_w").T), ("kp_b", g("kp_b")[:, None])] + [
        (k, const[k]) for k in ("forward", "inverse", "kernel_re", "kernel_re2", "kernel_im")]


def pack_l2_ffn(i, const):
    g = lambda n: i[f"L2_ffn_{n}"]
    low_b, up_b, one = (np.zeros(s, np.float32) for s in ((P, P), (P, 512), (P, 1)))
    for row, a, b, bias in ((0, "Wga", "Wgb", None), (64, "Wg1a", "Wg1b", "bg1"), (96, "Wg2a", "Wg2b", "bg2")):
        rank = g(a).shape[1]
        low_b[:, row:row + rank] = g(a)
        up_b[row:row + rank] = g(b)
        if bias:
            up_b[row + rank] = g(bias)
            one[row + rank] = 1.0
    return [("low_a", np.concatenate([g("Wqa"), g("Wka")], axis=1)), ("low_b", low_b), ("one_rows", one),
            ("up_a", np.concatenate([g("Wqb"), g("Wkb")])), ("up_b", up_b), ("wq", g("Wq")), ("wk", g("Wk")),
            ("wv", g("Wv")), ("router", g("We")), ("wo", tiles_of(g("Wo"))), ("eps", np.full((P, 1), 1e-5, np.float32)),
            ("norm_w", np.tile(g("norm_w"), 2)[:, None])]


def pack_l0_attn(i, const):
    g = lambda n: i[f"L0_attn_{n}"]
    rep = lambda a: np.broadcast_to(a[None], (P, a.shape[0]))
    return [("qkv", g("W_qkv").reshape(P, 16, P)), ("z", g("W_z")), ("ba", np.concatenate([g("W_b"), g("W_a")], axis=1)),
            ("dt_bias", rep(g("dt_bias"))), ("a_log", rep(g("A_log"))), ("conv_w", tiles_of(g("conv_w"))),
            ("norm_w", np.tile(g("norm_w"), 2)[:, None]), ("out", tiles_of(g("W_out"))),
            ("levels", const["levels"])]


OWN = ("levels", "spread8", "spread16", "forward", "inverse", "kernel_re", "kernel_re2", "kernel_im")
PACKS = {"l0_attn": pack_l0_attn, "l2_ffn": pack_l2_ffn, "l3_attn": pack_l3_attn, "l3_xattn": pack_l3_xattn,
         "l0_xattn": pack_xattn("L0_xattn"), "l1_xattn": pack_xattn("L1_xattn"), "l1_attn": pack_l1_attn,
         "l2_attn": pack_l2_attn, "l2_xattn": pack_l2_xattn,
         "l0_ffn": pack_l0_ffn, "l1_ffn": pack_l1_ffn, "l3_ffn": pack_l3_ffn, "columns": pack_columns}


def kernel(**inputs):
    import concourse.bacc as bacc
    from concourse.bass_utils import run_bass_kernel_spmd

    i = {k: np.asarray(v) for k, v in inputs.items()}
    nc = bacc.Bacc("TRN2", target_bir_lowering=False, num_devices=1)
    arrays, packed, places = {}, {}, {}

    def dram(name, a, kind="ExternalInput"):
        if kind == "ExternalInput":
            arrays[name] = np.ascontiguousarray(a)
        return nc.dram_tensor(name, a.shape, mybir.dt.from_np(a.dtype), kind=kind).ap()

    for n, parts in lay_out(i).items():
        a, places[n] = pack(parts)
        packed[n] = dram(f"pack_{n}", a)
    x = dram("x", i["x"])
    context = dram("context", i["ctx_1024"])
    mask = dram("context_mask", i["mask_BxS2_bk1"].reshape(B, S2, 1))
    out = dram("out", np.zeros((B, T, D), np.float32), kind="ExternalOutput")
    program(nc, x, context, mask, out, packed, places)
    r = run_bass_kernel_spmd(nc, [arrays], core_ids=[0])
    return r.results[0]["out"]
```
